# Optimizing a Trainium2 kernel written in Bass

```python
import numpy as np
import jax
import jax.numpy as jnp

def _softmax(x, axis=-1):
    return jax.nn.softmax(x, axis=axis)

def _gelu(x):
    return jax.nn.gelu(x, approximate=True)

def _silu(x):
    return jax.nn.silu(x)

def _sigmoid(x):
    return jax.nn.sigmoid(x)

def _layernorm(x, axis=-1, eps=1e-05):
    m = jnp.mean(x, axis=axis, keepdims=True)
    v = jnp.var(x, axis=axis, keepdims=True)
    return (x - m) / jnp.sqrt(v + eps)

def _scatter_add(tgt, idx, src, axis=0):
    return tgt.at[idx].add(src)

def _segment_sum(src, seg, n):
    return jax.ops.segment_sum(src, seg, n)
kernel_name = 'mk_flamingo_gated_d1_seqx_r2_5c27f4'

def setup_inputs(seed: int=0):
    np.random.seed(seed)
    _w = jnp.asarray

    def _rec_inputs():
        import jax
        import jax.numpy as jnp
        _rk = jax.random.key(seed)
        x = -0.0005207 + 1.001 * jax.random.normal(jax.random.fold_in(_rk, 1), (32, 512, 512), jnp.float32)
        _lenS = 512 - jax.random.randint(jax.random.fold_in(_rk, 7), (32,), 0, max(1, 512 // 4) + 1, jnp.int32)
        _lenS2 = 512 - jax.random.randint(jax.random.fold_in(_rk, 8), (32,), 0, max(1, 512 // 4) + 1, jnp.int32)
        _ctx_1024P = jax.random.normal(jax.random.fold_in(_rk, 11), (32, 16, 512), jnp.float32)
        _ctx_1024c = jax.random.dirichlet(jax.random.fold_in(_rk, 511), 0.3 * jnp.ones((16,), jnp.float32), (32, 512))
        _ctx_1024t = jnp.einsum('bsk,bkd->bsd', _ctx_1024c, _ctx_1024P)
        _ctx_1024t = _ctx_1024t * jax.lax.rsqrt(jnp.mean(jnp.square(_ctx_1024t)) + 1e-12) * 0.953939
        ctx_1024 = -0.000514642 + 1.00011 * (_ctx_1024t + 0.3 * jax.random.normal(jax.random.fold_in(_rk, 611), (32, 512, 512), jnp.float32))
        _g = jax.random.normal(jax.random.fold_in(_rk, 9001), (2, 1), jnp.float32)
        _g = jnp.sign(_g) * jnp.maximum(jnp.abs(_g), 1.0) + (_g == 0) * 1.0
        g_xattn = _g[0]
        g_ffn = _g[1]
        return (x, ctx_1024, g_xattn, g_ffn)
    x, ctx_1024, g_xattn, g_ffn = _rec_inputs()

    def _L0_xattn_setup():
        import jax, jax.numpy as jnp
        import numpy as np
        B, S, E, NH = (1, 1024, 512, 8)
        DH = E // NH
        EPS = 1e-06
        LN_EPS = 1e-05
        key = jax.random.key(seed)
        ks = jax.random.split(key, 8)
        q = jax.random.normal(ks[0], (B, S, E), dtype=jnp.float32)
        k = jax.random.normal(ks[1], (B, S, E), dtype=jnp.float32)
        v = jax.random.normal(ks[2], (B, S, E), dtype=jnp.float32)
        scale = 1.0 / np.sqrt(3 * E)
        igate_w = jax.random.normal(ks[3], (NH, 3 * E), dtype=jnp.float32) * scale
        igate_b = jax.random.normal(ks[4], (NH,), dtype=jnp.float32) * 0.1
        fgate_w = jax.random.normal(ks[5], (NH, 3 * E), dtype=jnp.float32) * scale
        fgate_b = jnp.linspace(3.0, 6.0, NH, dtype=jnp.float32)
        out_w = 1.0 + 0.1 * jax.random.normal(ks[6], (E,), dtype=jnp.float32)
        return {'q': q, 'k': k, 'v': v, 'igate_w': igate_w, 'igate_b': igate_b, 'fgate_w': fgate_w, 'fgate_b': fgate_b, 'out_w': out_w}
    _L0_xattn_all = _L0_xattn_setup()
    _L0_xattn_in = {k: v for k, v in _L0_xattn_all.items() if k in ('igate_w', 'igate_b', 'fgate_w', 'fgate_b', 'out_w')}
    del _L0_xattn_all

    def _L0_ffn_setup():
        import jax, jax.numpy as jnp
        import numpy as np
        B, S, H = (4, 1024, 512)
        E = 8
        GS = 2
        NG = E // GS
        F = int(H * 4 * (2.0 / 3.0))
        key = jax.random.key(seed)
        ks = jax.random.split(key, 7)
        sc_h = 1.0 / np.sqrt(H)
        sc_f = 1.0 / np.sqrt(F)
        return {'x': jax.random.normal(ks[0], (B, S, H), dtype=jnp.float32), 'Wr': jax.random.normal(ks[1], (H, E), dtype=jnp.float32) * sc_h, 'br': jnp.zeros((E,), dtype=jnp.float32), 'W_up': jax.random.normal(ks[2], (NG, H, F), dtype=jnp.float32) * sc_h, 'b_up': jax.random.normal(ks[3], (NG, F), dtype=jnp.float32) * 0.01, 'W_down': jax.random.normal(ks[4], (E, F, H), dtype=jnp.float32) * sc_f, 'b_down': jax.random.normal(ks[5], (E, H), dtype=jnp.float32) * 0.01}
    _L0_ffn_all = _L0_ffn_setup()
    _L0_ffn_in = {k: v for k, v in _L0_ffn_all.items() if k in ('Wr', 'br', 'W_up', 'b_up', 'W_down', 'b_down')}
    del _L0_ffn_all
    return {'x': x, 'ctx_1024': ctx_1024, 'g_xattn': g_xattn, 'g_ffn': g_ffn, 'L0_xattn_igate_w': _L0_xattn_in['igate_w'], 'L0_xattn_igate_b': _L0_xattn_in['igate_b'], 'L0_xattn_fgate_w': _L0_xattn_in['fgate_w'], 'L0_xattn_fgate_b': _L0_xattn_in['fgate_b'], 'L0_xattn_out_w': _L0_xattn_in['out_w'], 'L0_ffn_Wr': _L0_ffn_in['Wr'], 'L0_ffn_br': _L0_ffn_in['br'], 'L0_ffn_W_up': _L0_ffn_in['W_up'], 'L0_ffn_b_up': _L0_ffn_in['b_up'], 'L0_ffn_W_down': _L0_ffn_in['W_down'], 'L0_ffn_b_down': _L0_ffn_in['b_down']}

def reference(x, ctx_1024, g_xattn, g_ffn, L0_xattn_igate_w, L0_xattn_igate_b, L0_xattn_fgate_w, L0_xattn_fgate_b, L0_xattn_out_w, L0_ffn_Wr, L0_ffn_br, L0_ffn_W_up, L0_ffn_b_up, L0_ffn_W_down, L0_ffn_b_down):
    import jax
    import jax.numpy as jnp

    def _L0_xattn_ref(q, k, v, igate_w, igate_b, fgate_w, fgate_b, out_w):
        import jax, jax.numpy as jnp
        import numpy as np
        B, S, E, NH = (1, 1024, 512, 8)
        DH = E // NH
        EPS = 1e-06
        LN_EPS = 1e-05
        Bq, Sq, Eq = q.shape
        nh = igate_b.shape[0]
        dh = Eq // nh
        gi = jnp.concatenate([q, k, v], axis=-1)
        ig = (gi @ igate_w.T + igate_b).transpose(0, 2, 1)
        fg = (gi @ fgate_w.T + fgate_b).transpose(0, 2, 1)
        qh = q.reshape(Bq, Sq, nh, dh).transpose(0, 2, 1, 3)
        kh = k.reshape(Bq, Sq, nh, dh).transpose(0, 2, 1, 3)
        vh = v.reshape(Bq, Sq, nh, dh).transpose(0, 2, 1, 3)
        log_f = jax.nn.log_sigmoid(fg)
        cs = jnp.cumsum(log_f, axis=-1)
        diff = cs[..., :, None] - cs[..., None, :]
        mask = jnp.tril(jnp.ones((Sq, Sq), dtype=bool))
        log_fg_mat = jnp.where(mask, diff, -jnp.inf)
        log_D = log_fg_mat + ig[..., None, :]
        max_log_D = jnp.max(log_D, axis=-1, keepdims=True)
        D = jnp.exp(log_D - max_log_D)
        qk = jnp.einsum('bhsd,bhtd->bhst', qh, kh) / jnp.sqrt(jnp.float32(dh))
        C = qk * D
        normalizer = jnp.maximum(jnp.abs(C.sum(-1, keepdims=True)), jnp.exp(-max_log_D))
        h = jnp.einsum('bhst,bhtd->bhsd', C / (normalizer + EPS), vh)
        mean = h.mean(-1, keepdims=True)
        var = ((h - mean) ** 2).mean(-1, keepdims=True)
        hn = (h - mean) / jnp.sqrt(var + LN_EPS)
        hn = hn * out_w.reshape(nh, dh)[None, :, None, :]
        return hn.transpose(0, 2, 1, 3).reshape(Bq, Sq, Eq)

    def _L0_ffn_ref(x, Wr, br, W_up, b_up, W_down, b_down):
        import jax, jax.numpy as jnp
        import numpy as np
        B, S, H = (4, 1024, 512)
        E = 8
        GS = 2
        NG = E // GS
        F = int(H * 4 * (2.0 / 3.0))
        b, s, h = x.shape
        n_tok = b * s
        k = n_tok // E
        xf = x.reshape(n_tok, h)
        logits = xf @ Wr + br
        Sm = jax.nn.softmax(logits, axis=-1)
        G_t, idx_t = jax.lax.top_k(Sm.T, k)
        G = G_t.T
        idx = idx_t.T
        tokens = xf[idx]
        group = jnp.arange(E) // GS
        Wu = W_up[group]
        bu = b_up[group]
        mid = jax.nn.silu(jnp.einsum('keh,ehf->kef', tokens, Wu) + bu)
        out = jnp.einsum('kef,efh->keh', mid, W_down) + b_down
        y = jnp.zeros_like(xf).at[idx].add(G[..., None] * out)
        return y.reshape(b, s, h)
    x = x + jnp.tanh(g_xattn[0]) * _L0_xattn_ref(_layernorm(x, axis=-1), ctx_1024, ctx_1024, L0_xattn_igate_w, L0_xattn_igate_b, L0_xattn_fgate_w, L0_xattn_fgate_b, L0_xattn_out_w)
    x = x + jnp.tanh(g_ffn[0]) * _L0_ffn_ref(_layernorm(x, axis=-1), L0_ffn_Wr, L0_ffn_br, L0_ffn_W_up, L0_ffn_b_up, L0_ffn_W_down, L0_ffn_b_down)
    return x

_drawn_inputs = setup_inputs


def setup_inputs(seed=0):
    import zlib

    import numpy as np

    out = dict(_drawn_inputs(seed))
    spreads = {'L0_ffn_br': (0.0, 0.275)}
    factors = {'L0_xattn_igate_b': 64.0, 'L0_ffn_b_up': 35.449, 'L0_ffn_b_down': 21.532}
    for name, (base, spread) in spreads.items():
        noise = np.random.default_rng([zlib.crc32(name.encode()), seed]).standard_normal(out[name].shape)
        drawn = base * np.exp(spread * noise) if base else spread * noise
        out[name] = jnp.asarray(drawn.astype(out[name].dtype))
    for name, factor in factors.items():
        out[name] = (out[name] * factor).astype(out[name].dtype)
    return out
```

```python
import numpy as np
import concourse.bass as bass
from concourse import mybir
from concourse.alu_op_type import AluOpType as ALU
from contextlib import ExitStack

FP32 = mybir.dt.float32
FP32R = mybir.dt.float32r
BF16 = mybir.dt.bfloat16
I32 = mybir.dt.int32
U32 = mybir.dt.uint32
ACT = mybir.ActivationFunctionType
AX = mybir.AxisListType

P = 128
E_DIM = 512
TILES = 4
SEQ = TILES * P
HEADS = 8
DH = E_DIM // HEADS
PAIRS = HEADS // 2
CH = E_DIM // P
VW = DH + 2
ROWW = HEADS * VW
NEXP = 8
FDIM = int(E_DIM * 4 * (2.0 / 3.0))
FCH = -(-FDIM // P)
FLAST = FDIM - (FCH - 1) * P
XW = E_DIM + NEXP
QD = 32
LN_EPS = 1e-5
NORM_EPS = 1e-6
BIG = 1e30
XBUF = 4


class Line:

    def __init__(self, sem):
        self.sem, self.n = sem, 0

    def inc(self, instruction, by=1):
        instruction.then_inc(self.sem, by)
        self.n += by
        return self.n


class Chain:

    def __init__(self, eng, sem):
        self.eng, self.line = eng, Line(sem)

    def __call__(self, instruction):
        self.eng.wait_ge(self.line.sem, self.line.inc(instruction))


def spread(ap, axis, n):
    ap = ap.unsqueeze(axis)
    return ap.to_broadcast([n if i == axis else s for i, s in enumerate(ap.shape)])


def newton_rsqrt(step, eng, y, v, t):
    step(eng.tensor_tensor(t, y, y, ALU.mult))
    step(eng.tensor_tensor(t, t, v, ALU.mult))
    step(eng.tensor_scalar(t, t, -0.5, 1.5, ALU.mult, ALU.add))
    step(eng.tensor_tensor(y, y, t, ALU.mult))


def attention(nc, io, NB, dram, sm_all, tg, consts):
    x_v = io["x"].rearrange("b (j p) e -> b p j e", p=P)
    c_v = io["ctx"].rearrange("b (j p) e -> b p j e", p=P)
    out_v = io["out"].rearrange("b (j p) e -> b p j e", p=P)
    xf_v = dram["xf"].rearrange("(b j p) w -> b p j w", j=TILES, p=P)
    ident, identb, ones = consts["ident"], consts["identb"], consts["ones"]
    with ExitStack() as ctx:
        def sb(name, shape, dt=FP32):
            return ctx.enter_context(nc.sbuf_tensor(name, shape, dt))

        def pb(name, shape, dt=FP32):
            return ctx.enter_context(nc.psum_tensor(name, shape, dt))

        def sem(name):
            return ctx.enter_context(nc.semaphore(name))

        xs = sb("xs", [P, XBUF, TILES, E_DIM])
        craw = sb("craw", [P, TILES, E_DIM])
        vaug = sb("vaug", [P, 2, TILES * ROWW + P])
        q = sb("q", [P, TILES, E_DIM])
        qT = sb("qT", [P, 2, CH, SEQ])
        kT = sb("kT", [P, CH, SEQ])
        kpad = sb("kpad", [P, 2, CH, SEQ])
        xfb = sb("xfb", [P, 2, TILES, XW])
        C = sb("C", [P, HEADS, SEQ])
        D = sb("D", [P, 2, SEQ])
        qw = sb("qw", [P, CH, SEQ - P])
        uv = sb("uv", [P, TILES - 1, HEADS, VW])
        S = sb("S", [P, TILES - 1, PAIRS, 2 * VW])
        nsb = sb("nsb", [P, TILES, HEADS, VW])
        ee = sb("ee", [8, SEQ]); cs = sb("cs", [8, SEQ]); aa = sb("aa", [8, SEQ])
        MM = sb("MM", [8, SEQ])
        Z = sb("Z", [72, SEQ]); Zx = sb("Zx", [104, SEQ])
        Mhl = sb("Mhl", [40, SEQ], FP32R)
        whl = sb("whl", [40, SEQ - P], FP32R)
        gd = sb("gd", [8, 2]); gdiag = sb("gdiag", [8, 2, 8]); gb = sb("gb", [P, 2, 8])
        tm = sb("tm", [P, TILES, 4, HEADS])
        selM = sb("selM", [40, HEADS, P], FP32R); selP = sb("selP", [40, PAIRS, P], FP32R)
        maskneg = sb("maskneg", [P, SEQ], BF16)
        gW = sb("gW", [P, 2 * CH, 40])
        gbias = sb("gbias", [40, 1])
        Wr = sb("Wr", [P, CH, NEXP]); br = sb("br", [NEXP, 1]); Wo = sb("Wo", [P, E_DIM])
        st = sb("st", [P, TILES, 6]); mv = sb("mv", [P, TILES, 2]); va = sb("va", [P, TILES]); ra = sb("ra", [P, TILES]); ta = sb("ta", [P, TILES])
        st2 = sb("st2", [P, TILES, 6]); mv2 = sb("mv2", [P, TILES, 2]); vb = sb("vb", [P, TILES]); rb = sb("rb", [P, TILES]); tb = sb("tb", [P, TILES])
        la = sb("la", [P, TILES]); lb = sb("lb", [P, TILES]); lh = sb("lh", [P, TILES * HEADS])
        msum = sb("msum", [P, TILES * HEADS])
        nrm = sb("nrm", [P, 2, TILES * HEADS]); rn = sb("rn", [P, TILES * HEADS]); ssq = sb("ssq", [P, TILES * HEADS])
        vh = sb("vh", [P, TILES * HEADS]); rh = sb("rh", [P, TILES * HEADS]); th = sb("th", [P, TILES * HEADS])
        lg = sb("lg", [NEXP, SEQ]); lt = sb("lt", [P, TILES, NEXP]); mx = sb("mx", [P, TILES]); sx = sb("sx", [P, TILES]); ex = sb("ex", [P, TILES, NEXP])

        sq = C[:, 0:TILES, :].rearrange("p j (h d) -> p (j h) d", d=DH)
        xfT = C[:, TILES:2 * TILES, :]
        gwr = C[0:16, 0:3, :].rearrange("g n e -> g (n e)")
        self_ = kT[0:40, 0:2, :].rearrange("k a (h s) -> k (a h) s", s=P)

        T = [pb("T0", [P, SEQ]), pb("T1", [P, SEQ])]
        G = pb("G", [P, SEQ])
        EB = pb("EB", [P, SEQ])
        QK = [pb("QK0", [P, SEQ]), pb("QK1", [P, SEQ])]
        A = pb("A", [P, HEADS, P])

        names = ("tfull ta td init ldw xd cd stx2 stxf v1 r1 q v2 r2 xf2 vg gates gput ex1 ln1 zz zx gg gx "
                 "ms ws ee dd qk cc af an cen sq lnh o ow x2 lex smx vaug kpad uv "
                 "dchain achain pchain prep1 prep2 prep3 prep4 tr0 tr1").split()
        s = {n: sem("a_" + n) for n in names}
        s_xl = [sem(f"a_xl{i}") for i in range(XBUF)]
        s_xst = [sem(f"a_xst{i}") for i in range(XBUF)]
        s_fst = [sem(f"a_fst{i}") for i in range(2)]

        order, owner = [], {}

        def iteration_fills(i):
            if 0 <= i - 2 < NB:
                yield ("tm", i - 2, 0, "dve")
                yield ("g", i - 2, 0, "dve")
            if 0 <= i - 1 < NB:
                yield from [("q", i - 1, c, "act") for c in range(CH)]
                yield from [("k", i - 1, c, "act") for c in range(CH)]
            if 0 <= i - 2 < NB:
                for h in range(HEADS - 1):
                    yield (("st", i - 2, h // 2, "dve") if h in (0, 2, 4) else
                           ("qw", i - 2, {1: 0, 3: 1, 5: 2, 6: 3}[h], "dve"))
            if 0 <= i - 3 < NB:
                yield from [("xfT", i - 3, c, "act") for c in range(CH)]
                yield ("lg", i - 3, 0, "act")
                yield ("lt", i - 3, 0, "dve")

        number, freed, counts = {}, [], {"act": 0, "dve": 0}
        for i in range(NB + 4):
            for kind, b, k, who in iteration_fills(i):
                number[kind, b, k] = len(freed)
                counts[who] += 1
                freed.append((s["ta" if who == "act" else "td"], counts[who]))

        def bank(kind, b, k):
            return T[number[kind, b, k] % 2]

        def fill(pe, kind, b, k):
            n = number[kind, b, k]
            if n >= 2:
                pe.wait_ge(*freed[n - 2])
            return T[n % 2]

        def filled(eng, kind, b, k):
            eng.wait_ge(s["tfull"], number[kind, b, k] + 1)
            return bank(kind, b, k)

        def v_of(b, j, c0, n):
            return vaug[:, b % 2, j * ROWW + c0:j * ROWW + c0 + n]

        def v_wide(b, j, h):
            at, more = j * ROWW + DH * h, E_DIM + 2 * h - DH * h
            first = vaug[:, b % 2, at:at + DH]
            return bass.AP(tensor=first.tensor, offset=first.offset, ap=[first.ap[0], [more, 2], [1, DH]])

        with nc.Block() as block:
            @block.sync
            def _(sp):
                sp.dma_start(gwr[0:8, :], io["igw"]).then_inc(s["ldw"], 16)
                sp.dma_start(gwr[8:16, :], io["fgw"]).then_inc(s["ldw"], 16)
                sp.dma_start(gbias[0:8, :], io["igb"].unsqueeze(1)).then_inc(s["ldw"], 16)
                sp.dma_start(gbias[32:40, :], io["fgb"].unsqueeze(1)).then_inc(s["ldw"], 16)
                sp.dma_start(Wr[:, :, :], io["Wr"].rearrange("(c p) n -> p c n", p=P)).then_inc(s["ldw"], 16)
                sp.dma_start(br[:, :], io["br"].unsqueeze(1)).then_inc(s["ldw"], 16)
                sp.dma_start(Wo[:, :], io["outw"].partition_broadcast(P)).then_inc(s["ldw"], 16)
                sp.dma_start(xs[:, 0, :, :], x_v[0]).then_inc(s_xl[0], 16)
                sp.dma_start(craw[:, :, :], c_v[0]).then_inc(s["cd"], 16)
                for i in range(NB + 5):
                    if 0 <= i - 4 < NB:
                        b = i - 4
                        sp.wait_ge(s["smx"], b + 1)
                        sp.wait_ge(s["xf2"], b + 1)
                        sp.dma_start(xf_v[b], xfb[:, b % 2, :, :]).then_inc(s_fst[b % 2], 16)
                    if 0 <= i - 3 < NB:
                        b = i - 3
                        sp.wait_ge(s["x2"], b + 1)
                        sp.dma_start(out_v[b], xs[:, b % XBUF, :, :]).then_inc(s_xst[b % XBUF], 16)
                    if i + 1 < NB:
                        b = i + 1
                        if b >= XBUF:
                            sp.wait_ge(s_xst[b % XBUF], 16 * (b // XBUF))
                            sp.wait_ge(s["v2"], b - XBUF + 1)
                            sp.wait_ge(s["xf2"], b - XBUF + 1)
                        sp.dma_start(xs[:, b % XBUF, :, :], x_v[b]).then_inc(s_xl[b % XBUF], 16)
                        sp.wait_ge(s["vaug"], b)
                        sp.dma_start(craw[:, :, :], c_v[b]).then_inc(s["cd"], 16)
                for n in range(XBUF):
                    sp.wait_ge(s_xst[n], 16 * len(range(n, NB, XBUF)))
                for n in range(2):
                    sp.wait_ge(s_fst[n], 16 * len(range(n, NB, 2)))

            @block.gpsimd
            def _(pool):
                step = Chain(pool, s["pchain"])
                step(pool.memset(self_[:, :, :], 0.0))
                step(pool.affine_select(out=self_[:, :, :], in_=self_[:, :, :], compare_op=ALU.not_equal, fill=1.0,
                                        base=0, pattern=[[-1, HEADS], [0, P]], channel_multiplier=1))
                step(pool.affine_select(out=self_[:, :, :], in_=self_[:, :, :], compare_op=ALU.not_equal, fill=-1.0,
                                        base=-QD, pattern=[[-1, HEADS], [0, P]], channel_multiplier=1))
                step(pool.tensor_copy(selM[:, :, :], self_[:, :, :]))
                step(pool.memset(self_[:, :, :], 0.0))
                v = self_[:, 0:PAIRS, :].rearrange("k p (a d) -> k p a d", a=2)
                step(pool.affine_select(out=v, in_=v, compare_op=ALU.not_equal, fill=1.0, base=0,
                                        pattern=[[-2, PAIRS], [-1, 2], [0, DH]], channel_multiplier=1))
                step(pool.affine_select(out=v, in_=v, compare_op=ALU.not_equal, fill=1.0, base=-QD,
                                        pattern=[[-2, PAIRS], [-1, 2], [0, DH]], channel_multiplier=1))
                step(pool.tensor_copy(selP[:, :, :], self_[:, 0:PAIRS, :]))
                step(pool.memset(maskneg[:, :], 0.0))
                m = maskneg[:, :].rearrange("p (j s) -> p j s", j=TILES)
                step(pool.affine_select(out=m, in_=m, compare_op=ALU.is_ge, fill=-BIG, base=0,
                                        pattern=[[0, TILES], [1, P]], channel_multiplier=-1))
                step(pool.memset(vaug[:, :, :], 1.0))
                step(pool.memset(kpad[:, :, :, :], 0.0))
                step(pool.memset(S[:, :, :, :], 0.0))
                step(pool.memset(Z[:, :], 0.0))
                step(pool.memset(Zx[:, :], 0.0))
                step(pool.memset(Mhl[:, :].bitcast(FP32), 0.0))
                step(pool.memset(whl[:, :].bitcast(FP32), 0.0))
                pool.memset(gW[:, :, :], 0.0).then_inc(s["prep1"], 1)
                pool.wait_ge(s["prep1"], 1)
                pool.wait_ge(s["ldw"], 7 * 16)
                pool.wait_ge(tg["sem"], tg["ready"])
                step(pool.tensor_scalar(Wo[:, :], Wo[:, :], tg["ap"][:, 0:1], None, ALU.mult))

                def take_ctx(b):
                    pool.wait_ge(s["cd"], 16 * (b + 1))
                    if b >= 2:
                        pool.wait_ge(s["af"], TILES * (b - 1))
                    va_ = vaug[:, b % 2, 0:TILES * ROWW].rearrange("p (j w) -> p j w", w=ROWW)
                    cr = craw[:, :, :].rearrange("p j (h d) -> p (j h) d", d=DH)
                    step(pool.tensor_copy(va_[:, :, 0:E_DIM], craw[:, :, :]))
                    w = DH // 2
                    while w >= 1:
                        o_ = cr[:, :, 0:w] if w > 1 else msum[:, :].unsqueeze(2)
                        step(pool.tensor_tensor(o_, cr[:, :, 0:w], cr[:, :, w:2 * w], ALU.add))
                        w //= 2
                    pool.tensor_scalar(va_[:, :, E_DIM + 1:ROWW:2], msum[:, :].rearrange("p (j h) -> p j h", h=HEADS), 1.0 / DH, None, ALU.mult)\
                        .then_inc(s["vaug"], 1)
                    pool.wait_ge(s["vaug"], b + 1)

                def pad_k(b):
                    pool.wait_ge(*freed[number["k", b, CH - 1]])
                    if b >= 1:
                        pool.wait_ge(s["qk"], HEADS * b)
                    for par in range(2):
                        r = slice(DH * par, DH * par + DH)
                        pool.tensor_scalar(kpad[r, par, :, :], kT[r, :, :], DH ** -0.5, None, ALU.mult).then_inc(s["kpad"], 1)
                        pool.wait_ge(s["kpad"], 2 * b + par + 1)

                def weigh_v(b):
                    pool.wait_ge(*freed[number["tm", b, 0]])
                    if b >= 1:
                        pool.wait_ge(s["tfull"], number["st", b - 1, 2] + 1)
                    for j in range(TILES - 1):
                        pool.tensor_tensor(uv[:, j, :, 0:DH], v_of(b, j, 0, E_DIM).rearrange("p (h d) -> p h d", d=DH),
                                           spread(tm[:, j, 0, :], 2, DH), ALU.mult)
                        ins = pool.tensor_tensor(uv[:, j, :, DH:VW], v_of(b, j, E_DIM, 2 * HEADS).rearrange("p (h d) -> p h d", d=2),
                                                 spread(tm[:, j, 0, :], 2, 2), ALU.mult)
                    ins.then_inc(s["uv"], 1)
                    pool.wait_ge(s["uv"], b + 1)

                def centre(b):
                    pool.wait_ge(s["an"], TILES * (b + 1))
                    n = nsb[:, :, :, :].rearrange("p j h w -> p (j h) w")
                    pool.tensor_tensor(n[:, :, 0:DH], n[:, :, 0:DH], n[:, :, DH + 1:DH + 2].to_broadcast([P, TILES * HEADS, DH]),
                                       ALU.subtract).then_inc(s["cen"], 1)
                    pool.wait_ge(s["cen"], b + 1)

                def weigh_out(b):
                    pool.wait_ge(s["o"], b + 1)
                    n = nsb[:, :, :, :]
                    for j in range(TILES):
                        ins = pool.tensor_tensor(n[:, j, :, 0:DH], n[:, j, :, 0:DH],
                                                 Wo[:, :].rearrange("p (h d) -> p h d", d=DH), ALU.mult)
                    ins.then_inc(s["ow"], 1)
                    pool.wait_ge(s["ow"], b + 1)

                for i in range(NB + 4):
                    if 0 <= i - 2 < NB:
                        weigh_v(i - 2)
                    if 0 <= i - 3 < NB:
                        weigh_out(i - 3)
                    if 0 <= i - 2 < NB:
                        centre(i - 2)
                    if 0 <= i < NB:
                        take_ctx(i)
                    if 0 <= i - 1 < NB:
                        pad_k(i - 1)

            @block.scalar
            def _(act):
                step = Chain(act, s["achain"])

                def rsqrt_guess(src, tmp, dst, ready, by, log, done):
                    act.wait_ge(ready, by)
                    act.activation(tmp, src, ACT.Ln).then_inc(log, 1)
                    act.wait_ge(log, by)
                    act.activation(dst, tmp, ACT.Exp, scale=-0.5).then_inc(done, 1)

                for i in range(NB + 4):
                    if 0 <= i - 4 < NB:
                        act.wait_ge(*freed[number["lt", i - 4, 0]])
                        act.activation(ex[:, :, :], lt[:, :, :], ACT.Exp).then_inc(s["lex"], 1)
                    if 0 <= i - 1 < NB:
                        b = i - 1
                        if b >= 2:
                            act.wait_ge(s["qk"], HEADS * (b - 1))
                            act.wait_ge(*freed[number["qw", b - 2, PAIRS - 1]])
                        for c in range(CH):
                            t = filled(act, "q", b, c)
                            act.activation(qT[:, b % 2, c, :], t[:, :], ACT.Copy).then_inc(s["ta"], 1)
                    if i < NB:
                        rsqrt_guess(va[:, :], la[:, :], ra[:, :], s["v1"], i + 1, s["ln1"], s["r1"])
                    if 0 <= i - 1 < NB:
                        b = i - 1
                        if b >= 1:
                            act.wait_ge(s["kpad"], 2 * b)
                            act.wait_ge(s["gates"], b)
                        for c in range(CH):
                            t = filled(act, "k", b, c)
                            ins = act.activation(kT[:, c, :], t[:, :], ACT.Copy)
                            ins.then_inc(s["ta"], 1)
                    if 0 <= i - 3 < NB:
                        b = i - 3
                        rsqrt_guess(vh[:, :], lh[:, :], rh[:, :], s["lnh"], b + 1, s["ex1"], s["gg"])
                        rsqrt_guess(vb[:, :], lb[:, :], rb[:, :], s["v2"], b + 1, s["tr1"], s["r2"])
                    if 0 <= i - 2 < NB:
                        b = i - 2
                        for h in range(HEADS):
                            act.wait_ge(s["ee"], HEADS * b + h + 1)
                            if HEADS * b + h >= 2:
                                act.wait_ge(s["cc"], HEADS * b + h - 1)
                            if h == 0:
                                act.wait_ge(*freed[number["tm", b, 0]])
                            for j in range(TILES):
                                ins = act.activation(D[:, h % 2, j * P:(j + 1) * P], EB[:, j * P:(j + 1) * P], ACT.Exp,
                                                     bias=tm[:, j, 3, h:h + 1])
                            ins.then_inc(s["dd"], 1)
                        for j in range(TILES):
                            act.wait_ge(s["af"], TILES * b + j + 1)
                            if j == 0 and b >= 1:
                                act.wait_ge(s["x2"], b)
                            act.activation(nsb[:, j, :, :], A[:, :, 0:VW], ACT.Copy).then_inc(s["an"], 1)
                        act.wait_ge(s["cen"], b + 1)
                        act.activation(sq, nsb[:, :, :, :].rearrange("p j h w -> p (j h) w")[:, :, 0:DH], ACT.Square)\
                           .then_inc(s["sq"], 1)
                    if 0 <= i - 3 < NB:
                        b = i - 3
                        for c in range(CH):
                            t = filled(act, "xfT", b, c)
                            act.activation(xfT[:, c, :], t[:, :], ACT.Copy).then_inc(s["ta"], 1)
                        t = filled(act, "lg", b, 0)
                        act.activation(lg[:, :], t[0:NEXP, :], ACT.Identity, bias=br[:, :]).then_inc(s["ta"], 1)
                    if 0 <= i - 1 < NB:
                        b = i - 1
                        act.wait_ge(s["vg"], b + 1)
                        step(act.activation(ee[:, :], ee[:, :], ACT.Abs))
                        step(act.activation(ee[:, :], ee[:, :], ACT.Exp, scale=-1.0))
                        act.activation(ee[:, :], ee[:, :], ACT.Ln, bias=1.0).then_inc(s["gx"], 1)
                        act.wait_ge(s["zz"], b + 1)
                        if b >= 1:
                            act.wait_ge(s["tfull"], number["tm", b - 1, 0] + 1)
                        act.activation(Zx[0:72, :], Z[0:72, :], ACT.Exp).then_inc(s["zx"], 1)
                        act.activation(gd[:, :], gd[:, :], ACT.Exp).then_inc(s["zx"], 1)

            @block.tensor
            def _(pe):
                pe.wait_ge(s["ldw"], 7 * 16)
                pe.wait_ge(consts["sem"], consts["ready"])
                for c in range(3 * CH):
                    mm = pe.transpose(G[:, 16 * c:16 * c + 16], gwr[:, c * P:(c + 1) * P], ident[0:16, 0:16])
                mm.then_inc(s["prep2"], 1)
                pe.wait_ge(s["prep3"], 1)
                for i in range(NB + 4):
                    if 0 <= i - 2 < NB:
                        b = i - 2
                        t = fill(pe, "tm", b, 0)
                        pe.wait_ge(s["zx"], 2 * b + 2)
                        pe.wait_ge(s["ms"], b + 1)
                        for j in range(TILES):
                            mm = pe.transpose(t[:, j * P:j * P + 104], Zx[:, j * P:(j + 1) * P], ident[0:104, 0:104])
                        mm.then_inc(s["tfull"], 1)
                        t = fill(pe, "g", b, 0)
                        mm = pe.matmul(t[:, 0:16], ones[0:8, :], gdiag[:, :, :].rearrange("k j h -> k (j h)"), start=True, stop=True)
                        mm.then_inc(s["tfull"], 1)
                    if 0 <= i - 1 < NB:
                        b = i - 1
                        pe.wait_ge(s["q"], b + 1)
                        for c in range(CH):
                            t = fill(pe, "q", b, c)
                            for j in range(TILES):
                                mm = pe.transpose(t[:, j * P:(j + 1) * P], q[:, j, c * P:(c + 1) * P], ident[:, :])
                            mm.then_inc(s["tfull"], 1)
                        pe.wait_ge(s["vaug"], b + 1)
                        for c in range(CH):
                            t = fill(pe, "k", b, c)
                            for j in range(TILES):
                                src = v_of(b, j, c * P, P)
                                mm = pe.transpose(t[:, j * P:(j + 1) * P], src, ident[:, :])
                            mm.then_inc(s["tfull"], 1)
                        if b >= 1:
                            pe.wait_ge(s["gput"], b)
                        for c in range(2 * CH):
                            if c in (0, CH):
                                pe.wait_ge(*freed[number["q" if c == 0 else "k", b, CH - 1]])
                            src = qT[:, b % 2, c, :] if c < CH else kT[:, c - CH, :]
                            mm = pe.matmul(G[0:40, :], gW[:, c, :], src, start=(c == 0), stop=(c == 2 * CH - 1))
                        mm.then_inc(s["gates"], 1)
                    if 0 <= i - 2 < NB:
                        b = i - 2
                        pe.wait_ge(s["kpad"], 2 * b + 2)
                        for h in range(HEADS):
                            n = HEADS * b + h
                            if n >= 1:
                                pe.wait_ge(s["dd"], n)
                            pe.matmul(EB[:, :], identb[:, :], maskneg[:, :], start=True, stop=False)
                            pe.matmul(EB[:, :], selM[:, h, :], Mhl[:, :], start=False, stop=True).then_inc(s["ee"], 1)
                            if n >= 2:
                                pe.wait_ge(s["cc"], n - 1)
                            for j in range(TILES):
                                jj = slice(j * P, (j + 1) * P)
                                mm = pe.matmul(QK[h % 2][:, jj], kpad[:, h % 2, h // 2, jj], qT[:, b % 2, h // 2, jj], start=True, stop=True)
                            mm.then_inc(s["qk"], 1)
                            if h in (0, 2, 4):
                                j = h // 2
                                t = fill(pe, "st", b, j)
                                if h == 0:
                                    pe.wait_ge(s["uv"], b + 1)
                                for g in range(HEADS):
                                    r = DH * (g % 2)
                                    mm = pe.matmul(t[r:r + DH, (g // 2) * VW:(g // 2 + 1) * VW], v_of(b, j, g * DH, DH),
                                                   uv[:, j, g, :], start=True, stop=True)
                                mm.then_inc(s["tfull"], 1)
                            elif h != HEADS - 1:
                                p = {1: 0, 3: 1, 5: 2, 6: 3}[h]
                                t = fill(pe, "qw", b, p)
                                pe.matmul(t[:, 0:SEQ - P], selP[:, p, :], whl[:, :], start=True, stop=True).then_inc(s["tfull"], 1)
                        for j in range(TILES):
                            n = TILES * b + j
                            if j == 0:
                                pe.wait_ge(s["cc"], HEADS * (b + 1))
                            if j == 1:
                                pe.wait_ge(*freed[number["qw", b, 3]])
                            if n >= 1:
                                pe.wait_ge(s["an"], n)
                            for h in range(HEADS):
                                mm = pe.matmul(A[:, h, :].rearrange("p (a w) -> p a w", a=2), C[:, h, j * P:(j + 1) * P], v_wide(b, j, h),
                                               start=(h % 4 == 0), stop=(j == 0), skip_group_check=True)
                            if j:
                                for p in range(PAIRS):
                                    mm = pe.matmul(A[:, 2 * p:2 * p + 2, 0:VW], qw[:, p, (j - 1) * P:j * P],
                                                   S[:, j - 1, p, :].rearrange("k (a w) -> k a w", a=2),
                                                   start=False, stop=True, skip_group_check=True)
                            mm.then_inc(s["af"], 1)
                    if 0 <= i - 3 < NB:
                        b = i - 3
                        pe.wait_ge(s["xf2"], b + 1)
                        for c in range(CH):
                            t = fill(pe, "xfT", b, c)
                            for j in range(TILES):
                                mm = pe.transpose(t[:, j * P:(j + 1) * P], xfb[:, b % 2, j, c * P:(c + 1) * P], ident[:, :])
                            mm.then_inc(s["tfull"], 1)
                        t = fill(pe, "lg", b, 0)
                        pe.wait_ge(*freed[number["xfT", b, CH - 1]])
                        for c in range(CH):
                            mm = pe.matmul(t[0:NEXP, :], Wr[:, c, :], xfT[:, c, :], start=(c == 0), stop=(c == CH - 1))
                        mm.then_inc(s["tfull"], 1)
                        t = fill(pe, "lt", b, 0)
                        pe.wait_ge(*freed[number["lg", b, 0]])
                        for j in range(TILES):
                            mm = pe.transpose(t[:, j * NEXP:(j + 1) * NEXP], lg[:, j * P:(j + 1) * P], ident[0:NEXP, 0:NEXP])
                        mm.then_inc(s["tfull"], 1)

            @block.vector
            def _(dve):
                step = Chain(dve, s["dchain"])
                dve.wait_ge(s["prep1"], 1)
                dve.wait_ge(s["prep2"], 1)
                g3 = G[:, 0:48 * CH].rearrange("p (c g) -> p c g", g=16)
                step(dve.tensor_copy(gW[:, :, 0:8], g3[:, 0:2 * CH, 0:8]))
                step(dve.tensor_copy(gW[:, :, 32:40], g3[:, 0:2 * CH, 8:16]))
                step(dve.tensor_tensor(gW[:, CH:2 * CH, 0:8], gW[:, CH:2 * CH, 0:8], g3[:, 2 * CH:3 * CH, 0:8], ALU.add))
                dve.tensor_tensor(gW[:, CH:2 * CH, 32:40], gW[:, CH:2 * CH, 32:40], g3[:, 2 * CH:3 * CH, 8:16], ALU.add)\
                    .then_inc(s["prep3"], 1)

                def statistics(src, st_, mv_, v_):
                    for j in range(TILES):
                        ins = dve.bn_stats(st_[:, j, :], src[:, j, :])
                    step(ins)
                    for j in range(TILES):
                        ins = dve.bn_aggr(mv_[:, j, :], st_[:, j, :])
                    step(ins)
                    return dve.tensor_scalar(v_, mv_[:, :, 1], LN_EPS, None, ALU.add)

                for i in range(NB + 4):
                    if 0 <= i - 4 < NB:
                        b = i - 4
                        t = filled(dve, "lt", b, 0)
                        l3 = t[:, 0:TILES * NEXP].rearrange("p (j n) -> p j n", n=NEXP)
                        step(dve.tensor_reduce(mx[:, :], l3, AX.X, ALU.max))
                        dve.tensor_tensor(lt[:, :, :], l3, spread(mx[:, :], 2, NEXP), ALU.subtract).then_inc(s["td"], 1)
                    if 0 <= i - 2 < NB:
                        b = i - 2
                        t = filled(dve, "tm", b, 0)
                        t4 = t[:, :].rearrange("p (j k h) -> p j k h", k=4, h=QD)
                        dve.tensor_copy(nrm[:, b % 2, :].rearrange("p (j h) -> p j h", h=HEADS), t4[:, :, 2, 0:HEADS])
                        dve.tensor_copy(tm[:, :, :, :], t4[:, :, :, 0:HEADS]).then_inc(s["td"], 1)
                        t = filled(dve, "g", b, 0)
                        dve.tensor_copy(gb[:, :, :].rearrange("p j h -> p (j h)"), t[:, 0:16]).then_inc(s["td"], 1)
                        dve.wait_ge(*freed[number["g", b, 0]])
                    if i < NB:
                        dve.wait_ge(s_xl[i % XBUF], 16 * (i // XBUF + 1))
                        if i >= 1:
                            dve.wait_ge(s["r1"], i)
                        statistics(xs[:, i % XBUF, :, :], st, mv, va[:, :]).then_inc(s["v1"], 1)
                    if 0 <= i - 4 < NB:
                        b = i - 4
                        dve.wait_ge(s["lex"], i - 3)
                        step(dve.tensor_reduce(sx[:, :], ex[:, :, :], AX.X, ALU.add))
                        step(dve.reciprocal(sx[:, :], sx[:, :]))
                        step(dve.tensor_tensor(sm_all[:, b * TILES:(b + 1) * TILES, :], ex[:, :, :], spread(sx[:, :], 2, NEXP), ALU.mult))
                        dve.tensor_copy(xfb[:, b % 2, :, E_DIM:XW], sm_all[:, b * TILES:(b + 1) * TILES, :]).then_inc(s["smx"], 1)
                    if 0 <= i - 3 < NB:
                        b = i - 3
                        n = nsb[:, :, :, :].rearrange("p j h w -> p (j h) w")
                        dve.wait_ge(s["sq"], b + 1)
                        step(dve.tensor_reduce(ssq[:, :], sq, AX.X, ALU.add))
                        step(dve.scalar_tensor_tensor(out=rn[:, :].unsqueeze(2), in0=n[:, :, DH:DH + 1], scalar=-1.0,
                                                      in1=n[:, :, DH:DH + 1], op0=ALU.mult, op1=ALU.max))
                        step(dve.tensor_tensor(rn[:, :], rn[:, :], nrm[:, b % 2, :], ALU.max))
                        step(dve.tensor_scalar(rn[:, :], rn[:, :], NORM_EPS, None, ALU.add))
                        step(dve.reciprocal(rn[:, :], rn[:, :]))
                        step(dve.tensor_tensor(th[:, :], rn[:, :], rn[:, :], ALU.mult))
                        step(dve.scalar_tensor_tensor(out=th[:, :], in0=ssq[:, :], scalar=1.0 / DH, in1=th[:, :], op0=ALU.mult, op1=ALU.mult))
                        dve.tensor_scalar(vh[:, :], th[:, :], LN_EPS, None, ALU.add).then_inc(s["lnh"], 1)
                        dve.wait_ge(s["gg"], b + 1)
                        newton_rsqrt(step, dve, rh[:, :], vh[:, :], th[:, :])
                        step(dve.tensor_tensor(rh[:, :], rh[:, :], rn[:, :], ALU.mult))
                        dve.tensor_tensor(n[:, :, 0:DH], n[:, :, 0:DH], spread(rh[:, :], 2, DH), ALU.mult).then_inc(s["o"], 1)
                    if i < NB:
                        dve.wait_ge(s["r1"], i + 1)
                        newton_rsqrt(step, dve, ra[:, :], va[:, :], ta[:, :])
                        if i >= 1:
                            dve.wait_ge(s["tfull"], number["q", i - 1, CH - 1] + 1)
                        for j in range(TILES):
                            ins = dve.tensor_scalar(q[:, j, :], xs[:, i % XBUF, j, :], mv[:, j, 0:1], ra[:, j:j + 1], ALU.subtract, ALU.mult)
                        ins.then_inc(s["q"], 1)
                    if 0 <= i - 3 < NB:
                        b = i - 3
                        dve.wait_ge(s["ow"], b + 1)
                        xb = xs[:, b % XBUF, :, :]
                        ins = dve.tensor_tensor(xb.rearrange("p j (h d) -> p (j h) d", d=DH), xb.rearrange("p j (h d) -> p (j h) d", d=DH),
                                                nsb[:, :, :, :].rearrange("p j h w -> p (j h) w")[:, :, 0:DH], ALU.add)
                        ins.then_inc(s["x2"], 1)
                        dve.wait_ge(s["x2"], b + 1)
                        if b >= 2:
                            dve.wait_ge(s_fst[b % 2], 16 * (b // 2))
                        statistics(xb, st2, mv2, vb[:, :]).then_inc(s["v2"], 1)
                        dve.wait_ge(s["r2"], b + 1)
                        newton_rsqrt(step, dve, rb[:, :], vb[:, :], tb[:, :])
                        for j in range(TILES):
                            ins = dve.tensor_scalar(xfb[:, b % 2, j, 0:E_DIM], xb[:, j, :], mv2[:, j, 0:1], rb[:, j:j + 1], ALU.subtract, ALU.mult)
                        ins.then_inc(s["xf2"], 1)
                    if 0 <= i - 2 < NB:
                        b = i - 2
                        for h in range(HEADS):
                            n = HEADS * b + h
                            dve.wait_ge(s["dd"], n + 1)
                            dve.wait_ge(s["qk"], n + 1)
                            dve.tensor_tensor(C[:, h, :], QK[h % 2][:, :], D[:, h % 2, :], ALU.mult).then_inc(s["cc"], 1)
                            if h in (0, 2, 4):
                                j = h // 2
                                t = filled(dve, "st", b, j)
                                fresh = t[:, 0:PAIRS * VW].rearrange("k (p w) -> k p w", w=VW)
                                for par in range(2):
                                    r, w = slice(DH * par, DH * par + DH), slice(VW * par, VW * par + VW)
                                    if j == 0:
                                        ins = dve.tensor_copy(S[r, 0, :, w], fresh[r])
                                    else:
                                        gate = spread(gb[r, j - 1, par:HEADS:2], 2, VW)
                                        ins = dve.tensor_tensor(S[r, j, :, w], S[r, j - 1, :, w], gate, ALU.mult)
                                if j:
                                    step(ins)
                                    for par in range(2):
                                        r, w = slice(DH * par, DH * par + DH), slice(VW * par, VW * par + VW)
                                        ins = dve.tensor_tensor(S[r, j, :, w], S[r, j, :, w], fresh[r], ALU.add)
                                ins.then_inc(s["td"], 1)
                                dve.wait_ge(*freed[number["st", b, j]])
                            elif h != HEADS - 1:
                                p = {1: 0, 3: 1, 5: 2, 6: 3}[h]
                                t = filled(dve, "qw", b, p)
                                dve.scalar_tensor_tensor(out=qw[:, p, :], in0=qT[:, b % 2, p, P:SEQ], scalar=DH ** -0.5,
                                                         in1=t[:, 0:SEQ - P], op0=ALU.mult, op1=ALU.mult).then_inc(s["td"], 1)
                    if 0 <= i - 1 < NB:
                        b = i - 1
                        dve.wait_ge(s["gates"], b + 1)
                        fb = gbias[32:40, 0:1]
                        dve.tensor_scalar(ee[:, :], G[32:40, :], fb, None, ALU.add).then_inc(s["vg"], 1)
                        dve.tensor_scalar(MM[:, :], G[32:40, :], fb, 0.0, ALU.add, ALU.min)
                        dve.tensor_scalar(aa[:, :], G[0:8, :], gbias[0:8, 0:1], None, ALU.add).then_inc(s["gput"], 1)
                        dve.wait_ge(s["gput"], b + 1)
                        dve.wait_ge(s["gx"], b + 1)
                        step(dve.tensor_tensor_scan(cs[:, :], MM[:, :], ee[:, :], 0.0, ALU.add, ALU.subtract))
                        step(dve.tensor_tensor(aa[:, :], aa[:, :], cs[:, :], ALU.subtract))
                        step(dve.tensor_tensor_scan(MM[:, :], aa[:, :], aa[:, :], -3.0e38, ALU.max, ALU.max))
                        M3 = MM[:, :].rearrange("h (j s) -> h j s", j=TILES)
                        a3 = aa[:, :].rearrange("h (j s) -> h j s", j=TILES)
                        end = M3[:, :, P - 1:P]
                        dve.tensor_tensor(Z[0:8, :].rearrange("h (j s) -> h j s", j=TILES), a3, end.to_broadcast([8, TILES, P]), ALU.subtract)
                        dve.tensor_tensor(Z[32:40, P:SEQ].rearrange("h (j s) -> h j s", s=P), end[:, 0:3, :].to_broadcast([8, 3, P]), M3[:, 1:4, :], ALU.subtract)
                        dve.tensor_tensor(gd[:, :].unsqueeze(2), end[:, 0:2, :], end[:, 1:3, :], ALU.subtract)
                        dve.scalar_tensor_tensor(out=Z[64:72, :], in0=cs[:, :], scalar=-1.0, in1=MM[:, :], op0=ALU.mult, op1=ALU.subtract)\
                            .then_inc(s["zz"], 1)
                        dve.tensor_copy(Zx[96:104, :], aa[:, :])
                        step(dve.tensor_scalar(Mhl[0:8, :], MM[:, :], -1.0, None, ALU.mult))
                        dve.tensor_tensor(Mhl[32:40, :], MM[:, :], Mhl[0:8, :].bitcast(FP32), ALU.add)
                        dve.wait_ge(s["zx"], 2 * b + 2)
                        step(dve.tensor_copy(whl[32:40, :], Zx[32:40, P:SEQ]))
                        dve.tensor_tensor(whl[0:8, :], Zx[32:40, P:SEQ], whl[32:40, :].bitcast(FP32), ALU.subtract)
                        dve.tensor_tensor(gdiag[:, :, :], spread(gd[:, :], 2, 8), spread(ident[0:8, 0:8], 1, 2), ALU.mult).then_inc(s["ms"], 1)


def weight_pieces():
    pieces = []
    for e in range(NEXP):
        if e % 2 == 0:
            pieces += [("up", e, c, c + 1) for c in range(CH)]
        pieces += [("down", e, c, min(c + 2, FCH)) for c in range(0, FCH, 2)]
    return pieces


class Weights:

    def __init__(self, nc, io, ctx):
        def sb(name, shape, dt):
            return ctx.enter_context(nc.sbuf_tensor(name, shape, dt))

        self.io = io
        self.up = [sb("up_hi", [P, CH, FDIM], FP32R), sb("up_lo", [P, CH, FDIM], FP32R)]
        self.down = [sb("down_hi", [P, FCH, E_DIM], FP32R), sb("down_lo", [P, FCH, E_DIM], FP32R)]
        self.raw = sb("w_raw", [P, 2, FDIM + 1], FP32)
        self.loaded = [ctx.enter_context(nc.semaphore(f"w_loaded{n}")) for n in range(2)]
        self.hi_done = ctx.enter_context(nc.semaphore("w_hi_done"))
        self.lo_done = ctx.enter_context(nc.semaphore("w_lo_done"))
        self.pieces = weight_pieces()

    def parts(self, m):
        kind, e, a, b = self.pieces[m]
        raw = self.raw[:, m % 2, :]
        if kind == "up":
            src = self.io["Wup"][e // 2].rearrange("(c p) f -> p c f", p=P)[:, a, :]
            return [(src, raw[:, 0:FDIM], self.up[0][:, a, :], self.up[1][:, a, :])]
        if b < FCH:
            src = self.io["Wdown"][e, a * P:b * P, :].rearrange("(c p) n -> p c n", p=P)
            return [(src, raw[:, 0:(b - a) * E_DIM].rearrange("p (c n) -> p c n", n=E_DIM),
                     self.down[0][:, a:b, :], self.down[1][:, a:b, :])]
        out = []
        for c in range(a, b):
            rows = P if c < FCH - 1 else FLAST
            out.append((self.io["Wdown"][e, c * P:c * P + rows, :], raw[0:rows, (c - a) * E_DIM:(c - a + 1) * E_DIM],
                        self.down[0][0:rows, c, :], self.down[1][0:rows, c, :]))
        return out

    def due(self, m):
        return self.loaded[m % 2], sum(16 * len(self.parts(n)) for n in range(m % 2, m + 1, 2))

    def load(self, eng, m):
        if m >= 2:
            eng.wait_ge(self.lo_done, m - 1)
        for src, raw, _, _ in self.parts(m):
            eng.dma_start(raw, src).then_inc(self.loaded[m % 2], 16)

    def hi(self, act, m):
        act.wait_ge(*self.due(m))
        for _, raw, hi, _ in self.parts(m):
            ins = act.activation(hi, raw, ACT.Copy)
        ins.then_inc(self.hi_done, 1)

    def lo(self, eng, m):
        eng.wait_ge(self.hi_done, m + 1)
        for _, raw, hi, lo in self.parts(m):
            ins = eng.tensor_tensor(lo, raw, hi.bitcast(FP32), ALU.subtract)
        ins.then_inc(self.lo_done, 1)

    def upto(self, kind, e):
        return max(m for m, p in enumerate(self.pieces) if p[0] == kind and p[1] <= e) + 1


def choose(nc, dram, sm_all, slots, weights, consts, NTOK, K):
    GROUP = P // NEXP
    SPAN = NTOK // GROUP
    NT = NTOK // P
    STEPS = (SPAN - 1).bit_length()
    VALID = 1 << STEPS
    TOP_BIT = 29
    I16, FP16 = mybir.dt.int16, mybir.dt.float16
    KC = K // P
    ident = consts["ident"]
    with ExitStack() as ctx:
        def sb(name, shape, dt=FP32):
            return ctx.enter_context(nc.sbuf_tensor(name, shape, dt))

        def sem(name):
            return ctx.enter_context(nc.semaphore("c_" + name))

        turned = sb("turned", [NT, NEXP, P])
        V = sb("V", [P, SPAN])
        hit = sb("hit", [P, SPAN], FP16)
        over = sb("over", [P, SPAN]); same = sb("same", [P, SPAN]); rank = sb("rank", [P, SPAN])
        place = sb("place", [P, SPAN])
        ent = [sb("ent0", [P, SPAN], I16), sb("ent1", [P, SPAN], I16)]
        moving = sb("moving", [P, SPAN], I16); moved = sb("moved", [P, SPAN], I16)
        ids = sb("ids", [P, SPAN], I32)
        count = sb("count", [P, 1], FP16); low = sb("low", [P, 1], I32); cand = sb("cand", [P, 1], I32); bit = sb("bit", [P, 1], I32)
        same_groups = sb("same_groups", [P, P], FP16)
        groups32 = sb("groups32", [P, P]); before = sb("before", [P, P])
        tot = sb("tot", [P, 1]); need = sb("need", [P, 1]); offs = sb("offs", [P, 1]); nq = sb("nq", [P, 1]); wide = sb("wide", [P, P])
        base = sb("base", [P, P]); jump = sb("jump", [P, P])
        slot = sb("slot", [P, KC]); home = sb("home", [P, NEXP, KC])
        cmp_ = sb("cmp_", [P, NEXP, KC, GROUP - 1]); addr = sb("addr", [P, NEXP, KC])
        pst = ctx.enter_context(nc.psum_tensor("c_pst", [NT, NEXP, P], FP32))
        pc = ctx.enter_context(nc.psum_tensor("c_pc", [P, 512], FP32))
        s = {n: sem(n) for n in "turn out saved V pool cnt sum dve tie mm wide bases list done".split()}
        with nc.Block() as block:
            @block.sync
            def _(sp):
                for m in range(2):
                    weights.load(sp, m)
                sp.wait_ge(s["out"], 1)
                sp.dma_start(dram["gates"].rearrange("e (t p) -> t e p", p=P), turned[:, :, :]).then_inc(s["saved"], 16)
                sp.wait_ge(s["saved"], 16)
                sp.dma_start(V[:, :], dram["gates"].rearrange("e (q n) -> (e q) n", q=GROUP)).then_inc(s["V"], 16)
                for m in range(2, weights.upto("down", 0)):
                    weights.load(sp, m)
                sp.wait_ge(s["done"], 1)
                sp.dma_start(dram["list"].rearrange("(g n) o -> g (n o)", g=P), ids[:, :]).then_inc(s["list"], 16)
                sp.wait_ge(s["list"], 16)

            @block.scalar
            def _(act):
                for m in range(weights.upto("down", 0)):
                    weights.hi(act, m)

            @block.gpsimd
            def _(pool):
                step = Chain(pool, s["pool"])
                g3 = groups32[:, :].rearrange("k (a b) -> k a b", b=GROUP)
                step(pool.memset(groups32[:, :], 1.0))
                step(pool.affine_select(out=g3, in_=g3, compare_op=ALU.is_ge, fill=0.0, base=0,
                                        pattern=[[-GROUP, NEXP], [0, GROUP]], channel_multiplier=1))
                step(pool.affine_select(out=g3, in_=g3, compare_op=ALU.is_ge, fill=0.0, base=GROUP - 1,
                                        pattern=[[GROUP, NEXP], [0, GROUP]], channel_multiplier=-1))
                step(pool.affine_select(out=before[:, :], in_=groups32[:, :], compare_op=ALU.is_gt, fill=0.0, base=0,
                                        pattern=[[1, P]], channel_multiplier=-1))
                step(pool.tensor_copy(same_groups[:, :], groups32[:, :]))
                step(pool.iota(place[:, :], pattern=[[1, SPAN]], base=0, channel_multiplier=0, allow_small_or_imprecise_dtypes=True))
                step(pool.iota(slot[:, :], pattern=[[P, KC]], base=0, channel_multiplier=1, allow_small_or_imprecise_dtypes=True))
                step(pool.iota(home[:, :, :], pattern=[[NTOK, NEXP], [P, KC]], base=0, channel_multiplier=1, allow_small_or_imprecise_dtypes=True))
                for m in range(weights.upto("down", 0)):
                    weights.lo(pool, m)

            @block.tensor
            def _(pe):
                for e in range(NEXP):
                    mm = pe.transpose(pst[:, e, :], sm_all[:, :, e], ident[:, :])
                mm.then_inc(s["turn"], 1)
                pe.wait_ge(s["pool"], 5)
                for n in range(TOP_BIT + 1):
                    pe.wait_ge(s["cnt"], n + 1)
                    pe.matmul(pc[:, 0:1], same_groups[:, :], count[:, :], start=True, stop=True).then_inc(s["sum"], 1)
                pe.wait_ge(s["tie"], 1)
                pe.matmul(pc[:, 0:1], groups32[:, :], tot[:, :], start=True, stop=True).then_inc(s["mm"], 1)
                pe.wait_ge(s["tie"], 2)
                pe.matmul(pc[:, 0:1], before[:, :], offs[:, :], start=True, stop=True).then_inc(s["mm"], 1)
                pe.wait_ge(s["wide"], 1)
                pe.matmul(pc[:, 0:P], wide[:, :], before[:, :], start=True, stop=True)
                pe.matmul(pc[:, P:2 * P], wide[:, :], ident[:, :], start=True, stop=True).then_inc(s["bases"], 1)

            @block.vector
            def _(dve):
                step = Chain(dve, s["dve"])
                dve.wait_ge(s["turn"], 1)
                dve.tensor_copy(turned[:, :, :], pst[:, :, :]).then_inc(s["out"], 1)
                step(dve.memset(low[:, :], 0))
                dve.wait_ge(s["V"], 16)
                for n, k in enumerate(range(TOP_BIT, -1, -1)):
                    step(dve.tensor_scalar(cand[:, :], low[:, :], 1 << k, None, ALU.bitwise_or))
                    dve.tensor_scalar(hit[:, :], V[:, :], cand[:, :].bitcast(FP32), 0.0, ALU.is_ge, ALU.add, accum_out=count[:, :])\
                        .then_inc(s["cnt"], 1)
                    dve.wait_ge(s["sum"], n + 1)
                    step(dve.tensor_scalar(bit[:, :], pc[:, 0:1], float(K), float(1 << k), ALU.is_ge, ALU.mult))
                    step(dve.tensor_tensor(low[:, :], low[:, :], bit[:, :], ALU.bitwise_or))
                least = low[:, :].bitcast(FP32)
                dve.wait_ge(s["pool"], 8)
                dve.tensor_scalar(over[:, :], V[:, :], least, 0.0, ALU.is_gt, ALU.add, accum_out=tot[:, :]).then_inc(s["tie"], 1)
                dve.tensor_scalar(same[:, :], V[:, :], least, 0.0, ALU.is_equal, ALU.add, accum_out=offs[:, :])
                dve.wait_ge(s["mm"], 1)
                step(dve.tensor_scalar(need[:, :], pc[:, 0:1], -1.0, float(K), ALU.mult, ALU.add))
                dve.tensor_tensor_scan(rank[:, :], same[:, :], same[:, :], 0.0, ALU.add, ALU.bypass).then_inc(s["tie"], 1)
                dve.wait_ge(s["mm"], 2)
                step(dve.tensor_tensor(need[:, :], need[:, :], pc[:, 0:1], ALU.subtract))
                step(dve.scalar_tensor_tensor(out=same[:, :], in0=rank[:, :], scalar=need[:, :], in1=same[:, :], op0=ALU.is_le, op1=ALU.mult))
                step(dve.tensor_tensor(over[:, :], over[:, :], same[:, :], ALU.add))
                step(dve.tensor_tensor_scan(rank[:, :], over[:, :], over[:, :], 0.0, ALU.add, ALU.bypass))
                step(dve.tensor_copy(nq[:, :], rank[:, SPAN - 1:SPAN]))
                dve.tensor_scalar(wide[:, :], groups32[:, :], 0.0, nq[:, :], ALU.mult, ALU.add).then_inc(s["wide"], 1)
                step(dve.tensor_tensor(rank[:, :], place[:, :], rank[:, :], ALU.subtract))
                step(dve.scalar_tensor_tensor(out=ent[0][:, :], in0=rank[:, :], scalar=float(VALID + 1), in1=over[:, :], op0=ALU.add, op1=ALU.mult))
                for k in range(STEPS):
                    old, new = ent[k % 2], ent[1 - k % 2]
                    d = 1 << k
                    step(dve.tensor_scalar(moving[:, :], old[:, :], d, None, ALU.bitwise_and))
                    step(dve.scalar_tensor_tensor(out=new[:, :], in0=moving[:, :], scalar=0.0, in1=old[:, :], op0=ALU.is_equal, op1=ALU.mult))
                    step(dve.tensor_tensor(moved[:, :], old[:, :], new[:, :], ALU.subtract))
                    step(dve.tensor_tensor(new[:, 0:SPAN - d], new[:, 0:SPAN - d], moved[:, d:SPAN], ALU.add))
                step(dve.tensor_scalar(moving[:, :], ent[STEPS % 2][:, :], VALID - 1, None, ALU.bitwise_and))
                step(dve.tensor_tensor(rank[:, :], place[:, :], moving[:, :], ALU.add))
                dve.tensor_scalar(ids[:, :], rank[:, :], consts["span0"][:, 0:1], None, ALU.add).then_inc(s["done"], 1)
                dve.wait_ge(s["bases"], 1)
                dve.tensor_copy(base[:, :], pc[:, 0:P])
                step(dve.tensor_scalar(jump[:, :], pc[:, P:2 * P], -1.0, float(SPAN), ALU.mult, ALU.add))
                b3 = base[:, :].rearrange("p (e q) -> p e q", e=NEXP)[:, :, 1:GROUP]
                j3 = jump[:, :].rearrange("p (e q) -> p e q", e=NEXP)[:, :, 0:GROUP - 1]
                for e in range(NEXP):
                    ins = dve.tensor_tensor(cmp_[:, e, :, :], spread(b3[:, e, :], 1, KC), spread(slot[:, :], 2, GROUP - 1), ALU.is_le)
                step(ins)
                for e in range(NEXP):
                    ins = dve.tensor_tensor(cmp_[:, e, :, :], cmp_[:, e, :, :], spread(j3[:, e, :], 1, KC), ALU.mult)
                step(ins)
                step(dve.tensor_reduce(addr[:, :, :], cmp_[:, :, :, :], AX.X, ALU.add))
                step(dve.tensor_tensor(slots[:, :].rearrange("p (e t) -> p e t", e=NEXP), addr[:, :, :], home[:, :, :], ALU.add))


def experts(nc, io, dram, slots, weights, tg, consts, NTOK, K):
    BLK = 4 * P
    BPE = K // BLK
    NBLK = NEXP * BPE
    ident = consts["ident"]
    rows_v, list_v = dram["xf"], dram["list"]
    out_rows = io["out"].rearrange("b s e -> (b s) e")
    with ExitStack() as ctx:
        def sb(name, shape, dt=FP32):
            return ctx.enter_context(nc.sbuf_tensor(name, shape, dt))

        def sem(name):
            return ctx.enter_context(nc.semaphore("e_" + name))

        xg = sb("xg", [P, 4, XW])
        xT = [sb("xT_hi", [P, CH, BLK], FP32R), sb("xT_lo", [P, CH, BLK], FP32R)]
        mid = [sb("mid_hi", [P, FCH, BLK], FP32R), sb("mid_lo", [P, FCH, BLK], FP32R)]
        z = sb("z", [P, 2, BLK])
        y = sb("y", [P, 4, E_DIM])
        gs = sb("gs", [P, 2, 4])
        bup = sb("bup", [P, NEXP // 2, FCH])
        bdn = sb("bdn", [P, 2, E_DIM])
        idx = sb("idx", [P, 2, 4], I32)
        UP = [ctx.enter_context(nc.psum_tensor(f"UP{n}", [P, BLK], FP32)) for n in range(3)]
        DN = [ctx.enter_context(nc.psum_tensor(f"DN{n}", [P, E_DIM], FP32)) for n in range(2)]
        T = [ctx.enter_context(nc.psum_tensor(f"TT{n}", [P, BLK], FP32)) for n in range(2)]
        s = {n: sem(n) for n in "bup rows up z hi mid dn yp y tfull thi tlo gs dve".split()}
        s_ix = [sem(f"ix{n}") for n in range(2)]
        s_sc = [sem(f"sc{n}") for n in range(4)]
        s_bd = [sem(f"bd{n}") for n in range(2)]

        def rows_of(f):
            return P if f < FCH - 1 else FLAST

        first_down = weights.upto("down", 0)

        def down_pieces(n):
            e = n // BPE
            return [] if n % BPE or e == 0 else list(range(weights.upto("down", e) - (FCH + 1) // 2, weights.upto("down", e)))

        def up_pieces(n):
            e = (n + 1) // BPE
            return list(range(weights.upto("up", e) - CH, weights.upto("up", e))) if (n + 1) % BPE == 0 and e % 2 == 0 and e < NEXP else []

        with nc.Block() as block:
            @block.sync
            def _(sp):
                full = (FCH - 1) * P
                with nc.allow_non_contiguous_dma(reason="biases by partition, once"):
                    for g in range(NEXP // 2):
                        sp.dma_start(bup[:, g, 0:FCH - 1], io["bup"][g, 0:full].rearrange("(c p) -> p c", p=P)).then_inc(s["bup"], 16)
                        sp.dma_start(bup[0:FLAST, g, FCH - 1:FCH], io["bup"][g, full:FDIM].unsqueeze(1)).then_inc(s["bup"], 16)
                m = first_down
                for e in range(NEXP):
                    if e >= 2:
                        sp.wait_ge(s["y"], 4 * BPE * (e - 1))
                    sp.dma_start(bdn[:, e % 2, :], io["bdown"][e].partition_broadcast(P)).then_inc(s_bd[e % 2], 16)
                    while e + 1 < NEXP and m < weights.upto("down", e + 1):
                        weights.load(sp, m)
                        m += 1

            @block.gpsimd
            def _(pool):
                def list_rows(n):
                    if n >= 2:
                        for t in range(4):
                            pool.wait_ge(s_sc[t], 16 * (n - 1))
                    for t in range(4):
                        pool.indirect_dma_start(idx[:, n % 2, t:t + 1], None, list_v, bass.IndirectOffsetOnAxis(
                            ap=slots[:, 4 * n + t:4 * n + t + 1], axis=0)).then_inc(s_ix[n % 2], 16)

                def gather(n):
                    pool.wait_ge(s_ix[n % 2], 64 * (n // 2 + 1))
                    if n >= 1:
                        pool.wait_ge(s["tfull"], CH * n)
                        pool.wait_ge(s["gs"], n)
                    for t in range(4):
                        pool.indirect_dma_start(xg[:, t, :], None, rows_v, bass.IndirectOffsetOnAxis(
                            ap=idx[:, n % 2, t:t + 1].bitcast(U32), axis=0)).then_inc(s["rows"], 16)

                list_rows(0)
                gather(0)
                if NBLK > 1:
                    list_rows(1)
                for n in range(NBLK):
                    if n + 1 < NBLK:
                        gather(n + 1)
                    for t in range(4):
                        m = 4 * n + t
                        pool.wait_ge(s["y"], m + 1)
                        if n % BPE == 0 and n and t == 0:
                            for u in range(4):
                                pool.wait_ge(s_sc[u], 16 * n)
                        pool.indirect_dma_start(out_rows, bass.IndirectOffsetOnAxis(ap=idx[:, n % 2, t:t + 1].bitcast(U32), axis=0),
                                                y[:, t, :], None, compute_op=ALU.add).then_inc(s_sc[t], 16)
                    if n + 2 < NBLK:
                        list_rows(n + 2)
                for t in range(4):
                    pool.wait_ge(s_sc[t], 16 * NBLK)

            @block.scalar
            def _(act):
                def turn_hi(n, c):
                    act.wait_ge(s["tfull"], CH * n + c + 1)
                    act.activation(xT[0][:, c, :], T[c % 2][:, :], ACT.Copy).then_inc(s["thi"], 1)

                act.wait_ge(s["bup"], 16 * NEXP)
                for c in range(CH):
                    turn_hi(0, c)
                for n in range(NBLK):
                    e = n // BPE
                    more = down_pieces(n)
                    for f in range(FCH):
                        k, r = FCH * n + f, rows_of(f)
                        act.wait_ge(s["up"], k + 1)
                        if k >= 2:
                            act.wait_ge(s["mid"], k - 1)
                        act.activation(z[0:r, k % 2, :], UP[k % 3][0:r, :], ACT.Silu, bias=bup[0:r, e // 2, f:f + 1]).then_inc(s["z"], 1)
                        if more:
                            weights.hi(act, more.pop(0))
                    more = up_pieces(n)
                    for t in range(4):
                        if n + 1 < NBLK:
                            turn_hi(n + 1, t)
                        if more:
                            weights.hi(act, more.pop(0))

            @block.tensor
            def _(pe):
                def turn(n, c):
                    k = CH * n + c
                    if c == 0:
                        pe.wait_ge(s["rows"], 64 * (n + 1))
                    if k >= 2:
                        pe.wait_ge(s["tlo"], k - 1)
                    for t in range(4):
                        mm = pe.transpose(T[c % 2][:, t * P:(t + 1) * P], xg[:, t, c * P:(c + 1) * P], ident[:, :])
                    mm.then_inc(s["tfull"], 1)

                for c in range(CH):
                    turn(0, c)
                for n in range(NBLK):
                    e = n // BPE
                    if n % BPE == 0:
                        pe.wait_ge(weights.lo_done, weights.upto("up", e))
                    pe.wait_ge(s["tlo"], CH * (n + 1))
                    for f in range(FCH):
                        k, r = FCH * n + f, rows_of(f)
                        if k >= 3:
                            pe.wait_ge(s["z"], k - 2)
                        first = True
                        for c in range(CH):
                            for wa, xa in ((0, 0), (0, 1), (1, 0)):
                                mm = pe.matmul(UP[k % 3][0:r, :], weights.up[wa][:, c, f * P:f * P + r], xT[xa][:, c, :],
                                               start=first, stop=(c == CH - 1 and wa == 1))
                                first = False
                        mm.then_inc(s["up"], 1)
                    if n % BPE == 0:
                        pe.wait_ge(weights.lo_done, weights.upto("down", e))
                    for t in range(4):
                        if n + 1 < NBLK:
                            turn(n + 1, t)
                        m = 4 * n + t
                        if m >= 2:
                            pe.wait_ge(s["yp"], m - 1)
                        if t == 0:
                            pe.wait_ge(s["mid"], FCH * (n + 1))
                        first = True
                        for f in range(FCH):
                            r = rows_of(f)
                            for ma, wa in ((0, 0), (0, 1), (1, 0)):
                                mm = pe.matmul(DN[m % 2][:, :], mid[ma][0:r, f, t * P:(t + 1) * P], weights.down[wa][0:r, f, :],
                                               start=first, stop=(f == FCH - 1 and ma == 1))
                                first = False
                        mm.then_inc(s["dn"], 1)

            @block.vector
            def _(dve):
                def turn_lo(n, c):
                    k = CH * n + c
                    dve.wait_ge(s["thi"], k + 1)
                    dve.tensor_tensor(xT[1][:, c, :], T[c % 2][:, :], xT[0][:, c, :].bitcast(FP32), ALU.subtract).then_inc(s["tlo"], 1)

                def gate(n):
                    e = n // BPE
                    dve.wait_ge(s["rows"], 64 * (n + 1))
                    dve.tensor_scalar(gs[:, n % 2, :], xg[:, :, E_DIM + e], tg["ap"][:, 1:2], None, ALU.mult).then_inc(s["gs"], 1)

                gate(0)
                for c in range(CH):
                    turn_lo(0, c)
                for n in range(NBLK):
                    e = n // BPE
                    more = down_pieces(n)
                    for f in range(FCH):
                        k, r = FCH * n + f, rows_of(f)
                        dve.wait_ge(s["z"], k + 1)
                        dve.tensor_copy(mid[0][0:r, f, :], z[0:r, k % 2, :]).then_inc(s["hi"], 1)
                        dve.wait_ge(s["hi"], k + 1)
                        dve.tensor_tensor(mid[1][0:r, f, :], z[0:r, k % 2, :], mid[0][0:r, f, :].bitcast(FP32), ALU.subtract)\
                            .then_inc(s["mid"], 1)
                        if more:
                            weights.lo(dve, more.pop(0))
                    more = up_pieces(n)
                    if n % BPE == 0:
                        dve.wait_ge(s_bd[e % 2], 16 * (e // 2 + 1))
                    for t in range(4):
                        if n + 1 < NBLK:
                            if t == 0:
                                gate(n + 1)
                            turn_lo(n + 1, t)
                        if more:
                            weights.lo(dve, more.pop(0))
                        m = 4 * n + t
                        dve.wait_ge(s["dn"], m + 1)
                        if n:
                            dve.wait_ge(s_sc[t], 16 * n)
                        dve.tensor_tensor(y[:, t, :], DN[m % 2][:, :], bdn[:, e % 2, :], ALU.add).then_inc(s["yp"], 1)
                        dve.wait_ge(s["yp"], m + 1)
                        dve.tensor_scalar(y[:, t, :], y[:, t, :], gs[:, n % 2, t:t + 1], None, ALU.mult).then_inc(s["y"], 1)


def program(nc, x, ctx_, g_x, g_f, igw, igb, fgw, fgb, outw, Wr, br, Wup, bup, Wdown, bdown, out):
    NB = x.shape[0]
    NTOK = NB * SEQ
    K = NTOK // NEXP
    io = dict(x=x, ctx=ctx_, igw=igw, igb=igb, fgw=fgw, fgb=fgb, outw=outw, Wr=Wr, br=br,
              Wup=Wup, bup=bup, Wdown=Wdown, bdown=bdown, out=out)
    dram = {
        "xf": nc.dram_tensor("rows_scratch", (NTOK, XW), FP32).ap(),
        "gates": nc.dram_tensor("gates_scratch", (NEXP, NTOK), FP32).ap(),
        "list": nc.dram_tensor("list_scratch", (NEXP * NTOK, 1), I32).ap(),
    }
    with ExitStack() as c:
        def sb(name, shape, dt=FP32):
            return c.enter_context(nc.sbuf_tensor(name, shape, dt))

        ident = sb("ident", [P, P]); ones = sb("ones", [P, P]); identb = sb("identb", [P, P], BF16)
        tgt = sb("tanh_g", [P, 2])
        span0 = sb("span0", [P, 1]); part = sb("part", [P, 1], I32)
        sm_all = sb("sm_all", [P, NB * TILES, NEXP])
        slots = sb("slots", [P, NEXP * K // P], U32)
        s_con, s_g, s_tg, s_sp = (c.enter_context(nc.semaphore(n)) for n in ("s_con", "s_g", "s_tg", "s_sp"))
        SPAN = NTOK // (P // NEXP)
        with nc.Block() as block:
            @block.gpsimd
            def _(pool):
                step = Chain(pool, s_con)
                step(pool.memset(ident[:, :], 0.0))
                step(pool.memset(ones[:, :], 1.0))
                step(pool.affine_select(out=ident[:, :], in_=ident[:, :], compare_op=ALU.not_equal, fill=1.0,
                                        base=0, pattern=[[-1, P]], channel_multiplier=1))
                step(pool.tensor_copy(identb[:, :], ident[:, :]))
                step(pool.iota(part[:, :], pattern=[[0, 1]], base=0, channel_multiplier=SPAN))

            @block.scalar
            def _(act):
                act.dma_start(tgt[:, 0:1], g_x.partition_broadcast(P)).then_inc(s_g, 16)
                act.dma_start(tgt[:, 1:2], g_f.partition_broadcast(P)).then_inc(s_g, 16)
                act.wait_ge(s_g, 32)
                act.activation(tgt[:, :], tgt[:, :], ACT.Tanh).then_inc(s_tg, 1)

            @block.vector
            def _(dve):
                dve.wait_ge(s_con, 5)
                dve.tensor_scalar(part[:, :], part[:, :], NTOK - 1, None, ALU.bitwise_and).then_inc(s_sp, 1)
                dve.wait_ge(s_sp, 1)
                dve.tensor_copy(span0[:, :], part[:, :]).then_inc(s_sp, 1)
        consts = dict(ident=ident, identb=identb, ones=ones, span0=span0, sem=s_con, ready=5)
        tg = dict(sem=s_tg, ready=1, ap=tgt)
        attention(nc, io, NB, dram, sm_all, tg, consts)
        with ExitStack() as wctx:
            weights = Weights(nc, io, wctx)
            choose(nc, dram, sm_all, slots, weights, consts, NTOK, K)
            experts(nc, io, dram, slots, weights, tg, consts, NTOK, K)


_INS = ["x", "ctx_1024", "g_xattn", "g_ffn", "L0_xattn_igate_w", "L0_xattn_igate_b", "L0_xattn_fgate_w", "L0_xattn_fgate_b",
        "L0_xattn_out_w", "L0_ffn_Wr", "L0_ffn_br", "L0_ffn_W_up", "L0_ffn_b_up", "L0_ffn_W_down", "L0_ffn_b_down"]


def kernel(**inputs):
    import concourse.bacc as bacc
    from concourse.bass_utils import run_bass_kernel_spmd

    nc = bacc.Bacc("TRN2", target_bir_lowering=False, num_devices=1)
    arrays, args = {}, []
    for name in _INS:
        a = np.ascontiguousarray(inputs[name])
        arrays[f"in_{name}"] = a
        args.append(nc.dram_tensor(f"in_{name}", a.shape, mybir.dt.from_np(a.dtype), kind="ExternalInput").ap())
    shape = inputs["x"].shape
    args.append(nc.dram_tensor("out_x", shape, FP32, kind="ExternalOutput").ap())
    program(nc, *args)
    r = run_bass_kernel_spmd(nc, [arrays], core_ids=[0])
    return r.results[0]["out_x"]
```

```python
import numpy as np
import concourse.bass as bass
from concourse import mybir
from concourse.alu_op_type import AluOpType as ALU
from contextlib import ExitStack

FP32 = mybir.dt.float32
FP32R = mybir.dt.float32r
BF16 = mybir.dt.bfloat16
I32 = mybir.dt.int32
U32 = mybir.dt.uint32
ACT = mybir.ActivationFunctionType
AX = mybir.AxisListType

P = 128
E_DIM = 512
TILES = 4
SEQ = TILES * P
HEADS = 8
DH = E_DIM // HEADS
PAIRS = HEADS // 2
CH = E_DIM // P
VW = DH + 2
ROWW = HEADS * VW
NEXP = 8
FDIM = int(E_DIM * 4 * (2.0 / 3.0))
FCH = -(-FDIM // P)
FLAST = FDIM - (FCH - 1) * P
XW = E_DIM + NEXP
QD = 32
LN_EPS = 1e-5
NORM_EPS = 1e-6
BIG = 1e30
XBUF = 4
VBUF = 3


class Line:

    def __init__(self, sem):
        self.sem, self.n = sem, 0

    def inc(self, instruction, by=1):
        instruction.then_inc(self.sem, by)
        self.n += by
        return self.n


class Chain:

    def __init__(self, eng, sem):
        self.eng, self.line = eng, Line(sem)

    def __call__(self, instruction):
        self.eng.wait_ge(self.line.sem, self.line.inc(instruction))


def spread(ap, axis, n):
    ap = ap.unsqueeze(axis)
    return ap.to_broadcast([n if i == axis else s for i, s in enumerate(ap.shape)])


def newton_rsqrt(step, eng, y, v, t):
    step(eng.tensor_tensor(t, y, y, ALU.mult))
    step(eng.tensor_tensor(t, t, v, ALU.mult))
    step(eng.tensor_scalar(t, t, -0.5, 1.5, ALU.mult, ALU.add))
    step(eng.tensor_tensor(y, y, t, ALU.mult))


def attention(nc, io, NB, dram, sm_all, tg, consts):
    x_v = io["x"].rearrange("b (j p) e -> b p j e", p=P)
    c_v = io["ctx"].rearrange("b (j p) e -> b p j e", p=P)
    out_v = io["out"].rearrange("b (j p) e -> b p j e", p=P)
    xf_v = dram["xf"].rearrange("(b j p) w -> b p j w", j=TILES, p=P)
    ident, identb, ones = consts["ident"], consts["identb"], consts["ones"]
    with ExitStack() as ctx:
        def sb(name, shape, dt=FP32):
            return ctx.enter_context(nc.sbuf_tensor(name, shape, dt))

        def pb(name, shape, dt=FP32):
            return ctx.enter_context(nc.psum_tensor(name, shape, dt))

        def sem(name):
            return ctx.enter_context(nc.semaphore(name))

        xs = sb("xs", [P, XBUF, TILES, E_DIM])
        half = sb("half", [P, TILES, HEADS, DH // 2])
        vaug = sb("vaug", [P, VBUF, TILES * ROWW + P])
        q = sb("q", [P, TILES, E_DIM])
        qT = sb("qT", [P, 2, CH, SEQ])
        kT = sb("kT", [P, CH, SEQ])
        kpad = sb("kpad", [P, 2, CH, SEQ])
        xfb = sb("xfb", [P, 2, TILES, XW])
        C = sb("C", [P, HEADS, SEQ])
        D = sb("D", [P, 2, SEQ])
        qw = sb("qw", [P, CH, SEQ - P])
        uv = sb("uv", [P, TILES - 1, HEADS, VW])
        S = sb("S", [P, TILES - 1, PAIRS, 2 * VW])
        nsb = sb("nsb", [P, TILES, HEADS, VW])
        ee = sb("ee", [8, SEQ]); cs = sb("cs", [8, SEQ]); aa = sb("aa", [8, SEQ])
        MM = sb("MM", [8, SEQ])
        Z = sb("Z", [72, SEQ]); Zx = sb("Zx", [104, SEQ])
        Mhl = sb("Mhl", [40, SEQ], FP32R)
        whl = sb("whl", [40, SEQ - P], FP32R)
        gd = sb("gd", [8, 2]); gdiag = sb("gdiag", [8, 2, 8]); gb = sb("gb", [P, 2, 8])
        tm = sb("tm", [P, TILES, 4, HEADS])
        selM = sb("selM", [40, HEADS, P], FP32R); selP = sb("selP", [40, PAIRS, P], FP32R)
        maskneg = sb("maskneg", [P, SEQ], BF16)
        gW = sb("gW", [P, 2 * CH, 40])
        gbias = sb("gbias", [40, 1])
        Wr = sb("Wr", [P, CH, NEXP]); br = sb("br", [NEXP, 1]); Wo = sb("Wo", [P, E_DIM])
        st = sb("st", [P, TILES, 6]); mv = sb("mv", [P, TILES, 2]); va = sb("va", [P, TILES]); ra = sb("ra", [P, TILES]); ta = sb("ta", [P, TILES])
        st2 = sb("st2", [P, TILES, 6]); mv2 = sb("mv2", [P, TILES, 2]); vb = sb("vb", [P, TILES]); rb = sb("rb", [P, TILES]); tb = sb("tb", [P, TILES])
        la = sb("la", [P, TILES]); lb = sb("lb", [P, TILES]); lh = sb("lh", [P, TILES * HEADS])
        msum = sb("msum", [P, TILES * HEADS])
        nrm = sb("nrm", [P, 2, TILES * HEADS]); rn = sb("rn", [P, TILES * HEADS]); ssq = sb("ssq", [P, TILES * HEADS])
        vh = sb("vh", [P, TILES * HEADS]); rh = sb("rh", [P, TILES * HEADS]); th = sb("th", [P, TILES * HEADS])
        lt = sb("lt", [P, TILES, NEXP]); mx = sb("mx", [P, TILES]); sx = sb("sx", [P, TILES]); ex = sb("ex", [P, TILES, NEXP])

        xfT = q
        lg = ee
        gwr = C[0:16, 0:3, :].rearrange("g n e -> g (n e)")
        self_ = kT[0:40, 0:2, :].rearrange("k a (h s) -> k (a h) s", s=P)

        T = [pb("T0", [P, SEQ]), pb("T1", [P, SEQ])]
        G = pb("G", [P, SEQ])
        EB = pb("EB", [P, SEQ])
        W = pb("W", [P, 2, SEQ])
        A0 = pb("A0", [P, HEADS, P])
        EX = [EB, G]
        QK = [W[:, 0, :], W[:, 1, :]]
        A = [A0[:, :, :], W[:, :, :].rearrange("p a (h w) -> p (a h) w", w=P)]

        AHEAD = 2
        GCOL = 104
        names = ("tfull ta td init ldw xd v1 r1 q v2 r2 xf2 vg gates gput ex1 ln1 zz zx gg gx "
                 "ms tmf tmd ee dd qk cc af an cen sq lnh lnb rh x2 lex smx vaug kpad uv "
                 "dchain achain pchain prep1 prep2 prep3 prep4 tr0 tr1").split()
        s = {n: sem("a_" + n) for n in names}
        s_xl = [sem(f"a_xl{i}") for i in range(XBUF)]
        s_xst = [sem(f"a_xst{i}") for i in range(XBUF)]
        s_cd = [sem(f"a_cd{i}") for i in range(VBUF)]
        s_fst = [sem(f"a_fst{i}") for i in range(2)]

        order, owner = [], {}

        def iteration_fills(i):
            if 0 <= i - 1 < NB:
                yield from [("q", i - 1, c, "act") for c in range(CH)]
                yield from [("k", i - 1, c, "act") for c in range(CH)]
            if 0 <= i - 2 < NB:
                for h in range(HEADS - 1):
                    yield (("st", i - 2, h // 2, "dve") if h in (0, 2, 4) else
                           ("qw", i - 2, {1: 0, 3: 1, 5: 2, 6: 3}[h], "dve"))
            if 0 <= i - 4 < NB:
                yield from [("xfT", i - 4, c, "act") for c in range(CH)]
                yield ("lg", i - 4, 0, "act")
                yield ("lt", i - 4, 0, "dve")

        number, freed, counts = {}, [], {"act": 0, "dve": 0}
        for i in range(NB + 5):
            for kind, b, k, who in iteration_fills(i):
                number[kind, b, k] = len(freed)
                counts[who] += 1
                freed.append((s["ta" if who == "act" else "td"], counts[who]))

        def bank(kind, b, k):
            return T[number[kind, b, k] % 2]

        def fill(pe, kind, b, k):
            n = number[kind, b, k]
            if n >= 2:
                pe.wait_ge(*freed[n - 2])
            return T[n % 2]

        def filled(eng, kind, b, k):
            eng.wait_ge(s["tfull"], number[kind, b, k] + 1)
            return bank(kind, b, k)

        def v_of(b, j, c0, n):
            return vaug[:, b % VBUF, j * ROWW + c0:j * ROWW + c0 + n]

        def v_all(b):
            return vaug[:, b % VBUF, 0:TILES * ROWW].rearrange("p (j w) -> p j w", w=ROWW)[:, :, 0:E_DIM]

        def v_wide(b, j, h):
            at, more = j * ROWW + DH * h, E_DIM + 2 * h - DH * h
            first = vaug[:, b % VBUF, at:at + DH]
            return bass.AP(tensor=first.tensor, offset=first.offset, ap=[first.ap[0], [more, 2], [1, DH]])

        with nc.Block() as block:
            @block.sync
            def _(sp):
                sp.dma_start(gwr[0:8, :], io["igw"]).then_inc(s["ldw"], 16)
                sp.dma_start(gwr[8:16, :], io["fgw"]).then_inc(s["ldw"], 16)
                sp.dma_start(gbias[0:8, :], io["igb"].unsqueeze(1)).then_inc(s["ldw"], 16)
                sp.dma_start(gbias[32:40, :], io["fgb"].unsqueeze(1)).then_inc(s["ldw"], 16)
                sp.dma_start(Wr[:, :, :], io["Wr"].rearrange("(c p) n -> p c n", p=P)).then_inc(s["ldw"], 16)
                sp.dma_start(br[:, :], io["br"].unsqueeze(1)).then_inc(s["ldw"], 16)
                sp.dma_start(Wo[:, :], io["outw"].partition_broadcast(P)).then_inc(s["ldw"], 16)
                for b in range(min(XBUF, NB)):
                    if b < VBUF:
                        sp.dma_start(v_all(b), c_v[b]).then_inc(s_cd[b % VBUF], 16)
                    sp.dma_start(xs[:, b % XBUF, :, :], x_v[b]).then_inc(s_xl[b % XBUF], 16)
                for i in range(NB + 5):
                    if VBUF <= i < NB:
                        sp.wait_ge(s["af"], TILES * (i - VBUF + 1))
                        sp.dma_start(v_all(i), c_v[i]).then_inc(s_cd[i % VBUF], 16)
                    if XBUF <= i < NB:
                        sp.wait_ge(s_xst[i % XBUF], 16 * (i // XBUF))
                        sp.wait_ge(s["xf2"], i - XBUF + 1)
                        sp.dma_start(xs[:, i % XBUF, :, :], x_v[i]).then_inc(s_xl[i % XBUF], 16)
                    if 0 <= i - 3 < NB:
                        b = i - 3
                        sp.wait_ge(s["x2"], b + 1)
                        sp.dma_start(out_v[b], xs[:, b % XBUF, :, :]).then_inc(s_xst[b % XBUF], 16)
                    if 0 <= i - 5 < NB:
                        b = i - 5
                        sp.wait_ge(s["smx"], b + 1)
                        sp.dma_start(xf_v[b], xfb[:, b % 2, :, :]).then_inc(s_fst[b % 2], 16)
                for n in range(XBUF):
                    sp.wait_ge(s_xst[n], 16 * len(range(n, NB, XBUF)))
                for n in range(2):
                    sp.wait_ge(s_fst[n], 16 * len(range(n, NB, 2)))

            @block.gpsimd
            def _(pool):
                step = Chain(pool, s["pchain"])
                step(pool.memset(self_[:, :, :], 0.0))
                step(pool.affine_select(out=self_[:, :, :], in_=self_[:, :, :], compare_op=ALU.not_equal, fill=1.0,
                                        base=0, pattern=[[-1, HEADS], [0, P]], channel_multiplier=1))
                step(pool.affine_select(out=self_[:, :, :], in_=self_[:, :, :], compare_op=ALU.not_equal, fill=-1.0,
                                        base=-QD, pattern=[[-1, HEADS], [0, P]], channel_multiplier=1))
                step(pool.tensor_copy(selM[:, :, :], self_[:, :, :]))
                step(pool.memset(self_[:, :, :], 0.0))
                v = self_[:, 0:PAIRS, :].rearrange("k p (a d) -> k p a d", a=2)
                step(pool.affine_select(out=v, in_=v, compare_op=ALU.not_equal, fill=1.0, base=0,
                                        pattern=[[-2, PAIRS], [-1, 2], [0, DH]], channel_multiplier=1))
                step(pool.affine_select(out=v, in_=v, compare_op=ALU.not_equal, fill=1.0, base=-QD,
                                        pattern=[[-2, PAIRS], [-1, 2], [0, DH]], channel_multiplier=1))
                step(pool.tensor_copy(selP[:, :, :], self_[:, 0:PAIRS, :]))
                step(pool.memset(maskneg[:, :], 0.0))
                m = maskneg[:, :].rearrange("p (j s) -> p j s", j=TILES)
                step(pool.affine_select(out=m, in_=m, compare_op=ALU.is_ge, fill=-BIG, base=0,
                                        pattern=[[0, TILES], [1, P]], channel_multiplier=-1))
                for n in range(VBUF):
                    step(pool.memset(vaug[:, n, 0:TILES * ROWW].rearrange("p (j w) -> p j w", w=ROWW)[:, :, E_DIM:ROWW], 1.0))
                step(pool.memset(vaug[:, :, TILES * ROWW:TILES * ROWW + P], 1.0))
                step(pool.memset(kpad[:, :, :, :], 0.0))
                step(pool.memset(S[:, :, :, :], 0.0))
                step(pool.memset(Z[:, :], 0.0))
                step(pool.memset(Zx[:, :], 0.0))
                step(pool.memset(Mhl[:, :].bitcast(FP32), 0.0))
                step(pool.memset(whl[:, :].bitcast(FP32), 0.0))
                pool.memset(gW[:, :, :], 0.0).then_inc(s["prep1"], 1)
                pool.wait_ge(s["prep1"], 1)
                pool.wait_ge(s["ldw"], 7 * 16)
                pool.wait_ge(tg["sem"], tg["ready"])
                step(pool.tensor_scalar(Wo[:, :], Wo[:, :], tg["ap"][:, 0:1], None, ALU.mult))

                def head_means(b):
                    pool.wait_ge(s_cd[b % VBUF], 16 * (b // VBUF + 1))
                    w = DH // 2
                    src = v_all(b).rearrange("p j (h d) -> p j h d", d=DH)
                    for j in range(TILES):
                        ins = pool.tensor_tensor(half[:, j, :, :], src[:, j, :, 0:w], src[:, j, :, w:2 * w], ALU.add)
                    step(ins)
                    part = half[:, :, :, :].rearrange("p j h w -> p (j h) w")
                    while w > 1:
                        w //= 2
                        o_ = part[:, :, 0:w] if w > 1 else msum[:, :].unsqueeze(2)
                        step(pool.tensor_tensor(o_, part[:, :, 0:w], part[:, :, w:2 * w], ALU.add))
                    means = vaug[:, b % VBUF, 0:TILES * ROWW].rearrange("p (j w) -> p j w", w=ROWW)[:, :, E_DIM + 1:ROWW:2]
                    pool.tensor_scalar(means, msum[:, :].rearrange("p (j h) -> p j h", h=HEADS), 1.0 / DH, None, ALU.mult)\
                        .then_inc(s["vaug"], 1)
                    pool.wait_ge(s["vaug"], b + 1)

                def weigh_v(b):
                    pool.wait_ge(s["tmd"], b + 1)
                    if b >= 1:
                        pool.wait_ge(s["tfull"], number["st", b - 1, 2] + 1)
                    for j in range(TILES - 1):
                        pool.tensor_tensor(uv[:, j, :, 0:DH], v_of(b, j, 0, E_DIM).rearrange("p (h d) -> p h d", d=DH),
                                           spread(tm[:, j, 0, :], 2, DH), ALU.mult)
                        ins = pool.tensor_tensor(uv[:, j, :, DH:VW], v_of(b, j, E_DIM, 2 * HEADS).rearrange("p (h d) -> p h d", d=2),
                                                 spread(tm[:, j, 0, :], 2, 2), ALU.mult)
                    ins.then_inc(s["uv"], 1)
                    pool.wait_ge(s["uv"], b + 1)

                def centre(b):
                    pool.wait_ge(s["an"], TILES * (b + 1))
                    n = nsb[:, :, :, :].rearrange("p j h w -> p (j h) w")
                    pool.tensor_tensor(n[:, :, 0:DH], n[:, :, 0:DH], n[:, :, DH + 1:DH + 2].to_broadcast([P, TILES * HEADS, DH]),
                                       ALU.subtract).then_inc(s["cen"], 1)
                    pool.wait_ge(s["cen"], b + 1)

                def weigh_out(b):
                    pool.wait_ge(s["rh"], b + 1)
                    n = nsb[:, :, :, :]
                    rows = n.rearrange("p j h w -> p (j h) w")[:, :, 0:DH]
                    step(pool.tensor_tensor(rows, rows, spread(rh[:, :], 2, DH), ALU.mult))
                    for j in range(TILES):
                        ins = pool.tensor_tensor(n[:, j, :, 0:DH], n[:, j, :, 0:DH],
                                                 Wo[:, :].rearrange("p (h d) -> p h d", d=DH), ALU.mult)
                    step(ins)
                    xb = xs[:, b % XBUF, :, :].rearrange("p j (h d) -> p (j h) d", d=DH)
                    pool.tensor_tensor(xb, xb, rows, ALU.add).then_inc(s["x2"], 1)
                    pool.wait_ge(s["x2"], b + 1)

                for i in range(NB + 5):
                    if 0 <= i - 2 < NB:
                        weigh_v(i - 2)
                    if i < NB:
                        head_means(i)
                    if 0 <= i - 3 < NB:
                        weigh_out(i - 3)
                    if 0 <= i - 2 < NB:
                        centre(i - 2)

            @block.scalar
            def _(act):
                step = Chain(act, s["achain"])

                def rsqrt_guess(src, tmp, dst, ready, by, log, done):
                    act.wait_ge(ready, by)
                    act.activation(tmp, src, ACT.Ln).then_inc(log, 1)
                    act.wait_ge(log, by)
                    act.activation(dst, tmp, ACT.Exp, scale=-0.5).then_inc(done, 1)

                act.preload_act_table_set("natural_log_exp_and_others")
                for i in range(NB + 5):
                    if 0 <= i - 5 < NB:
                        act.wait_ge(*freed[number["lt", i - 5, 0]])
                        act.activation(ex[:, :, :], lt[:, :, :], ACT.Exp).then_inc(s["lex"], 1)
                    if 0 <= i - 1 < NB:
                        b = i - 1
                        if b >= 2:
                            act.wait_ge(s["qk"], HEADS * (b - 1))
                            act.wait_ge(*freed[number["qw", b - 2, PAIRS - 1]])
                        for c in range(CH):
                            t = filled(act, "q", b, c)
                            act.activation(qT[:, b % 2, c, :], t[:, :], ACT.Copy).then_inc(s["ta"], 1)
                    if 0 <= i - 4 < NB:
                        rsqrt_guess(vb[:, :], lb[:, :], rb[:, :], s["v2"], i - 3, s["lnb"], s["r2"])
                    for c in range(TILES):
                        if 0 <= i - 1 < NB:
                            t = filled(act, "k", i - 1, c)
                            act.activation(kT[:, c, :], t[:, :], ACT.Copy).then_inc(s["ta"], 1)
                        if 0 <= i - 3 < NB:
                            if c == 0:
                                act.wait_ge(s["cen"], i - 2)
                            act.activation(C[:, c, :].rearrange("p (h d) -> p h d", d=DH), nsb[:, c, :, 0:DH], ACT.Square)\
                               .then_inc(s["sq"], 1)
                    if 0 <= i - 3 < NB:
                        rsqrt_guess(vh[:, :], lh[:, :], rh[:, :], s["lnh"], i - 2, s["ex1"], s["gg"])

                    def log_sigmoid(k):
                        if 0 <= i - 1 < NB:
                            if k == 0:
                                act.wait_ge(s["vg"], i)
                                step(act.activation(ee[:, :], ee[:, :], ACT.Abs))
                            elif k == 1:
                                step(act.activation(ee[:, :], ee[:, :], ACT.Exp, scale=-1.0))
                            else:
                                act.activation(ee[:, :], ee[:, :], ACT.Ln, bias=1.0).then_inc(s["gx"], 1)

                    for h in range(HEADS):
                        if 0 <= i - 2 < NB:
                            b = i - 2
                            act.wait_ge(s["ee"], HEADS * b + h + 1)
                            if HEADS * b + h >= 2:
                                act.wait_ge(s["cc"], HEADS * b + h - 1)
                            if h == 0:
                                act.wait_ge(s["tmd"], b + 1)
                            for j in range(TILES):
                                ins = act.activation(D[:, h % 2, j * P:(j + 1) * P], EX[h % 2][:, j * P:(j + 1) * P], ACT.Exp,
                                                     bias=tm[:, j, 3, h:h + 1])
                            ins.then_inc(s["dd"], 1)
                        if 2 <= h < 5:
                            log_sigmoid(h - 2)

                    def numerators(j):
                        if 0 <= i - 2 < NB:
                            b = i - 2
                            act.wait_ge(s["af"], TILES * b + j + 1)
                            if j == 0 and b >= 1:
                                act.wait_ge(s["x2"], b)
                            act.activation(nsb[:, j, :, :], A[j % 2][:, :, 0:VW], ACT.Copy).then_inc(s["an"], 1)

                    def turned_rows(c):
                        if 0 <= i - 4 < NB:
                            t = filled(act, "xfT", i - 4, c)
                            act.activation(xfT[:, c, :], t[:, :], ACT.Copy).then_inc(s["ta"], 1)

                    def pad_keys(par):
                        if 0 <= i - 1 < NB:
                            b = i - 1
                            if b >= 1:
                                act.wait_ge(s["qk"], HEADS * b)
                            act.wait_ge(*freed[number["k", b, CH - 1]])
                            r = slice(DH * par, DH * par + DH)
                            act.activation(kpad[r, par, :, :], kT[r, :, :], ACT.Copy, scale=DH ** -0.5).then_inc(s["kpad"], 1)

                    turned_rows(0)
                    turned_rows(1)
                    if 0 <= i - 1 < NB:
                        b = i - 1
                        act.wait_ge(s["zz"], b + 1)
                        if b >= 1:
                            act.wait_ge(s["tmf"], b)
                        act.activation(Zx[0:72, :], Z[0:72, :], ACT.Exp).then_inc(s["zx"], 1)
                        act.activation(gd[:, :], gd[:, :], ACT.Exp).then_inc(s["zx"], 1)
                    numerators(0)
                    pad_keys(0)
                    numerators(1)
                    turned_rows(2)
                    turned_rows(3)
                    numerators(2)
                    if i < NB:
                        rsqrt_guess(va[:, :], la[:, :], ra[:, :], s["v1"], i + 1, s["ln1"], s["r1"])
                    pad_keys(1)
                    if 0 <= i - 4 < NB:
                        t = filled(act, "lg", i - 4, 0)
                        act.activation(lg[:, :], t[0:NEXP, :], ACT.Identity, bias=br[:, :]).then_inc(s["ta"], 1)
                    numerators(3)

            @block.tensor
            def _(pe):
                pe.wait_ge(s["ldw"], 7 * 16)
                pe.wait_ge(consts["sem"], consts["ready"])
                for c in range(3 * CH):
                    mm = pe.transpose(G[:, 16 * c:16 * c + 16], gwr[:, c * P:(c + 1) * P], ident[0:16, 0:16])
                mm.then_inc(s["prep2"], 1)
                pe.wait_ge(s["prep3"], 1)

                def scores(b, h):
                    n = HEADS * b + h
                    if n >= 2:
                        pe.wait_ge(s["cc"], n - 1)
                    for j in range(TILES):
                        jj = slice(j * P, (j + 1) * P)
                        mm = pe.matmul(QK[h % 2][:, jj], kpad[:, h % 2, h // 2, jj], qT[:, b % 2, h // 2, jj], start=True, stop=True)
                    mm.then_inc(s["qk"], 1)

                for i in range(NB + 5):
                    if 0 <= i - 2 < NB:
                        b = i - 2
                        if b >= 1:
                            pe.wait_ge(s["dd"], HEADS * b - 1)
                        pe.wait_ge(s["zx"], 2 * b + 2)
                        pe.wait_ge(s["ms"], b + 1)
                        for j in range(TILES):
                            pe.transpose(EB[:, j * P:j * P + 104], Zx[:, j * P:(j + 1) * P], ident[0:104, 0:104])
                        pe.matmul(EB[:, GCOL:GCOL + 16], ones[0:8, :], gdiag[:, :, :].rearrange("k j h -> k (j h)"), start=True, stop=True)\
                          .then_inc(s["tmf"], 1)
                    if 0 <= i - 1 < NB:
                        b = i - 1
                        pe.wait_ge(s["q"], b + 1)
                        pe.wait_ge(s["vaug"], b + 1)
                        if b >= 1:
                            pe.wait_ge(s["gput"], b)
                        if b >= 2:
                            pe.wait_ge(s["dd"], HEADS * (b - 1))
                        for c in range(2 * CH + AHEAD):
                            if c < 2 * CH:
                                kind, k = ("q", c) if c < CH else ("k", c - CH)
                                t = fill(pe, kind, b, k)
                                for j in range(TILES):
                                    src = q[:, j, k * P:(k + 1) * P] if kind == "q" else v_of(b, j, k * P, P)
                                    mm = pe.transpose(t[:, j * P:(j + 1) * P], src, ident[:, :])
                                mm.then_inc(s["tfull"], 1)
                            g = c - AHEAD
                            if g >= 0:
                                pe.wait_ge(*freed[number[("q", b, g) if g < CH else ("k", b, g - CH)]])
                                src = qT[:, b % 2, g, :] if g < CH else kT[:, g - CH, :]
                                mm = pe.matmul(G[0:40, :], gW[:, g, :], src, start=(g == 0), stop=(g == 2 * CH - 1))
                        mm.then_inc(s["gates"], 1)
                    if 0 <= i - 2 < NB:
                        b = i - 2
                        pe.wait_ge(s["kpad"], 2 * b + 2)
                        if b >= 1:
                            pe.wait_ge(s["an"], TILES * b)
                        for h in range(HEADS):
                            n = HEADS * b + h
                            if n >= 2:
                                pe.wait_ge(s["dd"], n - 1)
                            if h == 0:
                                pe.wait_ge(s["tmd"], b + 1)
                            if h == 1:
                                scores(b, h)
                                pe.wait_ge(s["gput"], min(i, NB))
                            pe.matmul(EX[h % 2][:, :], identb[:, :], maskneg[:, :], start=True, stop=False)
                            pe.matmul(EX[h % 2][:, :], selM[:, h, :], Mhl[:, :], start=False, stop=True).then_inc(s["ee"], 1)
                            if h != 1:
                                scores(b, h)
                            if h in (0, 2, 4):
                                j = h // 2
                                t = fill(pe, "st", b, j)
                                if h == 0:
                                    pe.wait_ge(s["uv"], b + 1)
                                for g in range(HEADS):
                                    r = DH * (g % 2)
                                    mm = pe.matmul(t[r:r + DH, (g // 2) * VW:(g // 2 + 1) * VW], v_of(b, j, g * DH, DH),
                                                   uv[:, j, g, :], start=True, stop=True)
                                mm.then_inc(s["tfull"], 1)
                            elif h != HEADS - 1:
                                p = {1: 0, 3: 1, 5: 2, 6: 3}[h]
                                t = fill(pe, "qw", b, p)
                                pe.matmul(t[:, 0:SEQ - P], selP[:, p, :], whl[:, :], start=True, stop=True).then_inc(s["tfull"], 1)

                    def product(j):
                        if not 0 <= i - 2 < NB:
                            return
                        b = i - 2
                        n = TILES * b + j
                        if j == 0:
                            pe.wait_ge(s["cc"], HEADS * (b + 1))
                        if j == 1:
                            pe.wait_ge(*freed[number["qw", b, 3]])
                        if n >= 2:
                            pe.wait_ge(s["an"], n - 1)
                        for h in range(HEADS):
                            mm = pe.matmul(A[j % 2][:, h, :].rearrange("p (a w) -> p a w", a=2), C[:, h, j * P:(j + 1) * P], v_wide(b, j, h),
                                           start=(h % 4 == 0), stop=(j == 0), skip_group_check=True)
                        if j:
                            for p in range(PAIRS):
                                mm = pe.matmul(A[j % 2][:, 2 * p:2 * p + 2, 0:VW], qw[:, p, (j - 1) * P:j * P],
                                               S[:, j - 1, p, :].rearrange("k (a w) -> k a w", a=2),
                                               start=False, stop=True, skip_group_check=True)
                        mm.then_inc(s["af"], 1)

                    def turn_rows(c):
                        if not 0 <= i - 4 < NB:
                            return
                        b = i - 4
                        if c == 0:
                            pe.wait_ge(s["xf2"], b + 1)
                        t = fill(pe, "xfT", b, c)
                        for j in range(TILES):
                            mm = pe.transpose(t[:, j * P:(j + 1) * P], xfb[:, b % 2, j, c * P:(c + 1) * P], ident[:, :])
                        mm.then_inc(s["tfull"], 1)

                    turn_rows(0)
                    turn_rows(1)
                    product(0)
                    product(1)
                    turn_rows(2)
                    turn_rows(3)
                    product(2)
                    if 0 <= i - 4 < NB:
                        b = i - 4
                        t = fill(pe, "lg", b, 0)
                        pe.wait_ge(*freed[number["xfT", b, CH - 1]])
                        for c in range(CH):
                            mm = pe.matmul(t[0:NEXP, :], Wr[:, c, :], xfT[:, c, :], start=(c == 0), stop=(c == CH - 1))
                        mm.then_inc(s["tfull"], 1)
                    product(3)
                    if 0 <= i - 4 < NB:
                        t = fill(pe, "lt", b, 0)
                        pe.wait_ge(*freed[number["lg", b, 0]])
                        for j in range(TILES):
                            mm = pe.transpose(t[:, j * NEXP:(j + 1) * NEXP], lg[:, j * P:(j + 1) * P], ident[0:NEXP, 0:NEXP])
                        mm.then_inc(s["tfull"], 1)

            @block.vector
            def _(dve):
                step = Chain(dve, s["dchain"])
                dve.wait_ge(s["prep1"], 1)
                dve.wait_ge(s["prep2"], 1)
                g3 = G[:, 0:48 * CH].rearrange("p (c g) -> p c g", g=16)
                step(dve.tensor_copy(gW[:, :, 0:8], g3[:, 0:2 * CH, 0:8]))
                step(dve.tensor_copy(gW[:, :, 32:40], g3[:, 0:2 * CH, 8:16]))
                step(dve.tensor_tensor(gW[:, CH:2 * CH, 0:8], gW[:, CH:2 * CH, 0:8], g3[:, 2 * CH:3 * CH, 0:8], ALU.add))
                dve.tensor_tensor(gW[:, CH:2 * CH, 32:40], gW[:, CH:2 * CH, 32:40], g3[:, 2 * CH:3 * CH, 8:16], ALU.add)\
                    .then_inc(s["prep3"], 1)

                def statistics(src, st_, mv_, v_):
                    for j in range(TILES):
                        ins = dve.bn_stats(st_[:, j, :], src[:, j, :])
                    step(ins)
                    for j in range(TILES):
                        ins = dve.bn_aggr(mv_[:, j, :], st_[:, j, :])
                    step(ins)
                    return dve.tensor_scalar(v_, mv_[:, :, 1], LN_EPS, None, ALU.add)

                for i in range(NB + 5):
                    if 0 <= i - 5 < NB:
                        b = i - 5
                        t = filled(dve, "lt", b, 0)
                        l3 = t[:, 0:TILES * NEXP].rearrange("p (j n) -> p j n", n=NEXP)
                        step(dve.tensor_reduce(mx[:, :], l3, AX.X, ALU.max))
                        dve.tensor_tensor(lt[:, :, :], l3, spread(mx[:, :], 2, NEXP), ALU.subtract).then_inc(s["td"], 1)
                    if 0 <= i - 2 < NB:
                        b = i - 2
                        dve.wait_ge(s["tmf"], b + 1)
                        t4 = EB[:, :].rearrange("p (j k h) -> p j k h", k=4, h=QD)
                        dve.tensor_copy(nrm[:, b % 2, :].rearrange("p (j h) -> p j h", h=HEADS), t4[:, :, 2, 0:HEADS])
                        dve.tensor_copy(gb[:, :, :].rearrange("p j h -> p (j h)"), EB[:, GCOL:GCOL + 16])
                        dve.tensor_copy(tm[:, :, :, :], t4[:, :, :, 0:HEADS]).then_inc(s["tmd"], 1)
                        dve.wait_ge(s["tmd"], b + 1)
                    if 0 <= i - 4 < NB:
                        b = i - 4
                        dve.wait_ge(s["x2"], b + 1)
                        xb = xs[:, b % XBUF, :, :]
                        statistics(xb, st2, mv2, vb[:, :]).then_inc(s["v2"], 1)
                    if 0 <= i - 3 < NB:
                        b = i - 3
                        n = nsb[:, :, :, :].rearrange("p j h w -> p (j h) w")
                        dve.wait_ge(s["an"], TILES * (b + 1))
                        step(dve.scalar_tensor_tensor(out=rn[:, :].unsqueeze(2), in0=n[:, :, DH:DH + 1], scalar=-1.0,
                                                      in1=n[:, :, DH:DH + 1], op0=ALU.mult, op1=ALU.max))
                        step(dve.tensor_tensor(rn[:, :], rn[:, :], nrm[:, b % 2, :], ALU.max))
                        step(dve.tensor_scalar(rn[:, :], rn[:, :], NORM_EPS, None, ALU.add))
                        step(dve.reciprocal(rn[:, :], rn[:, :]))
                        step(dve.tensor_tensor(th[:, :], rn[:, :], rn[:, :], ALU.mult))
                    if 0 <= i - 4 < NB:
                        b = i - 4
                        if b >= 2:
                            dve.wait_ge(s_fst[b % 2], 16 * (b // 2))
                        dve.wait_ge(s["r2"], b + 1)
                        newton_rsqrt(step, dve, rb[:, :], vb[:, :], tb[:, :])
                        for j in range(TILES):
                            ins = dve.tensor_scalar(xfb[:, b % 2, j, 0:E_DIM], xb[:, j, :], mv2[:, j, 0:1], rb[:, j:j + 1], ALU.subtract, ALU.mult)
                        ins.then_inc(s["xf2"], 1)
                    if 0 <= i - 3 < NB:
                        b = i - 3
                        for j in range(TILES):
                            dve.wait_ge(s["sq"], TILES * b + j + 1)
                            ins = dve.tensor_reduce(ssq[:, j * HEADS:(j + 1) * HEADS], C[:, j, :].rearrange("p (h d) -> p h d", d=DH), AX.X, ALU.add)
                        step(ins)
                        step(dve.scalar_tensor_tensor(out=th[:, :], in0=ssq[:, :], scalar=1.0 / DH, in1=th[:, :], op0=ALU.mult, op1=ALU.mult))
                        dve.tensor_scalar(vh[:, :], th[:, :], LN_EPS, None, ALU.add).then_inc(s["lnh"], 1)
                    if 0 <= i - 1 < NB:
                        b = i - 1
                        dve.wait_ge(s["gates"], b + 1)
                        fb = gbias[32:40, 0:1]
                        dve.tensor_scalar(ee[:, :], G[32:40, :], fb, None, ALU.add).then_inc(s["vg"], 1)
                        dve.tensor_scalar(MM[:, :], G[32:40, :], fb, 0.0, ALU.add, ALU.min)
                        dve.tensor_scalar(aa[:, :], G[0:8, :], gbias[0:8, 0:1], None, ALU.add).then_inc(s["gput"], 1)
                        dve.wait_ge(s["gput"], b + 1)
                    if 0 <= i - 3 < NB:
                        b = i - 3
                        dve.wait_ge(s["gg"], b + 1)
                        newton_rsqrt(step, dve, rh[:, :], vh[:, :], th[:, :])
                        dve.tensor_tensor(rh[:, :], rh[:, :], rn[:, :], ALU.mult).then_inc(s["rh"], 1)
                    if 0 <= i - 2 < NB:
                        b = i - 2
                        for h in range(HEADS):
                            n = HEADS * b + h
                            dve.wait_ge(s["dd"], n + 1)
                            dve.wait_ge(s["qk"], n + 1)
                            dve.tensor_tensor(C[:, h, :], QK[h % 2], D[:, h % 2, :], ALU.mult).then_inc(s["cc"], 1)
                            if h in (0, 2, 4):
                                j = h // 2
                                t = filled(dve, "st", b, j)
                                fresh = t[:, 0:PAIRS * VW].rearrange("k (p w) -> k p w", w=VW)
                                for par in range(2):
                                    r, w = slice(DH * par, DH * par + DH), slice(VW * par, VW * par + VW)
                                    if j == 0:
                                        ins = dve.tensor_copy(S[r, 0, :, w], fresh[r])
                                    else:
                                        gate = spread(gb[r, j - 1, par:HEADS:2], 2, VW)
                                        ins = dve.tensor_tensor(S[r, j, :, w], S[r, j - 1, :, w], gate, ALU.mult)
                                if j:
                                    step(ins)
                                    for par in range(2):
                                        r, w = slice(DH * par, DH * par + DH), slice(VW * par, VW * par + VW)
                                        ins = dve.tensor_tensor(S[r, j, :, w], S[r, j, :, w], fresh[r], ALU.add)
                                ins.then_inc(s["td"], 1)
                                dve.wait_ge(*freed[number["st", b, j]])
                            elif h != HEADS - 1:
                                p = {1: 0, 3: 1, 5: 2, 6: 3}[h]
                                t = filled(dve, "qw", b, p)
                                dve.scalar_tensor_tensor(out=qw[:, p, :], in0=qT[:, b % 2, p, P:SEQ], scalar=DH ** -0.5,
                                                         in1=t[:, 0:SEQ - P], op0=ALU.mult, op1=ALU.mult).then_inc(s["td"], 1)
                    if 0 <= i - 1 < NB:
                        b = i - 1
                        dve.wait_ge(s["gx"], b + 1)
                        step(dve.tensor_tensor_scan(cs[:, :], MM[:, :], ee[:, :], 0.0, ALU.add, ALU.subtract))
                        step(dve.tensor_tensor(aa[:, :], aa[:, :], cs[:, :], ALU.subtract))
                        step(dve.tensor_tensor_scan(MM[:, :], aa[:, :], aa[:, :], -3.0e38, ALU.max, ALU.max))
                        M3 = MM[:, :].rearrange("h (j s) -> h j s", j=TILES)
                        a3 = aa[:, :].rearrange("h (j s) -> h j s", j=TILES)
                        end = M3[:, :, P - 1:P]
                        dve.tensor_tensor(Z[0:8, :].rearrange("h (j s) -> h j s", j=TILES), a3, end.to_broadcast([8, TILES, P]), ALU.subtract)
                        dve.tensor_tensor(Z[32:40, P:SEQ].rearrange("h (j s) -> h j s", s=P), end[:, 0:3, :].to_broadcast([8, 3, P]), M3[:, 1:4, :], ALU.subtract)
                        dve.tensor_tensor(gd[:, :].unsqueeze(2), end[:, 0:2, :], end[:, 1:3, :], ALU.subtract)
                        dve.scalar_tensor_tensor(out=Z[64:72, :], in0=cs[:, :], scalar=-1.0, in1=MM[:, :], op0=ALU.mult, op1=ALU.subtract)\
                            .then_inc(s["zz"], 1)
                        dve.tensor_copy(Zx[96:104, :], aa[:, :])
                        step(dve.tensor_scalar(Mhl[0:8, :], MM[:, :], -1.0, None, ALU.mult))
                        dve.tensor_tensor(Mhl[32:40, :], MM[:, :], Mhl[0:8, :].bitcast(FP32), ALU.add)
                        dve.wait_ge(s["zx"], 2 * b + 2)
                        step(dve.tensor_copy(whl[32:40, :], Zx[32:40, P:SEQ]))
                        dve.tensor_tensor(whl[0:8, :], Zx[32:40, P:SEQ], whl[32:40, :].bitcast(FP32), ALU.subtract)
                        dve.tensor_tensor(gdiag[:, :, :], spread(gd[:, :], 2, 8), spread(ident[0:8, 0:8], 1, 2), ALU.mult).then_inc(s["ms"], 1)
                    if 0 <= i - 5 < NB:
                        b = i - 5
                        dve.wait_ge(s["lex"], b + 1)
                        step(dve.tensor_reduce(sx[:, :], ex[:, :, :], AX.X, ALU.add))
                        step(dve.reciprocal(sx[:, :], sx[:, :]))
                        step(dve.tensor_tensor(sm_all[:, b * TILES:(b + 1) * TILES, :], ex[:, :, :], spread(sx[:, :], 2, NEXP), ALU.mult))
                        dve.tensor_copy(xfb[:, b % 2, :, E_DIM:XW], sm_all[:, b * TILES:(b + 1) * TILES, :]).then_inc(s["smx"], 1)
                    if i < NB:
                        dve.wait_ge(s_xl[i % XBUF], 16 * (i // XBUF + 1))
                        statistics(xs[:, i % XBUF, :, :], st, mv, va[:, :]).then_inc(s["v1"], 1)
                        dve.wait_ge(s["r1"], i + 1)
                        newton_rsqrt(step, dve, ra[:, :], va[:, :], ta[:, :])
                        if i >= 1:
                            dve.wait_ge(s["tfull"], number["q", i - 1, CH - 1] + 1)
                        if i >= 4:
                            dve.wait_ge(s["tfull"], number["lg", i - 4, 0] + 1)
                        for j in range(TILES):
                            ins = dve.tensor_scalar(q[:, j, :], xs[:, i % XBUF, j, :], mv[:, j, 0:1], ra[:, j:j + 1], ALU.subtract, ALU.mult)
                        ins.then_inc(s["q"], 1)


def weight_pieces():
    pieces = []
    for e in range(NEXP):
        if e % 2 == 0:
            pieces += [("up", e, c, c + 1) for c in range(CH)]
        pieces += [("down", e, c, min(c + 2, FCH)) for c in range(0, FCH, 2)]
    return pieces


class Weights:

    def __init__(self, nc, io, ctx):
        def sb(name, shape, dt):
            return ctx.enter_context(nc.sbuf_tensor(name, shape, dt))

        self.io = io
        self.up = [sb("up_hi", [P, CH, FDIM], FP32R), sb("up_lo", [P, CH, FDIM], FP32R)]
        self.down = [sb("down_hi", [P, FCH, E_DIM], FP32R), sb("down_lo", [P, FCH, E_DIM], FP32R)]
        self.raw = sb("w_raw", [P, 2, FDIM + 1], FP32)
        self.loaded = [ctx.enter_context(nc.semaphore(f"w_loaded{n}")) for n in range(2)]
        self.hi_done = ctx.enter_context(nc.semaphore("w_hi_done"))
        self.lo_done = ctx.enter_context(nc.semaphore("w_lo_done"))
        self.pieces = weight_pieces()

    def parts(self, m):
        kind, e, a, b = self.pieces[m]
        raw = self.raw[:, m % 2, :]
        if kind == "up":
            src = self.io["Wup"][e // 2].rearrange("(c p) f -> p c f", p=P)[:, a, :]
            return [(src, raw[:, 0:FDIM], self.up[0][:, a, :], self.up[1][:, a, :])]
        if b < FCH:
            src = self.io["Wdown"][e, a * P:b * P, :].rearrange("(c p) n -> p c n", p=P)
            return [(src, raw[:, 0:(b - a) * E_DIM].rearrange("p (c n) -> p c n", n=E_DIM),
                     self.down[0][:, a:b, :], self.down[1][:, a:b, :])]
        out = []
        for c in range(a, b):
            rows = P if c < FCH - 1 else FLAST
            out.append((self.io["Wdown"][e, c * P:c * P + rows, :], raw[0:rows, (c - a) * E_DIM:(c - a + 1) * E_DIM],
                        self.down[0][0:rows, c, :], self.down[1][0:rows, c, :]))
        return out

    def due(self, m):
        return self.loaded[m % 2], sum(16 * len(self.parts(n)) for n in range(m % 2, m + 1, 2))

    def load(self, eng, m):
        if m >= 2:
            eng.wait_ge(self.lo_done, m - 1)
        for src, raw, _, _ in self.parts(m):
            eng.dma_start(raw, src).then_inc(self.loaded[m % 2], 16)

    def hi(self, act, m):
        act.wait_ge(*self.due(m))
        for _, raw, hi, _ in self.parts(m):
            ins = act.activation(hi, raw, ACT.Copy)
        ins.then_inc(self.hi_done, 1)

    def lo(self, eng, m):
        eng.wait_ge(self.hi_done, m + 1)
        for _, raw, hi, lo in self.parts(m):
            ins = eng.tensor_tensor(lo, raw, hi.bitcast(FP32), ALU.subtract)
        ins.then_inc(self.lo_done, 1)

    def upto(self, kind, e):
        return max(m for m, p in enumerate(self.pieces) if p[0] == kind and p[1] <= e) + 1


def choose(nc, dram, sm_all, slots, weights, consts, NTOK, K):
    GROUP = P // NEXP
    SPAN = NTOK // GROUP
    NT = NTOK // P
    STEPS = (SPAN - 1).bit_length()
    VALID = 1 << STEPS
    TOP_BIT = 29
    I16, FP16 = mybir.dt.int16, mybir.dt.float16
    KC = K // P
    ident = consts["ident"]
    with ExitStack() as ctx:
        def sb(name, shape, dt=FP32):
            return ctx.enter_context(nc.sbuf_tensor(name, shape, dt))

        def sem(name):
            return ctx.enter_context(nc.semaphore("c_" + name))

        turned = sb("turned", [NT, NEXP, P])
        V = sb("V", [P, SPAN])
        hit = sb("hit", [P, SPAN], FP16)
        over = sb("over", [P, SPAN]); same = sb("same", [P, SPAN]); rank = sb("rank", [P, SPAN])
        place = sb("place", [P, SPAN])
        ent = [sb("ent0", [P, SPAN], I16), sb("ent1", [P, SPAN], I16)]
        moving = sb("moving", [P, SPAN], I16); moved = sb("moved", [P, SPAN], I16)
        ids = sb("ids", [P, SPAN], I32)
        count = sb("count", [P, 1], FP16); low = sb("low", [P, 1], I32); cand = sb("cand", [P, 1], I32); bit = sb("bit", [P, 1], I32)
        same_groups = sb("same_groups", [P, P], FP16)
        groups32 = sb("groups32", [P, P]); before = sb("before", [P, P])
        tot = sb("tot", [P, 1]); need = sb("need", [P, 1]); offs = sb("offs", [P, 1]); nq = sb("nq", [P, 1]); wide = sb("wide", [P, P])
        base = sb("base", [P, P]); jump = sb("jump", [P, P])
        slot = sb("slot", [P, KC]); home = sb("home", [P, NEXP, KC])
        cmp_ = sb("cmp_", [P, NEXP, KC, GROUP - 1]); addr = sb("addr", [P, NEXP, KC])
        pst = ctx.enter_context(nc.psum_tensor("c_pst", [NT, NEXP, P], FP32))
        pc = ctx.enter_context(nc.psum_tensor("c_pc", [P, 512], FP32))
        s = {n: sem(n) for n in "turn out saved V pool cnt sum dve tie mm wide bases list done".split()}
        with nc.Block() as block:
            @block.sync
            def _(sp):
                for m in range(2):
                    weights.load(sp, m)
                sp.wait_ge(s["out"], 1)
                sp.dma_start(dram["gates"].rearrange("e (t p) -> t e p", p=P), turned[:, :, :]).then_inc(s["saved"], 16)
                sp.wait_ge(s["saved"], 16)
                sp.dma_start(V[:, :], dram["gates"].rearrange("e (q n) -> (e q) n", q=GROUP)).then_inc(s["V"], 16)
                for m in range(2, weights.upto("down", 0)):
                    weights.load(sp, m)
                sp.wait_ge(s["done"], 1)
                sp.dma_start(dram["list"].rearrange("(g n) o -> g (n o)", g=P), ids[:, :]).then_inc(s["list"], 16)
                sp.wait_ge(s["list"], 16)

            @block.scalar
            def _(act):
                for m in range(weights.upto("down", 0)):
                    weights.hi(act, m)

            @block.gpsimd
            def _(pool):
                step = Chain(pool, s["pool"])
                g3 = groups32[:, :].rearrange("k (a b) -> k a b", b=GROUP)
                step(pool.memset(groups32[:, :], 1.0))
                step(pool.affine_select(out=g3, in_=g3, compare_op=ALU.is_ge, fill=0.0, base=0,
                                        pattern=[[-GROUP, NEXP], [0, GROUP]], channel_multiplier=1))
                step(pool.affine_select(out=g3, in_=g3, compare_op=ALU.is_ge, fill=0.0, base=GROUP - 1,
                                        pattern=[[GROUP, NEXP], [0, GROUP]], channel_multiplier=-1))
                step(pool.affine_select(out=before[:, :], in_=groups32[:, :], compare_op=ALU.is_gt, fill=0.0, base=0,
                                        pattern=[[1, P]], channel_multiplier=-1))
                step(pool.tensor_copy(same_groups[:, :], groups32[:, :]))
                step(pool.iota(place[:, :], pattern=[[1, SPAN]], base=0, channel_multiplier=0, allow_small_or_imprecise_dtypes=True))
                step(pool.iota(slot[:, :], pattern=[[P, KC]], base=0, channel_multiplier=1, allow_small_or_imprecise_dtypes=True))
                step(pool.iota(home[:, :, :], pattern=[[NTOK, NEXP], [P, KC]], base=0, channel_multiplier=1, allow_small_or_imprecise_dtypes=True))
                for m in range(weights.upto("down", 0)):
                    weights.lo(pool, m)

            @block.tensor
            def _(pe):
                for e in range(NEXP):
                    mm = pe.transpose(pst[:, e, :], sm_all[:, :, e], ident[:, :])
                mm.then_inc(s["turn"], 1)
                pe.wait_ge(s["pool"], 5)
                for n in range(TOP_BIT + 1):
                    pe.wait_ge(s["cnt"], n + 1)
                    pe.matmul(pc[:, 0:1], same_groups[:, :], count[:, :], start=True, stop=True).then_inc(s["sum"], 1)
                pe.wait_ge(s["tie"], 1)
                pe.matmul(pc[:, 0:1], groups32[:, :], tot[:, :], start=True, stop=True).then_inc(s["mm"], 1)
                pe.wait_ge(s["tie"], 2)
                pe.matmul(pc[:, 0:1], before[:, :], offs[:, :], start=True, stop=True).then_inc(s["mm"], 1)
                pe.wait_ge(s["wide"], 1)
                pe.matmul(pc[:, 0:P], wide[:, :], before[:, :], start=True, stop=True)
                pe.matmul(pc[:, P:2 * P], wide[:, :], ident[:, :], start=True, stop=True).then_inc(s["bases"], 1)

            @block.vector
            def _(dve):
                step = Chain(dve, s["dve"])
                dve.wait_ge(s["turn"], 1)
                dve.tensor_copy(turned[:, :, :], pst[:, :, :]).then_inc(s["out"], 1)
                step(dve.memset(low[:, :], 0))
                dve.wait_ge(s["V"], 16)
                for n, k in enumerate(range(TOP_BIT, -1, -1)):
                    step(dve.tensor_scalar(cand[:, :], low[:, :], 1 << k, None, ALU.bitwise_or))
                    dve.tensor_scalar(hit[:, :], V[:, :], cand[:, :].bitcast(FP32), 0.0, ALU.is_ge, ALU.add, accum_out=count[:, :])\
                        .then_inc(s["cnt"], 1)
                    dve.wait_ge(s["sum"], n + 1)
                    step(dve.tensor_scalar(bit[:, :], pc[:, 0:1], float(K), float(1 << k), ALU.is_ge, ALU.mult))
                    step(dve.tensor_tensor(low[:, :], low[:, :], bit[:, :], ALU.bitwise_or))
                least = low[:, :].bitcast(FP32)
                dve.wait_ge(s["pool"], 8)
                dve.tensor_scalar(over[:, :], V[:, :], least, 0.0, ALU.is_gt, ALU.add, accum_out=tot[:, :]).then_inc(s["tie"], 1)
                dve.tensor_scalar(same[:, :], V[:, :], least, 0.0, ALU.is_equal, ALU.add, accum_out=offs[:, :])
                dve.wait_ge(s["mm"], 1)
                step(dve.tensor_scalar(need[:, :], pc[:, 0:1], -1.0, float(K), ALU.mult, ALU.add))
                dve.tensor_tensor_scan(rank[:, :], same[:, :], same[:, :], 0.0, ALU.add, ALU.bypass).then_inc(s["tie"], 1)
                dve.wait_ge(s["mm"], 2)
                step(dve.tensor_tensor(need[:, :], need[:, :], pc[:, 0:1], ALU.subtract))
                step(dve.scalar_tensor_tensor(out=same[:, :], in0=rank[:, :], scalar=need[:, :], in1=same[:, :], op0=ALU.is_le, op1=ALU.mult))
                step(dve.tensor_tensor(over[:, :], over[:, :], same[:, :], ALU.add))
                step(dve.tensor_tensor_scan(rank[:, :], over[:, :], over[:, :], 0.0, ALU.add, ALU.bypass))
                step(dve.tensor_copy(nq[:, :], rank[:, SPAN - 1:SPAN]))
                dve.tensor_scalar(wide[:, :], groups32[:, :], 0.0, nq[:, :], ALU.mult, ALU.add).then_inc(s["wide"], 1)
                step(dve.tensor_tensor(rank[:, :], place[:, :], rank[:, :], ALU.subtract))
                step(dve.scalar_tensor_tensor(out=ent[0][:, :], in0=rank[:, :], scalar=float(VALID + 1), in1=over[:, :], op0=ALU.add, op1=ALU.mult))
                for k in range(STEPS):
                    old, new = ent[k % 2], ent[1 - k % 2]
                    d = 1 << k
                    step(dve.tensor_scalar(moving[:, :], old[:, :], d, None, ALU.bitwise_and))
                    step(dve.scalar_tensor_tensor(out=new[:, :], in0=moving[:, :], scalar=0.0, in1=old[:, :], op0=ALU.is_equal, op1=ALU.mult))
                    step(dve.tensor_tensor(moved[:, :], old[:, :], new[:, :], ALU.subtract))
                    step(dve.tensor_tensor(new[:, 0:SPAN - d], new[:, 0:SPAN - d], moved[:, d:SPAN], ALU.add))
                step(dve.tensor_scalar(moving[:, :], ent[STEPS % 2][:, :], VALID - 1, None, ALU.bitwise_and))
                step(dve.tensor_tensor(rank[:, :], place[:, :], moving[:, :], ALU.add))
                dve.tensor_scalar(ids[:, :], rank[:, :], consts["span0"][:, 0:1], None, ALU.add).then_inc(s["done"], 1)
                dve.wait_ge(s["bases"], 1)
                dve.tensor_copy(base[:, :], pc[:, 0:P])
                step(dve.tensor_scalar(jump[:, :], pc[:, P:2 * P], -1.0, float(SPAN), ALU.mult, ALU.add))
                b3 = base[:, :].rearrange("p (e q) -> p e q", e=NEXP)[:, :, 1:GROUP]
                j3 = jump[:, :].rearrange("p (e q) -> p e q", e=NEXP)[:, :, 0:GROUP - 1]
                for e in range(NEXP):
                    ins = dve.tensor_tensor(cmp_[:, e, :, :], spread(b3[:, e, :], 1, KC), spread(slot[:, :], 2, GROUP - 1), ALU.is_le)
                step(ins)
                for e in range(NEXP):
                    ins = dve.tensor_tensor(cmp_[:, e, :, :], cmp_[:, e, :, :], spread(j3[:, e, :], 1, KC), ALU.mult)
                step(ins)
                step(dve.tensor_reduce(addr[:, :, :], cmp_[:, :, :, :], AX.X, ALU.add))
                step(dve.tensor_tensor(slots[:, :].rearrange("p (e t) -> p e t", e=NEXP), addr[:, :, :], home[:, :, :], ALU.add))


def experts(nc, io, dram, slots, weights, tg, consts, NTOK, K):
    BLK = 4 * P
    BPE = K // BLK
    NBLK = NEXP * BPE
    ident = consts["ident"]
    rows_v, list_v = dram["xf"], dram["list"]
    out_rows = io["out"].rearrange("b s e -> (b s) e")
    with ExitStack() as ctx:
        def sb(name, shape, dt=FP32):
            return ctx.enter_context(nc.sbuf_tensor(name, shape, dt))

        def sem(name):
            return ctx.enter_context(nc.semaphore("e_" + name))

        xg = sb("xg", [P, 4, XW])
        xT = [sb("xT_hi", [P, CH, BLK], FP32R), sb("xT_lo", [P, CH, BLK], FP32R)]
        mid = [sb("mid_hi", [P, FCH, BLK], FP32R), sb("mid_lo", [P, FCH, BLK], FP32R)]
        z = sb("z", [P, 2, BLK])
        y = sb("y", [P, 4, E_DIM])
        gs = sb("gs", [P, 2, 4])
        bup = sb("bup", [P, NEXP // 2, FCH])
        bdn = sb("bdn", [P, 2, E_DIM])
        idx = sb("idx", [P, 2, 4], I32)
        UP = [ctx.enter_context(nc.psum_tensor(f"UP{n}", [P, BLK], FP32)) for n in range(3)]
        DN = [ctx.enter_context(nc.psum_tensor(f"DN{n}", [P, E_DIM], FP32)) for n in range(2)]
        T = [ctx.enter_context(nc.psum_tensor(f"TT{n}", [P, BLK], FP32)) for n in range(2)]
        s = {n: sem(n) for n in "bup rows up z hi mid dn yp y tfull thi tlo gs dve".split()}
        s_ix = [sem(f"ix{n}") for n in range(2)]
        s_sc = [sem(f"sc{n}") for n in range(4)]
        s_bd = [sem(f"bd{n}") for n in range(2)]

        def rows_of(f):
            return P if f < FCH - 1 else FLAST

        first_down = weights.upto("down", 0)

        def down_pieces(n):
            e = n // BPE
            return [] if n % BPE or e == 0 else list(range(weights.upto("down", e) - (FCH + 1) // 2, weights.upto("down", e)))

        def up_pieces(n):
            e = (n + 1) // BPE
            return list(range(weights.upto("up", e) - CH, weights.upto("up", e))) if (n + 1) % BPE == 0 and e % 2 == 0 and e < NEXP else []

        with nc.Block() as block:
            @block.sync
            def _(sp):
                full = (FCH - 1) * P
                with nc.allow_non_contiguous_dma(reason="biases by partition, once"):
                    for g in range(NEXP // 2):
                        sp.dma_start(bup[:, g, 0:FCH - 1], io["bup"][g, 0:full].rearrange("(c p) -> p c", p=P)).then_inc(s["bup"], 16)
                        sp.dma_start(bup[0:FLAST, g, FCH - 1:FCH], io["bup"][g, full:FDIM].unsqueeze(1)).then_inc(s["bup"], 16)
                m = first_down
                for e in range(NEXP):
                    if e >= 2:
                        sp.wait_ge(s["y"], 4 * BPE * (e - 1))
                    sp.dma_start(bdn[:, e % 2, :], io["bdown"][e].partition_broadcast(P)).then_inc(s_bd[e % 2], 16)
                    while e + 1 < NEXP and m < weights.upto("down", e + 1):
                        weights.load(sp, m)
                        m += 1

            @block.gpsimd
            def _(pool):
                def list_rows(n):
                    if n >= 2:
                        for t in range(4):
                            pool.wait_ge(s_sc[t], 16 * (n - 1))
                    for t in range(4):
                        pool.indirect_dma_start(idx[:, n % 2, t:t + 1], None, list_v, bass.IndirectOffsetOnAxis(
                            ap=slots[:, 4 * n + t:4 * n + t + 1], axis=0)).then_inc(s_ix[n % 2], 16)

                def gather(n):
                    pool.wait_ge(s_ix[n % 2], 64 * (n // 2 + 1))
                    if n >= 1:
                        pool.wait_ge(s["tfull"], CH * n)
                        pool.wait_ge(s["gs"], n)
                    for t in range(4):
                        pool.indirect_dma_start(xg[:, t, :], None, rows_v, bass.IndirectOffsetOnAxis(
                            ap=idx[:, n % 2, t:t + 1].bitcast(U32), axis=0)).then_inc(s["rows"], 16)

                list_rows(0)
                gather(0)
                if NBLK > 1:
                    list_rows(1)
                for n in range(NBLK):
                    if n + 1 < NBLK:
                        gather(n + 1)
                    for t in range(4):
                        m = 4 * n + t
                        pool.wait_ge(s["y"], m + 1)
                        if n % BPE == 0 and n and t == 0:
                            for u in range(4):
                                pool.wait_ge(s_sc[u], 16 * n)
                        pool.indirect_dma_start(out_rows, bass.IndirectOffsetOnAxis(ap=idx[:, n % 2, t:t + 1].bitcast(U32), axis=0),
                                                y[:, t, :], None, compute_op=ALU.add).then_inc(s_sc[t], 16)
                    if n + 2 < NBLK:
                        list_rows(n + 2)
                for t in range(4):
                    pool.wait_ge(s_sc[t], 16 * NBLK)

            @block.scalar
            def _(act):
                def turn_hi(n, c):
                    act.wait_ge(s["tfull"], CH * n + c + 1)
                    act.activation(xT[0][:, c, :], T[c % 2][:, :], ACT.Copy).then_inc(s["thi"], 1)

                act.wait_ge(s["bup"], 16 * NEXP)
                for c in range(CH):
                    turn_hi(0, c)
                for n in range(NBLK):
                    e = n // BPE
                    more = down_pieces(n)
                    for f in range(FCH):
                        k, r = FCH * n + f, rows_of(f)
                        act.wait_ge(s["up"], k + 1)
                        if k >= 2:
                            act.wait_ge(s["mid"], k - 1)
                        act.activation(z[0:r, k % 2, :], UP[k % 3][0:r, :], ACT.Silu, bias=bup[0:r, e // 2, f:f + 1]).then_inc(s["z"], 1)
                        if more:
                            weights.hi(act, more.pop(0))
                    more = up_pieces(n)
                    for t in range(4):
                        if n + 1 < NBLK:
                            turn_hi(n + 1, t)
                        if more:
                            weights.hi(act, more.pop(0))

            @block.tensor
            def _(pe):
                def turn(n, c):
                    k = CH * n + c
                    if c == 0:
                        pe.wait_ge(s["rows"], 64 * (n + 1))
                    if k >= 2:
                        pe.wait_ge(s["tlo"], k - 1)
                    for t in range(4):
                        mm = pe.transpose(T[c % 2][:, t * P:(t + 1) * P], xg[:, t, c * P:(c + 1) * P], ident[:, :])
                    mm.then_inc(s["tfull"], 1)

                for c in range(CH):
                    turn(0, c)
                for n in range(NBLK):
                    e = n // BPE
                    if n % BPE == 0:
                        pe.wait_ge(weights.lo_done, weights.upto("up", e))
                    pe.wait_ge(s["tlo"], CH * (n + 1))
                    for f in range(FCH):
                        k, r = FCH * n + f, rows_of(f)
                        if k >= 3:
                            pe.wait_ge(s["z"], k - 2)
                        first = True
                        for c in range(CH):
                            for wa, xa in ((0, 0), (0, 1), (1, 0)):
                                mm = pe.matmul(UP[k % 3][0:r, :], weights.up[wa][:, c, f * P:f * P + r], xT[xa][:, c, :],
                                               start=first, stop=(c == CH - 1 and wa == 1))
                                first = False
                        mm.then_inc(s["up"], 1)
                    if n % BPE == 0:
                        pe.wait_ge(weights.lo_done, weights.upto("down", e))
                    for t in range(4):
                        if n + 1 < NBLK:
                            turn(n + 1, t)
                        m = 4 * n + t
                        if m >= 2:
                            pe.wait_ge(s["yp"], m - 1)
                        if t == 0:
                            pe.wait_ge(s["mid"], FCH * (n + 1))
                        first = True
                        for f in range(FCH):
                            r = rows_of(f)
                            for ma, wa in ((0, 0), (0, 1), (1, 0)):
                                mm = pe.matmul(DN[m % 2][:, :], mid[ma][0:r, f, t * P:(t + 1) * P], weights.down[wa][0:r, f, :],
                                               start=first, stop=(f == FCH - 1 and ma == 1))
                                first = False
                        mm.then_inc(s["dn"], 1)

            @block.vector
            def _(dve):
                def turn_lo(n, c):
                    k = CH * n + c
                    dve.wait_ge(s["thi"], k + 1)
                    dve.tensor_tensor(xT[1][:, c, :], T[c % 2][:, :], xT[0][:, c, :].bitcast(FP32), ALU.subtract).then_inc(s["tlo"], 1)

                def gate(n):
                    e = n // BPE
                    dve.wait_ge(s["rows"], 64 * (n + 1))
                    dve.tensor_scalar(gs[:, n % 2, :], xg[:, :, E_DIM + e], tg["ap"][:, 1:2], None, ALU.mult).then_inc(s["gs"], 1)

                gate(0)
                for c in range(CH):
                    turn_lo(0, c)
                for n in range(NBLK):
                    e = n // BPE
                    more = down_pieces(n)
                    for f in range(FCH):
                        k, r = FCH * n + f, rows_of(f)
                        dve.wait_ge(s["z"], k + 1)
                        dve.tensor_copy(mid[0][0:r, f, :], z[0:r, k % 2, :]).then_inc(s["hi"], 1)
                        dve.wait_ge(s["hi"], k + 1)
                        dve.tensor_tensor(mid[1][0:r, f, :], z[0:r, k % 2, :], mid[0][0:r, f, :].bitcast(FP32), ALU.subtract)\
                            .then_inc(s["mid"], 1)
                        if more:
                            weights.lo(dve, more.pop(0))
                    more = up_pieces(n)
                    if n % BPE == 0:
                        dve.wait_ge(s_bd[e % 2], 16 * (e // 2 + 1))
                    for t in range(4):
                        if n + 1 < NBLK:
                            if t == 0:
                                gate(n + 1)
                            turn_lo(n + 1, t)
                        if more:
                            weights.lo(dve, more.pop(0))
                        m = 4 * n + t
                        dve.wait_ge(s["dn"], m + 1)
                        if n:
                            dve.wait_ge(s_sc[t], 16 * n)
                        dve.tensor_tensor(y[:, t, :], DN[m % 2][:, :], bdn[:, e % 2, :], ALU.add).then_inc(s["yp"], 1)
                        dve.wait_ge(s["yp"], m + 1)
                        dve.tensor_scalar(y[:, t, :], y[:, t, :], gs[:, n % 2, t:t + 1], None, ALU.mult).then_inc(s["y"], 1)


def program(nc, x, ctx_, g_x, g_f, igw, igb, fgw, fgb, outw, Wr, br, Wup, bup, Wdown, bdown, out):
    NB = x.shape[0]
    NTOK = NB * SEQ
    K = NTOK // NEXP
    io = dict(x=x, ctx=ctx_, igw=igw, igb=igb, fgw=fgw, fgb=fgb, outw=outw, Wr=Wr, br=br,
              Wup=Wup, bup=bup, Wdown=Wdown, bdown=bdown, out=out)
    dram = {
        "xf": nc.dram_tensor("rows_scratch", (NTOK, XW), FP32).ap(),
        "gates": nc.dram_tensor("gates_scratch", (NEXP, NTOK), FP32).ap(),
        "list": nc.dram_tensor("list_scratch", (NEXP * NTOK, 1), I32).ap(),
    }
    with ExitStack() as c:
        def sb(name, shape, dt=FP32):
            return c.enter_context(nc.sbuf_tensor(name, shape, dt))

        ident = sb("ident", [P, P]); ones = sb("ones", [P, P]); identb = sb("identb", [P, P], BF16)
        tgt = sb("tanh_g", [P, 2])
        span0 = sb("span0", [P, 1]); part = sb("part", [P, 1], I32)
        sm_all = sb("sm_all", [P, NB * TILES, NEXP])
        slots = sb("slots", [P, NEXP * K // P], U32)
        s_con, s_g, s_tg, s_sp = (c.enter_context(nc.semaphore(n)) for n in ("s_con", "s_g", "s_tg", "s_sp"))
        SPAN = NTOK // (P // NEXP)
        with nc.Block() as block:
            @block.gpsimd
            def _(pool):
                step = Chain(pool, s_con)
                step(pool.memset(ident[:, :], 0.0))
                step(pool.memset(ones[:, :], 1.0))
                step(pool.affine_select(out=ident[:, :], in_=ident[:, :], compare_op=ALU.not_equal, fill=1.0,
                                        base=0, pattern=[[-1, P]], channel_multiplier=1))
                step(pool.tensor_copy(identb[:, :], ident[:, :]))
                step(pool.iota(part[:, :], pattern=[[0, 1]], base=0, channel_multiplier=SPAN))

            @block.scalar
            def _(act):
                act.dma_start(tgt[:, 0:1], g_x.partition_broadcast(P)).then_inc(s_g, 16)
                act.dma_start(tgt[:, 1:2], g_f.partition_broadcast(P)).then_inc(s_g, 16)
                act.wait_ge(s_g, 32)
                act.activation(tgt[:, :], tgt[:, :], ACT.Tanh).then_inc(s_tg, 1)

            @block.vector
            def _(dve):
                dve.wait_ge(s_con, 5)
                dve.tensor_scalar(part[:, :], part[:, :], NTOK - 1, None, ALU.bitwise_and).then_inc(s_sp, 1)
                dve.wait_ge(s_sp, 1)
                dve.tensor_copy(span0[:, :], part[:, :]).then_inc(s_sp, 1)
        consts = dict(ident=ident, identb=identb, ones=ones, span0=span0, sem=s_con, ready=5)
        tg = dict(sem=s_tg, ready=1, ap=tgt)
        attention(nc, io, NB, dram, sm_all, tg, consts)
        with ExitStack() as wctx:
            weights = Weights(nc, io, wctx)
            choose(nc, dram, sm_all, slots, weights, consts, NTOK, K)
            experts(nc, io, dram, slots, weights, tg, consts, NTOK, K)


_INS = ["x", "ctx_1024", "g_xattn", "g_ffn", "L0_xattn_igate_w", "L0_xattn_igate_b", "L0_xattn_fgate_w", "L0_xattn_fgate_b",
        "L0_xattn_out_w", "L0_ffn_Wr", "L0_ffn_br", "L0_ffn_W_up", "L0_ffn_b_up", "L0_ffn_W_down", "L0_ffn_b_down"]


def kernel(**inputs):
    import concourse.bacc as bacc
    from concourse.bass_utils import run_bass_kernel_spmd

    nc = bacc.Bacc("TRN2", target_bir_lowering=False, num_devices=1)
    arrays, args = {}, []
    for name in _INS:
        a = np.ascontiguousarray(inputs[name])
        arrays[f"in_{name}"] = a
        args.append(nc.dram_tensor(f"in_{name}", a.shape, mybir.dt.from_np(a.dtype), kind="ExternalInput").ap())
    shape = inputs["x"].shape
    args.append(nc.dram_tensor("out_x", shape, FP32, kind="ExternalOutput").ap())
    program(nc, *args)
    r = run_bass_kernel_spmd(nc, [arrays], core_ids=[0])
    return r.results[0]["out_x"]
```

```python
import numpy as np
import concourse.bass as bass
from concourse import mybir
from concourse.alu_op_type import AluOpType as ALU
from contextlib import ExitStack

FP32 = mybir.dt.float32
FP32R = mybir.dt.float32r
BF16 = mybir.dt.bfloat16
I32 = mybir.dt.int32
U32 = mybir.dt.uint32
ACT = mybir.ActivationFunctionType
AX = mybir.AxisListType

P = 128
E_DIM = 512
TILES = 4
SEQ = TILES * P
HEADS = 8
DH = E_DIM // HEADS
PAIRS = HEADS // 2
CH = E_DIM // P
VW = DH + 2
ROWW = HEADS * VW
NEXP = 8
FDIM = int(E_DIM * 4 * (2.0 / 3.0))
FCH = -(-FDIM // P)
FLAST = FDIM - (FCH - 1) * P
SPARE = P - FLAST
LAID = 2 * FLAST - SPARE
XW = E_DIM + NEXP
QD = 32
LN_EPS = 1e-5
NORM_EPS = 1e-6
BIG = 1e30
XBUF = 4
VBUF = 3


class Line:

    def __init__(self, sem):
        self.sem, self.n = sem, 0

    def inc(self, instruction, by=1):
        instruction.then_inc(self.sem, by)
        self.n += by
        return self.n


class Chain:

    def __init__(self, eng, sem):
        self.eng, self.line = eng, Line(sem)

    def __call__(self, instruction):
        self.eng.wait_ge(self.line.sem, self.line.inc(instruction))


def spread(ap, axis, n):
    ap = ap.unsqueeze(axis)
    return ap.to_broadcast([n if i == axis else s for i, s in enumerate(ap.shape)])


def newton_rsqrt(step, eng, y, v, t):
    step(eng.tensor_tensor(t, y, y, ALU.mult))
    step(eng.tensor_tensor(t, t, v, ALU.mult))
    step(eng.tensor_scalar(t, t, -0.5, 1.5, ALU.mult, ALU.add))
    step(eng.tensor_tensor(y, y, t, ALU.mult))


def attention(nc, io, NB, dram, sm_all, tg, consts):
    x_v = io["x"].rearrange("b (j p) e -> b p j e", p=P)
    c_v = io["ctx"].rearrange("b (j p) e -> b p j e", p=P)
    out_v = io["out"].rearrange("b (j p) e -> b p j e", p=P)
    xf_v = dram["xf"].rearrange("(b j p) w -> b p j w", j=TILES, p=P)
    ident, identb, ones = consts["ident"], consts["identb"], consts["ones"]
    with ExitStack() as ctx:
        def sb(name, shape, dt=FP32):
            return ctx.enter_context(nc.sbuf_tensor(name, shape, dt))

        def pb(name, shape, dt=FP32):
            return ctx.enter_context(nc.psum_tensor(name, shape, dt))

        def sem(name):
            return ctx.enter_context(nc.semaphore(name))

        xs = sb("xs", [P, XBUF, TILES, E_DIM])
        half = sb("half", [P, TILES, HEADS, DH // 2])
        vaug = sb("vaug", [P, VBUF, TILES * ROWW + P])
        q = sb("q", [P, TILES, E_DIM])
        qT = sb("qT", [P, 2, CH, SEQ])
        kT = sb("kT", [P, CH, SEQ])
        kpad = sb("kpad", [P, 2, CH, SEQ])
        xfb = sb("xfb", [P, 2, TILES, XW])
        C = sb("C", [P, HEADS, SEQ])
        D = sb("D", [P, 2, SEQ])
        qw = sb("qw", [P, CH, SEQ - P])
        uv = sb("uv", [P, TILES - 1, HEADS, VW])
        S = sb("S", [P, TILES - 1, PAIRS, 2 * VW])
        nsb = sb("nsb", [P, TILES, HEADS, VW])
        ee = sb("ee", [8, SEQ]); cs = sb("cs", [8, SEQ])
        aa = sb("aa", [8, SEQ]); MM = sb("MM", [8, SEQ])
        Z = sb("Z", [72, SEQ]); Zx = sb("Zx", [104, SEQ])
        Mhl = sb("Mhl", [40, SEQ], FP32R)
        whl = sb("whl", [40, SEQ - P], FP32R)
        gd = sb("gd", [8, 2]); gdiag = sb("gdiag", [8, 2, 8]); gb = sb("gb", [P, 2, 8])
        tm = sb("tm", [P, TILES, 4, HEADS])
        selM = sb("selM", [40, HEADS, P], FP32R); selP = sb("selP", [40, PAIRS, P], FP32R)
        maskneg = sb("maskneg", [P, SEQ], BF16)
        gW = sb("gW", [P, 2 * CH, 40])
        gbias = sb("gbias", [40, 1])
        Wr = sb("Wr", [P, CH, NEXP]); br = sb("br", [NEXP, 1]); Wo = sb("Wo", [P, E_DIM])
        st = sb("st", [P, TILES, 6]); mv = sb("mv", [P, TILES, 2]); va = sb("va", [P, TILES]); ra = sb("ra", [P, TILES]); ta = sb("ta", [P, TILES])
        st2 = sb("st2", [P, TILES, 6]); mv2 = sb("mv2", [P, TILES, 2]); vb = sb("vb", [P, TILES]); rb = sb("rb", [P, TILES]); tb = sb("tb", [P, TILES])
        la = sb("la", [P, TILES]); lb = sb("lb", [P, TILES]); lh = sb("lh", [P, TILES * HEADS])
        msum = sb("msum", [P, TILES * HEADS])
        nrm = sb("nrm", [P, 2, TILES * HEADS]); rn = sb("rn", [P, TILES * HEADS]); ssq = sb("ssq", [P, TILES * HEADS])
        vh = sb("vh", [P, TILES * HEADS]); rh = sb("rh", [P, TILES * HEADS]); th = sb("th", [P, TILES * HEADS])
        lt = sb("lt", [P, TILES, NEXP]); mx = sb("mx", [P, TILES]); sx = sb("sx", [P, TILES]); ex = sb("ex", [P, TILES, NEXP])

        xfT = q
        lg = ee
        gwr = C[0:16, 0:3, :].rearrange("g n e -> g (n e)")
        self_ = C[0:40, 4:6, :].rearrange("k a (h s) -> k (a h) s", s=P)

        T = [pb("T0", [P, SEQ]), pb("T1", [P, SEQ])]
        G = pb("G", [P, SEQ])
        EB = pb("EB", [P, SEQ])
        W = pb("W", [P, 2, SEQ])
        A0 = pb("A0", [P, HEADS, P])
        EX = [EB, G]
        QK = [W[:, 0, :], W[:, 1, :]]
        A = [A0[:, :, :], W[:, :, :].rearrange("p a (h w) -> p (a h) w", w=P)]

        AHEAD = 2
        GCOL = 104
        names = ("tfull ta td ldw v1 r1 q v2 r2 xf2 vg gates gput ex1 ln1 zz zx gg gx "
                 "ms tmf tmd ee dd qk cc af an cen sq lnh lnb rh x2 x2v lex smx vaug kpad uv "
                 "dchain achain pchain prep1 prep2 prep3 ").split()
        s = {n: sem("a_" + n) for n in names}
        s_xl = [sem(f"a_xl{i}") for i in range(XBUF)]
        s_xst = [sem(f"a_xst{i}") for i in range(XBUF)]
        s_cd = [sem(f"a_cd{i}") for i in range(VBUF)]
        s_fst = [sem(f"a_fst{i}") for i in range(2)]

        order, owner = [], {}

        def iteration_fills(i):
            if 0 <= i - 1 < NB:
                yield from [("q", i - 1, c, "act") for c in range(CH)]
                yield from [("k", i - 1, c, "act") for c in range(CH)]
            if 0 <= i - 2 < NB:
                for h in range(HEADS - 1):
                    yield (("st", i - 2, h // 2, "dve") if h in (0, 2, 4) else
                           ("qw", i - 2, {1: 0, 3: 1, 5: 2, 6: 3}[h], "dve"))
            if 0 <= i - 4 < NB:
                yield from [("xfT", i - 4, c, "act") for c in range(CH)]
                yield ("lg", i - 4, 0, "act")
                yield ("lt", i - 4, 0, "dve")

        number, freed, counts = {}, [], {"act": 0, "dve": 0}
        for i in range(NB + 5):
            for kind, b, k, who in iteration_fills(i):
                number[kind, b, k] = len(freed)
                counts[who] += 1
                freed.append((s["ta" if who == "act" else "td"], counts[who]))

        def bank(kind, b, k):
            return T[number[kind, b, k] % 2]

        def fill(pe, kind, b, k):
            n = number[kind, b, k]
            if n >= 2:
                pe.wait_ge(*freed[n - 2])
            return T[n % 2]

        def filled(eng, kind, b, k):
            eng.wait_ge(s["tfull"], number[kind, b, k] + 1)
            return bank(kind, b, k)

        def wait_x2(eng, b):
            eng.wait_ge(s["x2"], b + 1)
            if b == NB - 1:
                eng.wait_ge(s["x2v"], 1)

        def weigh(step, eng, b, tiles):
            n = nsb[:, tiles, :, 0:DH]
            scale = rh[:, :].rearrange("p (j h) -> p j h", h=HEADS)[:, tiles, :]
            count = tiles.stop - tiles.start
            step(eng.tensor_tensor(n.rearrange("p j h d -> p (j h) d"), n.rearrange("p j h d -> p (j h) d"),
                                   spread(scale.rearrange("p j h -> p (j h)"), 2, DH), ALU.mult))
            for j in range(tiles.start, tiles.stop):
                ins = eng.tensor_tensor(nsb[:, j, :, 0:DH], nsb[:, j, :, 0:DH], Wo[:, :].rearrange("p (h d) -> p h d", d=DH), ALU.mult)
            step(ins)
            xb = xs[:, b % XBUF, tiles, :].rearrange("p j (h d) -> p (j h) d", d=DH)
            return eng.tensor_tensor(xb, xb, n.rearrange("p j h d -> p (j h) d"), ALU.add)

        def v_of(b, j, c0, n):
            return vaug[:, b % VBUF, j * ROWW + c0:j * ROWW + c0 + n]

        def v_all(b):
            return vaug[:, b % VBUF, 0:TILES * ROWW].rearrange("p (j w) -> p j w", w=ROWW)[:, :, 0:E_DIM]

        def v_wide(b, j, h):
            at, more = j * ROWW + DH * h, E_DIM + 2 * h - DH * h
            first = vaug[:, b % VBUF, at:at + DH]
            return bass.AP(tensor=first.tensor, offset=first.offset, ap=[first.ap[0], [more, 2], [1, DH]])

        with nc.Block() as block:
            @block.sync
            def _(sp):
                def store_x2(b):
                    if 0 <= b < NB:
                        wait_x2(sp, b)
                        sp.dma_start(out_v[b], xs[:, b % XBUF, :, :]).then_inc(s_xst[b % XBUF], 16)

                def store_rows(b):
                    if 0 <= b < NB:
                        sp.wait_ge(s["smx"], b + 1)
                        sp.dma_start(xf_v[b], xfb[:, b % 2, :, :]).then_inc(s_fst[b % 2], 16)

                sp.dma_start(xs[:, 0, :, :], x_v[0]).then_inc(s_xl[0], 16)
                sp.dma_start(v_all(0), c_v[0]).then_inc(s_cd[0], 16)
                sp.dma_start(gwr[0:8, :], io["igw"]).then_inc(s["ldw"], 16)
                sp.dma_start(gwr[8:16, :], io["fgw"]).then_inc(s["ldw"], 16)
                sp.dma_start(gbias[0:8, :], io["igb"].unsqueeze(1)).then_inc(s["ldw"], 16)
                sp.dma_start(gbias[32:40, :], io["fgb"].unsqueeze(1)).then_inc(s["ldw"], 16)
                sp.dma_start(Wr[:, :, :], io["Wr"].rearrange("(c p) n -> p c n", p=P)).then_inc(s["ldw"], 16)
                sp.dma_start(br[:, :], io["br"].unsqueeze(1)).then_inc(s["ldw"], 16)
                sp.dma_start(Wo[:, :], io["outw"].partition_broadcast(P)).then_inc(s["ldw"], 16)
                for b in range(1, min(XBUF, NB)):
                    if b < VBUF:
                        sp.dma_start(v_all(b), c_v[b]).then_inc(s_cd[b % VBUF], 16)
                    sp.dma_start(xs[:, b % XBUF, :, :], x_v[b]).then_inc(s_xl[b % XBUF], 16)
                for i in range(NB + 5):
                    if VBUF <= i < NB:
                        sp.wait_ge(s["af"], TILES * (i - VBUF + 1))
                        sp.dma_start(v_all(i), c_v[i]).then_inc(s_cd[i % VBUF], 16)
                    if XBUF <= i < NB:
                        sp.wait_ge(s_xst[i % XBUF], 16 * (i // XBUF))
                        sp.wait_ge(s["xf2"], i - XBUF + 1)
                        sp.dma_start(xs[:, i % XBUF, :, :], x_v[i]).then_inc(s_xl[i % XBUF], 16)
                    if i <= NB:
                        store_x2(i - 3)
                        store_rows(i - 5)
                    else:
                        store_rows(i - 5)
                        store_x2(i - 3)
                for n in range(XBUF):
                    sp.wait_ge(s_xst[n], 16 * len(range(n, NB, XBUF)))
                for n in range(2):
                    sp.wait_ge(s_fst[n], 16 * len(range(n, NB, 2)))

            @block.gpsimd
            def _(pool):
                step = Chain(pool, s["pchain"])
                for n in range(VBUF):
                    step(pool.memset(vaug[:, n, 0:TILES * ROWW].rearrange("p (j w) -> p j w", w=ROWW)[:, :, E_DIM:ROWW], 1.0))
                step(pool.memset(vaug[:, :, TILES * ROWW:TILES * ROWW + P], 1.0))

                def constants():
                    step(pool.memset(self_[:, :, :], 0.0))
                    step(pool.affine_select(out=self_[:, :, :], in_=self_[:, :, :], compare_op=ALU.not_equal, fill=1.0,
                                            base=0, pattern=[[-1, HEADS], [0, P]], channel_multiplier=1))
                    step(pool.affine_select(out=self_[:, :, :], in_=self_[:, :, :], compare_op=ALU.not_equal, fill=-1.0,
                                            base=-QD, pattern=[[-1, HEADS], [0, P]], channel_multiplier=1))
                    step(pool.tensor_copy(selM[:, :, :], self_[:, :, :]))
                    step(pool.memset(self_[:, :, :], 0.0))
                    v = self_[:, 0:PAIRS, :].rearrange("k p (a d) -> k p a d", a=2)
                    step(pool.affine_select(out=v, in_=v, compare_op=ALU.not_equal, fill=1.0, base=0,
                                            pattern=[[-2, PAIRS], [-1, 2], [0, DH]], channel_multiplier=1))
                    step(pool.affine_select(out=v, in_=v, compare_op=ALU.not_equal, fill=1.0, base=-QD,
                                            pattern=[[-2, PAIRS], [-1, 2], [0, DH]], channel_multiplier=1))
                    step(pool.tensor_copy(selP[:, :, :], self_[:, 0:PAIRS, :]))
                    step(pool.memset(maskneg[:, :], 0.0))
                    m = maskneg[:, :].rearrange("p (j s) -> p j s", j=TILES)
                    step(pool.affine_select(out=m, in_=m, compare_op=ALU.is_ge, fill=-BIG, base=0,
                                            pattern=[[0, TILES], [1, P]], channel_multiplier=-1))
                    pool.wait_ge(s["ldw"], 7 * 16)
                    pool.wait_ge(tg["sem"], tg["ready"])
                    pool.tensor_scalar(Wo[:, :], Wo[:, :], tg["ap"][:, 0:1], None, ALU.mult).then_inc(s["prep1"], 1)
                    pool.wait_ge(s["prep1"], 1)

                def head_means(b):
                    pool.wait_ge(s_cd[b % VBUF], 16 * (b // VBUF + 1))
                    w = DH // 2
                    src = v_all(b).rearrange("p j (h d) -> p j h d", d=DH)
                    for j in range(TILES):
                        ins = pool.tensor_tensor(half[:, j, :, :], src[:, j, :, 0:w], src[:, j, :, w:2 * w], ALU.add)
                    step(ins)
                    part = half[:, :, :, :].rearrange("p j h w -> p (j h) w")
                    while w > 1:
                        w //= 2
                        o_ = part[:, :, 0:w] if w > 1 else msum[:, :].unsqueeze(2)
                        step(pool.tensor_tensor(o_, part[:, :, 0:w], part[:, :, w:2 * w], ALU.add))
                    means = vaug[:, b % VBUF, 0:TILES * ROWW].rearrange("p (j w) -> p j w", w=ROWW)[:, :, E_DIM + 1:ROWW:2]
                    pool.tensor_scalar(means, msum[:, :].rearrange("p (j h) -> p j h", h=HEADS), 1.0 / DH, None, ALU.mult)\
                        .then_inc(s["vaug"], 1)
                    pool.wait_ge(s["vaug"], b + 1)

                def weigh_v(b):
                    pool.wait_ge(s["tmd"], b + 1)
                    if b >= 1:
                        pool.wait_ge(s["tfull"], number["st", b - 1, 2] + 1)
                    for j in range(TILES - 1):
                        pool.tensor_tensor(uv[:, j, :, 0:DH], v_of(b, j, 0, E_DIM).rearrange("p (h d) -> p h d", d=DH),
                                           spread(tm[:, j, 0, :], 2, DH), ALU.mult)
                        ins = pool.tensor_tensor(uv[:, j, :, DH:VW], v_of(b, j, E_DIM, 2 * HEADS).rearrange("p (h d) -> p h d", d=2),
                                                 spread(tm[:, j, 0, :], 2, 2), ALU.mult)
                    ins.then_inc(s["uv"], 1)
                    pool.wait_ge(s["uv"], b + 1)

                def centre(b):
                    for j in range(TILES):
                        pool.wait_ge(s["an"], TILES * b + j + 1)
                        pool.tensor_tensor(nsb[:, j, :, 0:DH], nsb[:, j, :, 0:DH], nsb[:, j, :, DH + 1:DH + 2].to_broadcast([P, HEADS, DH]),
                                           ALU.subtract).then_inc(s["cen"], 1)
                    pool.wait_ge(s["cen"], TILES * (b + 1))

                def weigh_out(b):
                    pool.wait_ge(s["rh"], b + 1)
                    weigh(step, pool, b, slice(0, TILES if b < NB - 1 else 1)).then_inc(s["x2"], 1)
                    pool.wait_ge(s["x2"], b + 1)

                for i in range(NB + 5):
                    if 0 <= i - 2 < NB:
                        weigh_v(i - 2)
                    if i < NB:
                        head_means(i)
                    if i == 0:
                        constants()
                    if 0 <= i - 3 < NB:
                        weigh_out(i - 3)
                    if 0 <= i - 2 < NB:
                        centre(i - 2)

            @block.scalar
            def _(act):
                step = Chain(act, s["achain"])

                def rsqrt_guess(src, tmp, dst, ready, by, log, done):
                    act.wait_ge(ready, by)
                    act.activation(tmp, src, ACT.Ln).then_inc(log, 1)
                    act.wait_ge(log, by)
                    act.activation(dst, tmp, ACT.Exp, scale=-0.5).then_inc(done, 1)

                def exponentials(b):
                    if 0 <= b < NB:
                        act.wait_ge(*freed[number["lt", b, 0]])
                        act.activation(ex[:, :, :], lt[:, :, :], ACT.Exp).then_inc(s["lex"], 1)

                act.preload_act_table_set("natural_log_exp_and_others")
                for i in range(NB + 5):
                    if i != NB + 3:
                        exponentials(i - 5)
                    if 0 <= i - 1 < NB:
                        b = i - 1
                        if b >= 2:
                            act.wait_ge(s["qk"], HEADS * (b - 1))
                            act.wait_ge(*freed[number["qw", b - 2, PAIRS - 1]])
                        for c in range(CH):
                            t = filled(act, "q", b, c)
                            act.activation(qT[:, b % 2, c, :], t[:, :], ACT.Copy).then_inc(s["ta"], 1)
                    if i == 1 < NB:
                        rsqrt_guess(va[:, :], la[:, :], ra[:, :], s["v1"], i + 1, s["ln1"], s["r1"])
                    if 0 <= i - 4 < NB:
                        rsqrt_guess(vb[:, :], lb[:, :], rb[:, :], s["v2"], i - 3, s["lnb"], s["r2"])
                    if i == NB + 3:
                        exponentials(i - 5)
                    for c in range(TILES):
                        if 0 <= i - 1 < NB:
                            t = filled(act, "k", i - 1, c)
                            act.activation(kT[:, c, :], t[:, :], ACT.Copy).then_inc(s["ta"], 1)
                        if 0 <= i - 3 < NB:
                            act.wait_ge(s["cen"], TILES * (i - 3) + c + 1)
                            if c == 0:
                                act.wait_ge(s["af"], TILES * (i - 2))
                            act.activation(C[:, c, :].rearrange("p (h d) -> p h d", d=DH), nsb[:, c, :, 0:DH], ACT.Square)\
                               .then_inc(s["sq"], 1)
                    if 0 <= i - 3 < NB:
                        rsqrt_guess(vh[:, :], lh[:, :], rh[:, :], s["lnh"], i - 2, s["ex1"], s["gg"])

                    def log_sigmoid(k):
                        if 0 <= i - 1 < NB:
                            if k == 0:
                                act.wait_ge(s["vg"], i)
                                step(act.activation(ee[:, :], ee[:, :], ACT.Abs))
                            elif k == 1:
                                step(act.activation(ee[:, :], ee[:, :], ACT.Exp, scale=-1.0))
                            else:
                                act.activation(ee[:, :], ee[:, :], ACT.Ln, bias=1.0).then_inc(s["gx"], 1)

                    for h in range(HEADS):
                        if 0 <= i - 2 < NB:
                            b = i - 2
                            act.wait_ge(s["ee"], HEADS * b + h + 1)
                            if HEADS * b + h >= 2:
                                act.wait_ge(s["cc"], HEADS * b + h - 1)
                            if h == 0:
                                act.wait_ge(s["tmd"], b + 1)
                            for j in range(TILES):
                                ins = act.activation(D[:, h % 2, j * P:(j + 1) * P], EX[h % 2][:, j * P:(j + 1) * P], ACT.Exp,
                                                     bias=tm[:, j, 3, h:h + 1])
                            ins.then_inc(s["dd"], 1)
                        if 2 <= h < 5:
                            log_sigmoid(h - 2)

                    def numerators(j):
                        if 0 <= i - 2 < NB:
                            b = i - 2
                            act.wait_ge(s["af"], TILES * b + j + 1)
                            if j == 0 and b >= 1:
                                act.wait_ge(s["x2"], b)
                            act.activation(nsb[:, j, :, :], A[j % 2][:, :, 0:VW], ACT.Copy).then_inc(s["an"], 1)

                    def turned_rows(c):
                        if 0 <= i - 4 < NB:
                            t = filled(act, "xfT", i - 4, c)
                            act.activation(xfT[:, c, :], t[:, :], ACT.Copy).then_inc(s["ta"], 1)

                    def pad_keys(par):
                        if 0 <= i - 1 < NB:
                            b = i - 1
                            if b >= 1:
                                act.wait_ge(s["qk"], HEADS * b)
                            act.wait_ge(*freed[number["k", b, CH - 1]])
                            r = slice(DH * par, DH * par + DH)
                            act.activation(kpad[r, par, :, :], kT[r, :, :], ACT.Copy, scale=DH ** -0.5).then_inc(s["kpad"], 1)

                    turned_rows(0)
                    turned_rows(1)
                    if 0 <= i - 1 < NB:
                        b = i - 1
                        act.wait_ge(s["zz"], b + 1)
                        if b >= 1:
                            act.wait_ge(s["tmf"], b)
                        act.activation(Zx[0:72, :], Z[0:72, :], ACT.Exp).then_inc(s["zx"], 1)
                        act.activation(gd[:, :], gd[:, :], ACT.Exp).then_inc(s["zx"], 1)
                    numerators(0)
                    turned_rows(2)
                    turned_rows(3)
                    numerators(1)
                    pad_keys(0)
                    numerators(2)
                    if i < NB and i != 1:
                        rsqrt_guess(va[:, :], la[:, :], ra[:, :], s["v1"], i + 1, s["ln1"], s["r1"])
                    pad_keys(1)
                    if 0 <= i - 4 < NB:
                        t = filled(act, "lg", i - 4, 0)
                        act.activation(lg[:, :], t[0:NEXP, :], ACT.Identity, bias=br[:, :]).then_inc(s["ta"], 1)
                    numerators(3)

            @block.tensor
            def _(pe):
                pe.wait_ge(s["ldw"], 7 * 16)
                pe.wait_ge(consts["sem"], consts["ready"])
                for c in range(3 * CH):
                    mm = pe.transpose(G[:, 16 * c:16 * c + 16], gwr[:, c * P:(c + 1) * P], ident[0:16, 0:16])
                mm.then_inc(s["prep2"], 1)
                pe.wait_ge(s["prep3"], 1)

                def turn_gates(b):
                    if b >= 1:
                        pe.wait_ge(s["dd"], HEADS * b - 1)
                    pe.wait_ge(s["zx"], 2 * b + 2)
                    pe.wait_ge(s["ms"], b + 1)
                    for j in range(TILES):
                        pe.transpose(EB[:, j * P:j * P + 104], Zx[:, j * P:(j + 1) * P], ident[0:104, 0:104])
                    pe.matmul(EB[:, GCOL:GCOL + 16], ones[0:8, :], gdiag[:, :, :].rearrange("k j h -> k (j h)"), start=True, stop=True)\
                      .then_inc(s["tmf"], 1)

                def scores(b, h):
                    n = HEADS * b + h
                    if n >= 2:
                        pe.wait_ge(s["cc"], n - 1)
                    for j in range(TILES):
                        jj = slice(j * P, (j + 1) * P)
                        mm = pe.matmul(QK[h % 2][:, jj], kpad[:, h % 2, h // 2, jj], qT[:, b % 2, h // 2, jj], start=True, stop=True)
                    mm.then_inc(s["qk"], 1)

                for i in range(NB + 5):
                    if 0 <= i - 1 < NB:
                        b = i - 1
                        pe.wait_ge(s["q"], b + 1)
                        pe.wait_ge(s["vaug"], b + 1)
                        if b >= 1:
                            pe.wait_ge(s["gput"], b)
                        if b >= 2:
                            pe.wait_ge(s["dd"], HEADS * (b - 1))
                        for c in range(2 * CH + AHEAD):
                            if c < 2 * CH:
                                kind, k = ("q", c) if c < CH else ("k", c - CH)
                                t = fill(pe, kind, b, k)
                                for j in range(TILES):
                                    src = q[:, j, k * P:(k + 1) * P] if kind == "q" else v_of(b, j, k * P, P)
                                    mm = pe.transpose(t[:, j * P:(j + 1) * P], src, ident[:, :])
                                mm.then_inc(s["tfull"], 1)
                            if c == AHEAD - 1 and i >= 2:
                                turn_gates(i - 2)
                            g = c - AHEAD
                            if g >= 0:
                                pe.wait_ge(*freed[number[("q", b, g) if g < CH else ("k", b, g - CH)]])
                                src = qT[:, b % 2, g, :] if g < CH else kT[:, g - CH, :]
                                mm = pe.matmul(G[0:40, :], gW[:, g, :], src, start=(g == 0), stop=(g == 2 * CH - 1))
                        mm.then_inc(s["gates"], 1)
                    if i == NB + 1:
                        turn_gates(i - 2)
                    if 0 <= i - 2 < NB:
                        b = i - 2
                        if b == 0:
                            pe.wait_ge(s["prep1"], 1)
                        pe.wait_ge(s["kpad"], 2 * b + 2)
                        if b >= 1:
                            pe.wait_ge(s["an"], TILES * b)
                        for h in range(HEADS):
                            n = HEADS * b + h
                            if n >= 2:
                                pe.wait_ge(s["dd"], n - 1)
                            if h == 0:
                                pe.wait_ge(s["tmd"], b + 1)
                            if h == 1:
                                scores(b, h)
                                pe.wait_ge(s["gput"], min(i, NB))
                            pe.matmul(EX[h % 2][:, :], identb[:, :], maskneg[:, :], start=True, stop=False)
                            pe.matmul(EX[h % 2][:, :], selM[:, h, :], Mhl[:, :], start=False, stop=True).then_inc(s["ee"], 1)
                            if h != 1:
                                scores(b, h)
                            if h in (0, 2, 4):
                                j = h // 2
                                t = fill(pe, "st", b, j)
                                if h == 0:
                                    pe.wait_ge(s["uv"], b + 1)
                                for g in range(HEADS):
                                    r = DH * (g % 2)
                                    mm = pe.matmul(t[r:r + DH, (g // 2) * VW:(g // 2 + 1) * VW], v_of(b, j, g * DH, DH),
                                                   uv[:, j, g, :], start=True, stop=True)
                                mm.then_inc(s["tfull"], 1)
                            elif h != HEADS - 1:
                                p = {1: 0, 3: 1, 5: 2, 6: 3}[h]
                                t = fill(pe, "qw", b, p)
                                pe.matmul(t[:, 0:SEQ - P], selP[:, p, :], whl[:, :], start=True, stop=True).then_inc(s["tfull"], 1)

                    def product(j):
                        if not 0 <= i - 2 < NB:
                            return
                        b = i - 2
                        n = TILES * b + j
                        if j == 1:
                            pe.wait_ge(*freed[number["qw", b, 3]])
                        if n >= 2:
                            pe.wait_ge(s["an"], n - 1)
                        for h in range(HEADS):
                            if j == 0:
                                pe.wait_ge(s["cc"], HEADS * b + h + 1)
                            mm = pe.matmul(A[j % 2][:, h, :].rearrange("p (a w) -> p a w", a=2), C[:, h, j * P:(j + 1) * P], v_wide(b, j, h),
                                           start=(h % 4 == 0), stop=(j == 0), skip_group_check=True)
                        if j:
                            for p in range(PAIRS):
                                mm = pe.matmul(A[j % 2][:, 2 * p:2 * p + 2, 0:VW], qw[:, p, (j - 1) * P:j * P],
                                               S[:, j - 1, p, :].rearrange("k (a w) -> k a w", a=2),
                                               start=False, stop=True, skip_group_check=True)
                        mm.then_inc(s["af"], 1)

                    def turn_rows(c):
                        if not 0 <= i - 4 < NB:
                            return
                        b = i - 4
                        if c == 0:
                            pe.wait_ge(s["xf2"], b + 1)
                        t = fill(pe, "xfT", b, c)
                        for j in range(TILES):
                            mm = pe.transpose(t[:, j * P:(j + 1) * P], xfb[:, b % 2, j, c * P:(c + 1) * P], ident[:, :])
                        mm.then_inc(s["tfull"], 1)

                    product(0)
                    turn_rows(0)
                    turn_rows(1)
                    product(1)
                    turn_rows(2)
                    turn_rows(3)
                    product(2)
                    if 0 <= i - 4 < NB:
                        b = i - 4
                        t = fill(pe, "lg", b, 0)
                        pe.wait_ge(*freed[number["xfT", b, CH - 1]])
                        for c in range(CH):
                            mm = pe.matmul(t[0:NEXP, :], Wr[:, c, :], xfT[:, c, :], start=(c == 0), stop=(c == CH - 1))
                        mm.then_inc(s["tfull"], 1)
                    product(3)
                    if 0 <= i - 4 < NB:
                        t = fill(pe, "lt", b, 0)
                        pe.wait_ge(*freed[number["lg", b, 0]])
                        for j in range(TILES):
                            mm = pe.transpose(t[:, j * NEXP:(j + 1) * NEXP], lg[:, j * P:(j + 1) * P], ident[0:NEXP, 0:NEXP])
                        mm.then_inc(s["tfull"], 1)

            @block.vector
            def _(dve):
                step = Chain(dve, s["dchain"])
                for t in (gW[:, :, :], kpad[:, :, :, :], S[:, :, :, :], Z[:, :], Zx[:, :],
                          Mhl[:, :].bitcast(FP32), whl[:, :].bitcast(FP32)):
                    step(dve.memset(t, 0.0))
                dve.wait_ge(s["prep2"], 1)
                g3 = G[:, 0:48 * CH].rearrange("p (c g) -> p c g", g=16)
                step(dve.tensor_copy(gW[:, :, 0:8], g3[:, 0:2 * CH, 0:8]))
                step(dve.tensor_copy(gW[:, :, 32:40], g3[:, 0:2 * CH, 8:16]))
                step(dve.tensor_tensor(gW[:, CH:2 * CH, 0:8], gW[:, CH:2 * CH, 0:8], g3[:, 2 * CH:3 * CH, 0:8], ALU.add))
                dve.tensor_tensor(gW[:, CH:2 * CH, 32:40], gW[:, CH:2 * CH, 32:40], g3[:, 2 * CH:3 * CH, 8:16], ALU.add)\
                    .then_inc(s["prep3"], 1)

                def statistics(src, st_, mv_, v_):
                    for j in range(TILES):
                        ins = dve.bn_stats(st_[:, j, :], src[:, j, :])
                    step(ins)
                    for j in range(TILES):
                        ins = dve.bn_aggr(mv_[:, j, :], st_[:, j, :])
                    step(ins)
                    return dve.tensor_scalar(v_, mv_[:, :, 1], LN_EPS, None, ALU.add)

                def normalised_rows(b):
                    if not 0 <= b < NB:
                        return
                    xb = xs[:, b % XBUF, :, :]
                    if b >= 2:
                        dve.wait_ge(s_fst[b % 2], 16 * (b // 2))
                    dve.wait_ge(s["r2"], b + 1)
                    newton_rsqrt(step, dve, rb[:, :], vb[:, :], tb[:, :])
                    for j in range(TILES):
                        ins = dve.tensor_scalar(xfb[:, b % 2, j, 0:E_DIM], xb[:, j, :], mv2[:, j, 0:1], rb[:, j:j + 1], ALU.subtract, ALU.mult)
                    ins.then_inc(s["xf2"], 1)

                def shifted_logits(b):
                    if not 0 <= b < NB:
                        return
                    t = filled(dve, "lt", b, 0)
                    l3 = t[:, 0:TILES * NEXP].rearrange("p (j n) -> p j n", n=NEXP)
                    step(dve.tensor_reduce(mx[:, :], l3, AX.X, ALU.max))
                    dve.tensor_tensor(lt[:, :, :], l3, spread(mx[:, :], 2, NEXP), ALU.subtract).then_inc(s["td"], 1)

                def layernorm_x(i):
                    dve.wait_ge(s_xl[i % XBUF], 16 * (i // XBUF + 1))
                    statistics(xs[:, i % XBUF, :, :], st, mv, va[:, :]).then_inc(s["v1"], 1)
                    dve.wait_ge(s["r1"], i + 1)
                    newton_rsqrt(step, dve, ra[:, :], va[:, :], ta[:, :])
                    if i >= 1:
                        dve.wait_ge(s["tfull"], number["q", i - 1, CH - 1] + 1)
                    if i >= 4:
                        dve.wait_ge(s["tfull"], number["lg", i - 4, 0] + 1)
                    for j in range(TILES):
                        ins = dve.tensor_scalar(q[:, j, :], xs[:, i % XBUF, j, :], mv[:, j, 0:1], ra[:, j:j + 1], ALU.subtract, ALU.mult)
                    ins.then_inc(s["q"], 1)

                for i in range(NB + 5):
                    if i == 1 < NB:
                        layernorm_x(i)
                    if i != NB + 3:
                        shifted_logits(i - 5)
                    if 0 <= i - 4 < NB:
                        b = i - 4
                        wait_x2(dve, b)
                        xb = xs[:, b % XBUF, :, :]
                        statistics(xb, st2, mv2, vb[:, :]).then_inc(s["v2"], 1)
                    if 0 <= i - 2 < NB:
                        b = i - 2
                        dve.wait_ge(s["tmf"], b + 1)
                        t4 = EB[:, :].rearrange("p (j k h) -> p j k h", k=4, h=QD)
                        dve.tensor_copy(nrm[:, b % 2, :].rearrange("p (j h) -> p j h", h=HEADS), t4[:, :, 2, 0:HEADS])
                        dve.tensor_copy(gb[:, :, :].rearrange("p j h -> p (j h)"), EB[:, GCOL:GCOL + 16])
                        dve.tensor_copy(tm[:, :, :, :], t4[:, :, :, 0:HEADS]).then_inc(s["tmd"], 1)
                        dve.wait_ge(s["tmd"], b + 1)
                    if 0 <= i - 3 < NB:
                        b = i - 3
                        n = nsb[:, :, :, :].rearrange("p j h w -> p (j h) w")
                        dve.wait_ge(s["an"], TILES * (b + 1))
                        step(dve.scalar_tensor_tensor(out=rn[:, :].unsqueeze(2), in0=n[:, :, DH:DH + 1], scalar=-1.0,
                                                      in1=n[:, :, DH:DH + 1], op0=ALU.mult, op1=ALU.max))
                        step(dve.tensor_tensor(rn[:, :], rn[:, :], nrm[:, b % 2, :], ALU.max))
                        step(dve.tensor_scalar(rn[:, :], rn[:, :], NORM_EPS, None, ALU.add))
                        step(dve.reciprocal(rn[:, :], rn[:, :]))
                        step(dve.tensor_tensor(th[:, :], rn[:, :], rn[:, :], ALU.mult))
                    normalised_rows(i - 4)
                    if i == NB + 3:
                        shifted_logits(i - 5)
                    if 0 <= i - 3 < NB:
                        b = i - 3
                        for j in range(TILES):
                            dve.wait_ge(s["sq"], TILES * b + j + 1)
                            ins = dve.tensor_reduce(ssq[:, j * HEADS:(j + 1) * HEADS], C[:, j, :].rearrange("p (h d) -> p h d", d=DH), AX.X, ALU.add)
                        step(ins)
                        step(dve.scalar_tensor_tensor(out=th[:, :], in0=ssq[:, :], scalar=1.0 / DH, in1=th[:, :], op0=ALU.mult, op1=ALU.mult))
                        dve.tensor_scalar(vh[:, :], th[:, :], LN_EPS, None, ALU.add).then_inc(s["lnh"], 1)
                    if 0 <= i - 1 < NB:
                        b = i - 1
                        dve.wait_ge(s["gates"], b + 1)
                        fb = gbias[32:40, 0:1]
                        dve.tensor_scalar(ee[:, :], G[32:40, :], fb, None, ALU.add).then_inc(s["vg"], 1)
                        dve.tensor_scalar(MM[:, :], G[32:40, :], fb, 0.0, ALU.add, ALU.min)
                        dve.tensor_scalar(aa[:, :], G[0:8, :], gbias[0:8, 0:1], None, ALU.add).then_inc(s["gput"], 1)
                        dve.wait_ge(s["gput"], b + 1)
                    if 0 <= i - 3 < NB:
                        b = i - 3
                        dve.wait_ge(s["gg"], b + 1)
                        newton_rsqrt(step, dve, rh[:, :], vh[:, :], th[:, :])
                        dve.tensor_tensor(rh[:, :], rh[:, :], rn[:, :], ALU.mult).then_inc(s["rh"], 1)
                        if b == NB - 1:
                            dve.wait_ge(s["rh"], b + 1)
                            weigh(step, dve, b, slice(1, TILES)).then_inc(s["x2v"], 1)
                    if 0 <= i - 2 < NB:
                        b = i - 2
                        for h in range(HEADS):
                            n = HEADS * b + h
                            dve.wait_ge(s["dd"], n + 1)
                            dve.wait_ge(s["qk"], n + 1)
                            dve.tensor_tensor(C[:, h, :], QK[h % 2], D[:, h % 2, :], ALU.mult).then_inc(s["cc"], 1)
                            if h in (0, 2, 4):
                                j = h // 2
                                t = filled(dve, "st", b, j)
                                fresh = t[:, 0:PAIRS * VW].rearrange("k (p w) -> k p w", w=VW)
                                for par in range(2):
                                    r, w = slice(DH * par, DH * par + DH), slice(VW * par, VW * par + VW)
                                    if j == 0:
                                        ins = dve.tensor_copy(S[r, 0, :, w], fresh[r])
                                    else:
                                        gate = spread(gb[r, j - 1, par:HEADS:2], 2, VW)
                                        ins = dve.tensor_tensor(S[r, j, :, w], S[r, j - 1, :, w], gate, ALU.mult)
                                if j:
                                    step(ins)
                                    for par in range(2):
                                        r, w = slice(DH * par, DH * par + DH), slice(VW * par, VW * par + VW)
                                        ins = dve.tensor_tensor(S[r, j, :, w], S[r, j, :, w], fresh[r], ALU.add)
                                ins.then_inc(s["td"], 1)
                                dve.wait_ge(*freed[number["st", b, j]])
                            elif h != HEADS - 1:
                                p = {1: 0, 3: 1, 5: 2, 6: 3}[h]
                                t = filled(dve, "qw", b, p)
                                dve.scalar_tensor_tensor(out=qw[:, p, :], in0=qT[:, b % 2, p, P:SEQ], scalar=DH ** -0.5,
                                                         in1=t[:, 0:SEQ - P], op0=ALU.mult, op1=ALU.mult).then_inc(s["td"], 1)
                    if 0 <= i - 1 < NB:
                        b = i - 1
                        dve.wait_ge(s["gx"], b + 1)
                        step(dve.tensor_tensor_scan(cs[:, :], MM[:, :], ee[:, :], 0.0, ALU.add, ALU.subtract))
                        step(dve.tensor_tensor(aa[:, :], aa[:, :], cs[:, :], ALU.subtract))
                        step(dve.tensor_tensor_scan(MM[:, :], aa[:, :], aa[:, :], -3.0e38, ALU.max, ALU.max))
                        M3 = MM[:, :].rearrange("h (j s) -> h j s", j=TILES)
                        a3 = aa[:, :].rearrange("h (j s) -> h j s", j=TILES)
                        end = M3[:, :, P - 1:P]
                        dve.tensor_tensor(Z[0:8, :].rearrange("h (j s) -> h j s", j=TILES), a3, end.to_broadcast([8, TILES, P]), ALU.subtract)
                        dve.tensor_tensor(Z[32:40, P:SEQ].rearrange("h (j s) -> h j s", s=P), end[:, 0:3, :].to_broadcast([8, 3, P]), M3[:, 1:4, :], ALU.subtract)
                        dve.tensor_tensor(gd[:, :].unsqueeze(2), end[:, 0:2, :], end[:, 1:3, :], ALU.subtract)
                        dve.scalar_tensor_tensor(out=Z[64:72, :], in0=cs[:, :], scalar=-1.0, in1=MM[:, :], op0=ALU.mult, op1=ALU.subtract)\
                            .then_inc(s["zz"], 1)
                        dve.tensor_copy(Zx[96:104, :], aa[:, :])
                        step(dve.tensor_scalar(Mhl[0:8, :], MM[:, :], -1.0, None, ALU.mult))
                        dve.tensor_tensor(Mhl[32:40, :], MM[:, :], Mhl[0:8, :].bitcast(FP32), ALU.add)
                        dve.wait_ge(s["zx"], 2 * b + 2)
                        step(dve.tensor_copy(whl[32:40, :], Zx[32:40, P:SEQ]))
                        dve.tensor_tensor(whl[0:8, :], Zx[32:40, P:SEQ], whl[32:40, :].bitcast(FP32), ALU.subtract)
                        dve.tensor_tensor(gdiag[:, :, :], spread(gd[:, :], 2, 8), spread(ident[0:8, 0:8], 1, 2), ALU.mult).then_inc(s["ms"], 1)
                    if 0 <= i - 5 < NB:
                        b = i - 5
                        dve.wait_ge(s["lex"], b + 1)
                        step(dve.tensor_reduce(sx[:, :], ex[:, :, :], AX.X, ALU.add))
                        step(dve.reciprocal(sx[:, :], sx[:, :]))
                        step(dve.tensor_tensor(sm_all[:, b * TILES:(b + 1) * TILES, :], ex[:, :, :], spread(sx[:, :], 2, NEXP), ALU.mult))
                        dve.tensor_copy(xfb[:, b % 2, :, E_DIM:XW], sm_all[:, b * TILES:(b + 1) * TILES, :]).then_inc(s["smx"], 1)
                    if i < NB and i != 1:
                        layernorm_x(i)


def weight_pieces():
    pieces = []
    for e in range(NEXP):
        if e % 2 == 0:
            pieces += [("up", e, c, c + 1) for c in range(CH)]
        pieces += [("down", e, c, min(c + 2, FCH)) for c in range(0, FCH, 2)]
    return pieces


class Weights:

    def __init__(self, nc, io, ctx):
        def sb(name, shape, dt):
            return ctx.enter_context(nc.sbuf_tensor(name, shape, dt))

        self.io = io
        self.up = [sb("up_hi", [P, CH, FDIM], FP32R), sb("up_lo", [P, CH, FDIM], FP32R)]
        self.down = [sb("down_hi", [P, FCH, E_DIM], FP32R), sb("down_lo", [P, FCH, E_DIM], FP32R)]
        self.second = sb("down_2nd", [P, E_DIM], FP32R)
        self.raw = sb("w_raw", [P, 2, FDIM + 1], FP32)
        self.loaded = [ctx.enter_context(nc.semaphore(f"w_loaded{n}")) for n in range(2)]
        self.hi_done = ctx.enter_context(nc.semaphore("w_hi_done"))
        self.lo_done = ctx.enter_context(nc.semaphore("w_lo_done"))
        self.laid = ctx.enter_context(nc.semaphore("w_laid"))
        self.pieces = weight_pieces()

    def parts(self, m):
        kind, e, a, b = self.pieces[m]
        raw = self.raw[:, m % 2, :]
        if kind == "up":
            src = self.io["Wup"][e // 2].rearrange("(c p) f -> p c f", p=P)[:, a, :]
            return [(src, raw[:, 0:FDIM], self.up[0][:, a, :], self.up[1][:, a, :])]
        if b < FCH:
            src = self.io["Wdown"][e, a * P:b * P, :].rearrange("(c p) n -> p c n", p=P)
            return [(src, raw[:, 0:(b - a) * E_DIM].rearrange("p (c n) -> p c n", n=E_DIM),
                     self.down[0][:, a:b, :], self.down[1][:, a:b, :])]
        out = []
        for c in range(a, b):
            rows = P if c < FCH - 1 else FLAST
            out.append((self.io["Wdown"][e, c * P:c * P + rows, :], raw[0:rows, (c - a) * E_DIM:(c - a + 1) * E_DIM],
                        self.down[0][0:rows, c, :], self.down[1][0:rows, c, :]))
        return out

    def due(self, m):
        return self.loaded[m % 2], sum(16 * len(self.parts(n)) for n in range(m % 2, m + 1, 2))

    def load(self, eng, m):
        if m >= 2:
            eng.wait_ge(self.lo_done, m - 1)
        for src, raw, _, _ in self.parts(m):
            eng.dma_start(raw, src).then_inc(self.loaded[m % 2], 16)

    def hi(self, act, m):
        act.wait_ge(*self.due(m))
        for _, raw, hi, _ in self.parts(m):
            ins = act.activation(hi, raw, ACT.Copy)
        ins.then_inc(self.hi_done, 1)

    def lo(self, eng, m):
        eng.wait_ge(self.hi_done, m + 1)
        for _, raw, hi, lo in self.parts(m):
            ins = eng.tensor_tensor(lo, raw, hi.bitcast(FP32), ALU.subtract)
        ins.then_inc(self.lo_done, 1)

    def lay(self, eng, e):
        eng.wait_ge(self.lo_done, self.upto("down", e))
        hi, lo, second = (w.bitcast(FP32) for w in (self.down[0][:, FCH - 1, :], self.down[1][:, FCH - 1, :], self.second[:, :]))
        eng.dma_start(hi[FLAST:P, :], lo[0:SPARE, :]).then_inc(self.laid, 16)
        eng.dma_start(second[0:FLAST, :], hi[0:FLAST, :]).then_inc(self.laid, 16)
        eng.dma_start(second[FLAST:LAID, :], lo[SPARE:FLAST, :]).then_inc(self.laid, 16)

    def upto(self, kind, e):
        return max(m for m, p in enumerate(self.pieces) if p[0] == kind and p[1] <= e) + 1


def choose(nc, dram, sm_all, slots, weights, consts, NTOK, K):
    GROUP = P // NEXP
    SPAN = NTOK // GROUP
    NT = NTOK // P
    STEPS = (SPAN - 1).bit_length()
    VALID = 1 << STEPS
    TOP_BIT = 29
    LOWER = 16
    U16 = mybir.dt.uint16
    I16, FP16 = mybir.dt.int16, mybir.dt.float16
    KC = K // P
    ident = consts["ident"]
    with ExitStack() as ctx:
        def sb(name, shape, dt=FP32):
            return ctx.enter_context(nc.sbuf_tensor(name, shape, dt))

        def sem(name):
            return ctx.enter_context(nc.semaphore("c_" + name))

        turned = sb("turned", [NT, NEXP, P])
        V = sb("V", [P, SPAN])
        hit = sb("hit", [P, SPAN], FP16)
        over = sb("over", [P, SPAN]); same = sb("same", [P, SPAN]); rank = sb("rank", [P, SPAN])
        place = sb("place", [P, SPAN])
        ent = [sb("ent0", [P, SPAN], I16), sb("ent1", [P, SPAN], I16)]
        moving = sb("moving", [P, SPAN], I16); moved = sb("moved", [P, SPAN], I16)
        ids = sb("ids", [P, SPAN], I32)
        count = sb("count", [P, 1], FP16); low = [sb("low0", [P, 1]), sb("low1", [P, 1])]
        cand = sb("cand", [P, 1]); bit = sb("bit", [P, 1]); low32 = sb("low32", [P, 2], I32)
        upper = sb("upper", [P, SPAN], I16)
        lower = sb("lower", [P, SPAN], U16); beyond = sb("beyond", [P, SPAN], U16); key = sb("key", [P, SPAN], U16)
        same_groups = sb("same_groups", [P, P], FP16)
        groups32 = sb("groups32", [P, P]); before = sb("before", [P, P])
        tot = sb("tot", [P, 1]); need = sb("need", [P, 1]); offs = sb("offs", [P, 1]); nq = sb("nq", [P, 1]); wide = sb("wide", [P, P])
        base = sb("base", [P, P]); jump = sb("jump", [P, P])
        slot = sb("slot", [P, KC]); home = sb("home", [P, NEXP, KC])
        begun = sb("begun", [P, NEXP, KC, GROUP]); skip = sb("skip", [P, NEXP, KC, GROUP])
        pst = ctx.enter_context(nc.psum_tensor("c_pst", [NT, NEXP, P], FP32))
        pc = ctx.enter_context(nc.psum_tensor("c_pc", [P, 512], FP32))
        s = {n: sem(n) for n in "turn out saved V pool cnt sum dve tie mm wide bases jump lower list done".split()}
        halves = V[:, :].bitcast(U16)
        with nc.Block() as block:
            @block.sync
            def _(sp):
                for m in range(2):
                    weights.load(sp, m)
                sp.wait_ge(s["out"], 1)
                sp.dma_start(dram["gates"].rearrange("e (t p) -> t e p", p=P), turned[:, :, :]).then_inc(s["saved"], 16)
                sp.wait_ge(s["saved"], 16)
                sp.dma_start(V[:, :], dram["gates"].rearrange("e (q n) -> (e q) n", q=GROUP)).then_inc(s["V"], 16)
                for m in range(2, weights.upto("down", 0)):
                    weights.load(sp, m)
                sp.wait_ge(s["done"], 1)
                sp.dma_start(dram["list"].rearrange("(g n) o -> g (n o)", g=P), ids[:, :]).then_inc(s["list"], 16)
                sp.wait_ge(s["list"], 16)

            @block.scalar
            def _(act):
                first = weights.upto("down", 0)
                weights.hi(act, 0)
                weights.hi(act, 1)
                act.wait_ge(s["V"], 16)
                act.activation(lower[:, :], halves[:, 0:2 * SPAN:2], ACT.Copy).then_inc(s["lower"], 1)
                for m in range(2, first):
                    weights.hi(act, m)
                weights.lay(act, 0)
                act.preload_act_table_set("silu_and_others")

            @block.gpsimd
            def _(pool):
                step = Chain(pool, s["pool"])
                g3 = groups32[:, :].rearrange("k (a b) -> k a b", b=GROUP)
                step(pool.memset(groups32[:, :], 1.0))
                step(pool.affine_select(out=g3, in_=g3, compare_op=ALU.is_ge, fill=0.0, base=0,
                                        pattern=[[-GROUP, NEXP], [0, GROUP]], channel_multiplier=1))
                step(pool.affine_select(out=g3, in_=g3, compare_op=ALU.is_ge, fill=0.0, base=GROUP - 1,
                                        pattern=[[GROUP, NEXP], [0, GROUP]], channel_multiplier=-1))
                step(pool.affine_select(out=before[:, :], in_=groups32[:, :], compare_op=ALU.is_gt, fill=0.0, base=0,
                                        pattern=[[1, P]], channel_multiplier=-1))
                step(pool.tensor_copy(same_groups[:, :], groups32[:, :]))
                step(pool.iota(place[:, :], pattern=[[1, SPAN]], base=0, channel_multiplier=0, allow_small_or_imprecise_dtypes=True))
                step(pool.iota(slot[:, :], pattern=[[P, KC]], base=0, channel_multiplier=1, allow_small_or_imprecise_dtypes=True))
                step(pool.iota(home[:, :, :], pattern=[[NTOK, NEXP], [P, KC]], base=0, channel_multiplier=1, allow_small_or_imprecise_dtypes=True))
                for m in range(weights.upto("down", 0)):
                    weights.lo(pool, m)
                pool.wait_ge(s["jump"], 1)
                b3 = base[:, :].rearrange("p (e q) -> p e q", e=NEXP)
                j3 = jump[:, :].rearrange("p (e q) -> p e q", e=NEXP)
                for e in range(NEXP):
                    ins = pool.tensor_tensor(begun[:, e, :, :], spread(b3[:, e, :], 1, KC), spread(slot[:, :], 2, GROUP), ALU.subtract)
                step(ins)
                step(pool.tensor_scalar(begun[:, :, :, :], begun[:, :, :, :], 0.0, None, ALU.is_le))
                for e in range(NEXP):
                    ins = pool.tensor_tensor(skip[:, e, :, 0:GROUP - 1], begun[:, e, :, 1:GROUP], spread(j3[:, e, 0:GROUP - 1], 1, KC), ALU.mult)
                step(ins)
                step(pool.memset(skip[:, :, :, GROUP - 1:GROUP], 0.0))
                w = GROUP
                while w > 1:
                    w //= 2
                    step(pool.tensor_tensor(skip[:, :, :, 0:w], skip[:, :, :, 0:w], skip[:, :, :, w:2 * w], ALU.add))
                step(pool.tensor_tensor(home[:, :, :], skip[:, :, :, 0], home[:, :, :], ALU.add))
                step(pool.tensor_copy(slots[:, :].rearrange("p (e t) -> p e t", e=NEXP), home[:, :, :]))

            @block.tensor
            def _(pe):
                for e in range(NEXP):
                    mm = pe.transpose(pst[:, e, :], sm_all[:, :, e], ident[:, :])
                mm.then_inc(s["turn"], 1)
                pe.wait_ge(s["pool"], 5)
                for n in range(TOP_BIT + 1):
                    pe.wait_ge(s["cnt"], n + 1)
                    pe.matmul(pc[:, 0:1], same_groups[:, :], count[:, :], start=True, stop=True).then_inc(s["sum"], 1)
                pe.wait_ge(s["tie"], 1)
                pe.matmul(pc[:, 0:1], groups32[:, :], tot[:, :], start=True, stop=True).then_inc(s["mm"], 1)
                pe.wait_ge(s["tie"], 2)
                pe.matmul(pc[:, 0:1], before[:, :], offs[:, :], start=True, stop=True).then_inc(s["mm"], 1)
                pe.wait_ge(s["wide"], 1)
                pe.matmul(pc[:, 0:P], wide[:, :], before[:, :], start=True, stop=True)
                pe.matmul(pc[:, P:2 * P], wide[:, :], ident[:, :], start=True, stop=True).then_inc(s["bases"], 1)

            @block.vector
            def _(dve):
                step = Chain(dve, s["dve"])
                dve.wait_ge(s["turn"], 1)
                dve.tensor_copy(turned[:, :, :], pst[:, :, :]).then_inc(s["out"], 1)
                dve.wait_ge(s["V"], 16)
                step(dve.tensor_copy(upper[:, :], halves[:, 1:2 * SPAN:2].bitcast(I16)))
                rounds = 0
                for part, bits in enumerate((TOP_BIT - LOWER + 1, LOWER)):
                    if part:
                        dve.wait_ge(s["lower"], 1)
                        step(dve.scalar_tensor_tensor(out=key[:, :], in0=upper[:, :], scalar=low[0][:, :], in1=lower[:, :], op0=ALU.is_equal, op1=ALU.mult))
                        step(dve.tensor_scalar(beyond[:, :], upper[:, :], low[0][:, :], float((1 << LOWER) - 1), ALU.is_gt, ALU.mult))
                        step(dve.tensor_tensor(key[:, :], key[:, :], beyond[:, :], ALU.add))
                    value = low[part]
                    step(dve.memset(value[:, :], 0.0))
                    step(dve.memset(cand[:, :], float(1 << (bits - 1))))
                    for k in range(bits - 1, -1, -1):
                        dve.tensor_scalar(hit[:, :], (key if part else upper)[:, :], cand[:, :], 0.0, ALU.is_ge, ALU.add, accum_out=count[:, :])\
                            .then_inc(s["cnt"], 1)
                        rounds += 1
                        dve.wait_ge(s["sum"], rounds)
                        step(dve.tensor_scalar(bit[:, :], pc[:, 0:1], float(K), float(1 << k), ALU.is_ge, ALU.mult))
                        if k:
                            step(dve.scalar_tensor_tensor(out=cand[:, :], in0=bit[:, :], scalar=float(1 << (k - 1)), in1=value[:, :], op0=ALU.add, op1=ALU.add))
                        step(dve.tensor_tensor(value[:, :], value[:, :], bit[:, :], ALU.add))
                step(dve.tensor_scalar(low32[:, 0:1], low[0][:, :], float(1 << LOWER), None, ALU.mult))
                step(dve.tensor_copy(low32[:, 1:2], low[1][:, :]))
                step(dve.tensor_tensor(low32[:, 0:1], low32[:, 0:1], low32[:, 1:2], ALU.bitwise_or))
                least = low32[:, 0:1].bitcast(FP32)
                dve.wait_ge(s["pool"], 8)
                dve.tensor_scalar(over[:, :], V[:, :], least, 0.0, ALU.is_gt, ALU.add, accum_out=tot[:, :]).then_inc(s["tie"], 1)
                dve.tensor_scalar(same[:, :], V[:, :], least, 0.0, ALU.is_equal, ALU.add, accum_out=offs[:, :])
                dve.wait_ge(s["mm"], 1)
                step(dve.tensor_scalar(need[:, :], pc[:, 0:1], -1.0, float(K), ALU.mult, ALU.add))
                dve.tensor_tensor_scan(rank[:, :], same[:, :], same[:, :], 0.0, ALU.add, ALU.bypass).then_inc(s["tie"], 1)
                dve.wait_ge(s["mm"], 2)
                step(dve.tensor_tensor(need[:, :], need[:, :], pc[:, 0:1], ALU.subtract))
                step(dve.scalar_tensor_tensor(out=same[:, :], in0=rank[:, :], scalar=need[:, :], in1=same[:, :], op0=ALU.is_le, op1=ALU.mult))
                step(dve.tensor_tensor(over[:, :], over[:, :], same[:, :], ALU.add))
                step(dve.tensor_tensor_scan(rank[:, :], over[:, :], over[:, :], 0.0, ALU.add, ALU.bypass))
                step(dve.tensor_copy(nq[:, :], rank[:, SPAN - 1:SPAN]))
                dve.tensor_scalar(wide[:, :], groups32[:, :], 0.0, nq[:, :], ALU.mult, ALU.add).then_inc(s["wide"], 1)
                step(dve.tensor_tensor(rank[:, :], place[:, :], rank[:, :], ALU.subtract))
                step(dve.scalar_tensor_tensor(out=ent[0][:, :], in0=rank[:, :], scalar=float(VALID + 1), in1=over[:, :], op0=ALU.add, op1=ALU.mult))
                dve.wait_ge(s["bases"], 1)
                dve.tensor_copy(base[:, :], pc[:, 0:P])
                dve.tensor_scalar(jump[:, :], pc[:, P:2 * P], -1.0, float(SPAN), ALU.mult, ALU.add).then_inc(s["jump"], 1)
                for k in range(STEPS):
                    old, new = ent[k % 2], ent[1 - k % 2]
                    d = 1 << k
                    step(dve.tensor_scalar(moving[:, :], old[:, :], d, None, ALU.bitwise_and))
                    step(dve.scalar_tensor_tensor(out=new[:, :], in0=moving[:, :], scalar=0.0, in1=old[:, :], op0=ALU.is_equal, op1=ALU.mult))
                    step(dve.tensor_tensor(moved[:, :], old[:, :], new[:, :], ALU.subtract))
                    step(dve.tensor_tensor(new[:, 0:SPAN - d], new[:, 0:SPAN - d], moved[:, d:SPAN], ALU.add))
                step(dve.tensor_scalar(moving[:, :], ent[STEPS % 2][:, :], VALID - 1, None, ALU.bitwise_and))
                step(dve.tensor_tensor(rank[:, :], place[:, :], moving[:, :], ALU.add))
                dve.tensor_scalar(ids[:, :], rank[:, :], consts["span0"][:, 0:1], None, ALU.add).then_inc(s["done"], 1)


def experts(nc, io, dram, slots, weights, tg, consts, NTOK, K):
    BLK = 4 * P
    BPE = K // BLK
    NBLK = NEXP * BPE
    ident = consts["ident"]
    rows_v, list_v = dram["xf"], dram["list"]
    out_rows = io["out"].rearrange("b s e -> (b s) e")
    with ExitStack() as ctx:
        def sb(name, shape, dt=FP32):
            return ctx.enter_context(nc.sbuf_tensor(name, shape, dt))

        def sem(name):
            return ctx.enter_context(nc.semaphore("e_" + name))

        xg = sb("xg", [P, 4, XW])
        xT = [sb("xT_hi", [P, CH, BLK], FP32R), sb("xT_lo", [P, CH, BLK], FP32R)]
        mid = [sb("mid_hi", [P, FCH, BLK], FP32R), sb("mid_lo", [P, FCH, BLK], FP32R)]
        z = sb("z", [P, 2, BLK])
        y = sb("y", [P, 4, E_DIM])
        gs = sb("gs", [P, 2, 4])
        bup = sb("bup", [P, NEXP // 2, FCH])
        bdn = sb("bdn", [P, 2, E_DIM])
        idx = sb("idx", [P, 2, 4], I32)
        UP = [ctx.enter_context(nc.psum_tensor(f"UP{n}", [P, BLK], FP32)) for n in range(3)]
        DN = [ctx.enter_context(nc.psum_tensor(f"DN{n}", [P, E_DIM], FP32)) for n in range(2)]
        T = [ctx.enter_context(nc.psum_tensor(f"TT{n}", [P, BLK], FP32)) for n in range(2)]
        s = {n: sem(n) for n in "bup rows up z hi mid dn yp y tfull thi tlo gs dve laid".split()}
        s_ix = [sem(f"ix{n}") for n in range(2)]
        s_sc = [sem(f"sc{n}") for n in range(4)]
        s_bd = [sem(f"bd{n}") for n in range(2)]

        def rows_of(f):
            return P if f < FCH - 1 else FLAST

        first_down = weights.upto("down", 0)

        def down_pieces(n):
            e = n // BPE
            return [] if n % BPE or e == 0 else list(range(weights.upto("down", e) - (FCH + 1) // 2, weights.upto("down", e)))

        def up_pieces(n):
            e = (n + 1) // BPE
            return list(range(weights.upto("up", e) - CH, weights.upto("up", e))) if (n + 1) % BPE == 0 and e % 2 == 0 and e < NEXP else []

        with nc.Block() as block:
            @block.sync
            def _(sp):
                full = (FCH - 1) * P
                with nc.allow_non_contiguous_dma(reason="biases by partition, once"):
                    for g in range(NEXP // 2):
                        sp.dma_start(bup[:, g, 0:FCH - 1], io["bup"][g, 0:full].rearrange("(c p) -> p c", p=P)).then_inc(s["bup"], 16)
                        sp.dma_start(bup[0:FLAST, g, FCH - 1:FCH], io["bup"][g, full:FDIM].unsqueeze(1)).then_inc(s["bup"], 16)
                m = first_down
                for e in range(NEXP):
                    if e >= 2:
                        sp.wait_ge(s["y"], 4 * BPE * (e - 1))
                    sp.dma_start(bdn[:, e % 2, :], io["bdown"][e].partition_broadcast(P)).then_inc(s_bd[e % 2], 16)
                    while e + 1 < NEXP and m < weights.upto("down", e + 1):
                        weights.load(sp, m)
                        m += 1

            @block.gpsimd
            def _(pool):
                def list_rows(n):
                    if n >= 2:
                        for t in range(4):
                            pool.wait_ge(s_sc[t], 16 * (n - 1))
                    for t in range(4):
                        pool.indirect_dma_start(idx[:, n % 2, t:t + 1], None, list_v, bass.IndirectOffsetOnAxis(
                            ap=slots[:, 4 * n + t:4 * n + t + 1], axis=0)).then_inc(s_ix[n % 2], 16)

                def gather(n):
                    pool.wait_ge(s_ix[n % 2], 64 * (n // 2 + 1))
                    if n >= 1:
                        pool.wait_ge(s["tfull"], CH * n)
                        pool.wait_ge(s["gs"], n)
                    for t in range(4):
                        pool.indirect_dma_start(xg[:, t, :], None, rows_v, bass.IndirectOffsetOnAxis(
                            ap=idx[:, n % 2, t:t + 1].bitcast(U32), axis=0)).then_inc(s["rows"], 16)

                list_rows(0)
                gather(0)
                if NBLK > 1:
                    list_rows(1)
                for n in range(NBLK):
                    if n + 1 < NBLK:
                        gather(n + 1)
                    for t in range(4):
                        m = 4 * n + t
                        pool.wait_ge(s["y"], m + 1)
                        if n % BPE == 0 and n and t == 0:
                            for u in range(4):
                                pool.wait_ge(s_sc[u], 16 * n)
                        pool.indirect_dma_start(out_rows, bass.IndirectOffsetOnAxis(ap=idx[:, n % 2, t:t + 1].bitcast(U32), axis=0),
                                                y[:, t, :], None, compute_op=ALU.add).then_inc(s_sc[t], 16)
                    if n + 2 < NBLK:
                        list_rows(n + 2)
                for t in range(4):
                    pool.wait_ge(s_sc[t], 16 * NBLK)

            @block.scalar
            def _(act):
                def turn_hi(n, c):
                    act.wait_ge(s["tfull"], CH * n + c + 1)
                    act.activation(xT[0][:, c, :], T[c % 2][:, :], ACT.Copy).then_inc(s["thi"], 1)

                act.wait_ge(s["bup"], 16 * NEXP)
                for c in range(CH):
                    turn_hi(0, c)
                for n in range(NBLK):
                    e = n // BPE
                    more = down_pieces(n)
                    for f in range(FCH):
                        k, r = FCH * n + f, rows_of(f)
                        act.wait_ge(s["up"], k + 1)
                        if k >= 2:
                            act.wait_ge(s["mid"], k - 1)
                        act.activation(z[0:r, k % 2, :], UP[k % 3][0:r, :], ACT.Silu, bias=bup[0:r, e // 2, f:f + 1]).then_inc(s["z"], 1)
                        if more:
                            weights.hi(act, more.pop(0))
                        if f == FCH - 3 and n and n % BPE == 0:
                            weights.lay(act, e)
                    act.wait_ge(s["hi"], FCH * (n + 1))
                    last = [m_[:, FCH - 1, :].bitcast(FP32) for m_ in mid]
                    act.dma_start(last[0][FLAST:P, :], last[0][0:SPARE, :]).then_inc(s["laid"], 16)
                    act.dma_start(last[1][FLAST:LAID, :], last[0][SPARE:FLAST, :]).then_inc(s["laid"], 16)
                    more = up_pieces(n)
                    for t in range(4):
                        if n + 1 < NBLK:
                            turn_hi(n + 1, t)
                        if more:
                            weights.hi(act, more.pop(0))

            @block.tensor
            def _(pe):
                def turn(n, c):
                    k = CH * n + c
                    if c == 0:
                        pe.wait_ge(s["rows"], 64 * (n + 1))
                    if k >= 2:
                        pe.wait_ge(s["tlo"], k - 1)
                    for t in range(4):
                        mm = pe.transpose(T[c % 2][:, t * P:(t + 1) * P], xg[:, t, c * P:(c + 1) * P], ident[:, :])
                    mm.then_inc(s["tfull"], 1)

                for c in range(CH):
                    turn(0, c)
                for n in range(NBLK):
                    e = n // BPE
                    if n % BPE == 0:
                        pe.wait_ge(weights.lo_done, weights.upto("up", e))
                    pe.wait_ge(s["tlo"], CH * (n + 1))
                    for f in range(FCH):
                        k, r = FCH * n + f, rows_of(f)
                        if k >= 3:
                            pe.wait_ge(s["z"], k - 2)
                        first = True
                        for c in range(CH):
                            for wa, xa in ((0, 0), (0, 1), (1, 0)):
                                mm = pe.matmul(UP[k % 3][0:r, :], weights.up[wa][:, c, f * P:f * P + r], xT[xa][:, c, :],
                                               start=first, stop=(c == CH - 1 and wa == 1))
                                first = False
                        mm.then_inc(s["up"], 1)
                    if n % BPE == 0:
                        pe.wait_ge(weights.lo_done, weights.upto("down", e))
                    for t in range(4):
                        if n + 1 < NBLK:
                            turn(n + 1, t)
                        m = 4 * n + t
                        if m >= 2:
                            pe.wait_ge(s["yp"], m - 1)
                        first = True
                        for f in range(FCH):
                            if t == 0:
                                pe.wait_ge(s["mid"], FCH * n + f + 1)
                            tt = slice(t * P, (t + 1) * P)
                            if f < FCH - 1:
                                parts = [(mid[ma][:, f, tt], weights.down[wa][:, f, :]) for ma, wa in ((0, 0), (0, 1), (1, 0))]
                            else:
                                parts = [(mid[0][:, f, tt], weights.down[0][:, f, :]),
                                         (mid[1][0:LAID, f, tt], weights.second[0:LAID, :])]
                                if t == 0:
                                    pe.wait_ge(s["laid"], 32 * (n + 1))
                                    pe.wait_ge(weights.laid, 48 * (e + 1))
                            for lhs, rhs in parts:
                                mm = pe.matmul(DN[m % 2][:, :], lhs, rhs, start=first, stop=(f == FCH - 1 and lhs is parts[-1][0]))
                                first = False
                        mm.then_inc(s["dn"], 1)

            @block.vector
            def _(dve):
                def turn_lo(n, c):
                    k = CH * n + c
                    dve.wait_ge(s["thi"], k + 1)
                    dve.tensor_tensor(xT[1][:, c, :], T[c % 2][:, :], xT[0][:, c, :].bitcast(FP32), ALU.subtract).then_inc(s["tlo"], 1)

                def gate(n):
                    e = n // BPE
                    dve.wait_ge(s["rows"], 64 * (n + 1))
                    dve.tensor_scalar(gs[:, n % 2, :], xg[:, :, E_DIM + e], tg["ap"][:, 1:2], None, ALU.mult).then_inc(s["gs"], 1)

                gate(0)
                for c in range(CH):
                    turn_lo(0, c)
                for n in range(NBLK):
                    e = n // BPE
                    more = down_pieces(n)
                    for f in range(FCH):
                        k, r = FCH * n + f, rows_of(f)
                        dve.wait_ge(s["z"], k + 1)
                        dve.tensor_copy(mid[0][0:r, f, :], z[0:r, k % 2, :]).then_inc(s["hi"], 1)
                        dve.wait_ge(s["hi"], k + 1)
                        dve.tensor_tensor(mid[1][0:r, f, :], z[0:r, k % 2, :], mid[0][0:r, f, :].bitcast(FP32), ALU.subtract)\
                            .then_inc(s["mid"], 1)
                        if more:
                            weights.lo(dve, more.pop(0))
                    more = up_pieces(n)
                    if n % BPE == 0:
                        dve.wait_ge(s_bd[e % 2], 16 * (e // 2 + 1))
                    for t in range(4):
                        if n + 1 < NBLK:
                            if t == 0:
                                gate(n + 1)
                            turn_lo(n + 1, t)
                        if more:
                            weights.lo(dve, more.pop(0))
                        m = 4 * n + t
                        dve.wait_ge(s["dn"], m + 1)
                        if n:
                            dve.wait_ge(s_sc[t], 16 * n)
                        dve.tensor_tensor(y[:, t, :], DN[m % 2][:, :], bdn[:, e % 2, :], ALU.add).then_inc(s["yp"], 1)
                        dve.wait_ge(s["yp"], m + 1)
                        dve.tensor_scalar(y[:, t, :], y[:, t, :], gs[:, n % 2, t:t + 1], None, ALU.mult).then_inc(s["y"], 1)


def program(nc, x, ctx_, g_x, g_f, igw, igb, fgw, fgb, outw, Wr, br, Wup, bup, Wdown, bdown, out):
    NB = x.shape[0]
    NTOK = NB * SEQ
    K = NTOK // NEXP
    io = dict(x=x, ctx=ctx_, igw=igw, igb=igb, fgw=fgw, fgb=fgb, outw=outw, Wr=Wr, br=br,
              Wup=Wup, bup=bup, Wdown=Wdown, bdown=bdown, out=out)
    dram = {
        "xf": nc.dram_tensor("rows_scratch", (NTOK, XW), FP32).ap(),
        "gates": nc.dram_tensor("gates_scratch", (NEXP, NTOK), FP32).ap(),
        "list": nc.dram_tensor("list_scratch", (NEXP * NTOK, 1), I32).ap(),
    }
    with ExitStack() as c:
        def sb(name, shape, dt=FP32):
            return c.enter_context(nc.sbuf_tensor(name, shape, dt))

        ident = sb("ident", [P, P]); ones = sb("ones", [P, P]); identb = sb("identb", [P, P], BF16)
        tgt = sb("tanh_g", [P, 2])
        span0 = sb("span0", [P, 1]); part = sb("part", [P, 1], I32)
        sm_all = sb("sm_all", [P, NB * TILES, NEXP])
        slots = sb("slots", [P, NEXP * K // P], U32)
        s_con, s_g, s_tg, s_sp = (c.enter_context(nc.semaphore(n)) for n in ("s_con", "s_g", "s_tg", "s_sp"))
        SPAN = NTOK // (P // NEXP)
        with nc.Block() as block:
            @block.gpsimd
            def _(pool):
                step = Chain(pool, s_con)
                step(pool.memset(ident[:, :], 0.0))
                step(pool.memset(ones[:, :], 1.0))
                step(pool.affine_select(out=ident[:, :], in_=ident[:, :], compare_op=ALU.not_equal, fill=1.0,
                                        base=0, pattern=[[-1, P]], channel_multiplier=1))
                step(pool.tensor_copy(identb[:, :], ident[:, :]))
                step(pool.iota(part[:, :], pattern=[[0, 1]], base=0, channel_multiplier=SPAN))

            @block.scalar
            def _(act):
                act.dma_start(tgt[:, 0:1], g_x.partition_broadcast(P)).then_inc(s_g, 16)
                act.dma_start(tgt[:, 1:2], g_f.partition_broadcast(P)).then_inc(s_g, 16)
                act.wait_ge(s_g, 32)
                act.activation(tgt[:, :], tgt[:, :], ACT.Tanh).then_inc(s_tg, 1)

            @block.vector
            def _(dve):
                dve.wait_ge(s_con, 5)
                dve.tensor_scalar(part[:, :], part[:, :], NTOK - 1, None, ALU.bitwise_and).then_inc(s_sp, 1)
                dve.wait_ge(s_sp, 1)
                dve.tensor_copy(span0[:, :], part[:, :]).then_inc(s_sp, 1)
        consts = dict(ident=ident, identb=identb, ones=ones, span0=span0, sem=s_con, ready=5)
        tg = dict(sem=s_tg, ready=1, ap=tgt)
        attention(nc, io, NB, dram, sm_all, tg, consts)
        with ExitStack() as wctx:
            weights = Weights(nc, io, wctx)
            choose(nc, dram, sm_all, slots, weights, consts, NTOK, K)
            experts(nc, io, dram, slots, weights, tg, consts, NTOK, K)


_INS = ["x", "ctx_1024", "g_xattn", "g_ffn", "L0_xattn_igate_w", "L0_xattn_igate_b", "L0_xattn_fgate_w", "L0_xattn_fgate_b",
        "L0_xattn_out_w", "L0_ffn_Wr", "L0_ffn_br", "L0_ffn_W_up", "L0_ffn_b_up", "L0_ffn_W_down", "L0_ffn_b_down"]


def kernel(**inputs):
    import concourse.bacc as bacc
    from concourse.bass_utils import run_bass_kernel_spmd

    nc = bacc.Bacc("TRN2", target_bir_lowering=False, num_devices=1)
    arrays, args = {}, []
    for name in _INS:
        a = np.ascontiguousarray(inputs[name])
        arrays[f"in_{name}"] = a
        args.append(nc.dram_tensor(f"in_{name}", a.shape, mybir.dt.from_np(a.dtype), kind="ExternalInput").ap())
    shape = inputs["x"].shape
    args.append(nc.dram_tensor("out_x", shape, FP32, kind="ExternalOutput").ap())
    program(nc, *args)
    r = run_bass_kernel_spmd(nc, [arrays], core_ids=[0])
    return r.results[0]["out_x"]
```
